# Optimizing a Trainium2 kernel written in Bass

```python
import numpy as np
import jax
import jax.numpy as jnp

def _softmax(x, axis=-1):
    return jax.nn.softmax(x, axis=axis)
def _gelu(x):
    return jax.nn.gelu(x, approximate=True)
def _silu(x):
    return jax.nn.silu(x)
def _sigmoid(x):
    return jax.nn.sigmoid(x)
def _layernorm(x, axis=-1, eps=1e-5):
    m = jnp.mean(x, axis=axis, keepdims=True)
    v = jnp.var(x, axis=axis, keepdims=True)
    return (x - m) / jnp.sqrt(v + eps)
def _scatter_add(tgt, idx, src, axis=0):
    return tgt.at[idx].add(src)
def _segment_sum(src, seg, n):
    return jax.ops.segment_sum(src, seg, n)

kernel_name = 'mk_conv_attn_hybrid_d2_conv_nhwc256_eec95d'

def setup_inputs(seed: int = 0):
    np.random.seed(seed)
    _w = jnp.asarray
    def _rec_inputs():
        import jax
        import jax.numpy as jnp
        _gk = jax.random.key(seed)
        x = -0.0005207 + 1.001 * jax.random.normal(jax.random.fold_in(_gk, 1), (2, 64, 64, 256), jnp.float32)
        return x
    x = _rec_inputs()
    def _L0_conv_setup():
        import jax, jax.numpy as jnp
        import numpy as np
        key = jax.random.key(seed)
        ks = jax.random.split(key, 8)
        B, S, K, D = (2, 64, 64, 256)
        C = D // 8
        return {'x': jax.random.normal(ks[0], (B, S, K, D), dtype=jnp.float32), 'Wq': jax.random.normal(ks[1], (C, D), dtype=jnp.float32) * (1.0 / np.sqrt(D)), 'bq': jax.random.normal(ks[2], (C,), dtype=jnp.float32) * 0.01, 'Wk': jax.random.normal(ks[3], (C, D), dtype=jnp.float32) * (1.0 / np.sqrt(D)), 'bk': jax.random.normal(ks[4], (C,), dtype=jnp.float32) * 0.01, 'Wv': jax.random.normal(ks[5], (D, D), dtype=jnp.float32) * (1.0 / np.sqrt(D)), 'bv': jax.random.normal(ks[6], (D,), dtype=jnp.float32) * 0.01, 'gamma': jax.random.uniform(ks[7], (1,), dtype=jnp.float32)}
    _L0_conv_all = _L0_conv_setup()
    _L0_conv_in = {k: v for k, v in _L0_conv_all.items() if k in ('Wq', 'bq', 'Wk', 'bk', 'Wv', 'bv', 'gamma', )}
    del _L0_conv_all

    def _L1_attn_setup():
        import jax, jax.numpy as jnp
        import numpy as np
        B, N, D_IN, E, H = (4, 512, 256, 64, 4)
        NEG = 1000000000.0

        def _sdp(q, k, v):
            logits = jnp.einsum('bne,bme->bnm', q, k) / jnp.sqrt(jnp.asarray(E, q.dtype))
            return jnp.einsum('bnm,bme->bne', jax.nn.softmax(logits, axis=-1), v)

        def _cosine(q, k, v):
            qn = q / jnp.linalg.norm(q, axis=-1, keepdims=True)
            kn = k / jnp.linalg.norm(k, axis=-1, keepdims=True)
            logits = jnp.einsum('bne,bme->bnm', qn, kn)
            return jnp.einsum('bnm,bme->bne', jax.nn.softmax(logits, axis=-1), v)

        def _l1(q, k, v):
            d = jnp.sum(jnp.abs(q[:, :, None, :] - k[:, None, :, :]), axis=-1)
            return jnp.einsum('bnm,bme->bne', jax.nn.softmax(-d, axis=-1), v)

        def _l2(q, k, v):
            d = jnp.sqrt(jnp.sum(jnp.square(q[:, :, None, :] - k[:, None, :, :]), axis=-1))
            return jnp.einsum('bnm,bme->bne', jax.nn.softmax(-d, axis=-1), v)
        _HEAD_FNS = (_sdp, _cosine, _l1, _l2)
        key = jax.random.key(seed)
        ks = jax.random.split(key, 7)
        s = 1.0 / np.sqrt(D_IN)
        return {'x': jax.random.normal(ks[0], (B, N, D_IN), jnp.float32), 'Wq': jax.random.normal(ks[1], (H, D_IN, E), jnp.float32) * s, 'bq': jnp.zeros((H, E), jnp.float32), 'Wk': jax.random.normal(ks[2], (H, D_IN, E), jnp.float32) * s, 'bk': jnp.zeros((H, E), jnp.float32), 'Wv': jax.random.normal(ks[3], (H, D_IN, E), jnp.float32) * s, 'bv': jnp.zeros((H, E), jnp.float32)}
    _L1_attn_all = _L1_attn_setup()
    _L1_attn_in = {k: v for k, v in _L1_attn_all.items() if k in ('Wq', 'bq', 'Wk', 'bk', 'Wv', 'bv', )}
    del _L1_attn_all

    def _L1_ffn_setup():
        import jax, jax.numpy as jnp
        import numpy as np
        NUM_EXPERTS = 8
        TOP_K = 2
        B, S, D = (8, 8192, 256)

        def _moe(tokens, router_w, w1, b1, w2, b2):
            N = tokens.shape[0]
            E = router_w.shape[0]
            logits = tokens.astype(jnp.float32) @ router_w.astype(jnp.float32).T
            probs = jax.nn.softmax(logits, axis=-1)
            rw, re = jax.lax.top_k(probs, TOP_K)
            if TOP_K > 1:
                rw = rw / jnp.maximum(rw.sum(-1, keepdims=True), 1e-12)
            rw = rw.astype(tokens.dtype)
            combine = jnp.zeros((N, E), tokens.dtype).at[jnp.arange(N)[:, None], re].set(rw)
            out = tokens
            for e in range(E):
                h = jax.nn.gelu(tokens @ w1[e] + b1[e], approximate=False)
                y = h @ w2[e] + b2[e]
                out = out + combine[:, e:e + 1] * y
            return out
        key = jax.random.key(seed)
        ks = jax.random.split(key, 4)
        scale = 1.0 / np.sqrt(D).astype(np.float32)
        return {'input_embeddings': jax.random.normal(ks[0], (B, S, D), jnp.float32), 'router_w': jax.random.normal(ks[1], (NUM_EXPERTS, D), jnp.float32) * scale, 'w1': jax.random.normal(ks[2], (NUM_EXPERTS, D, D), jnp.float32) * scale, 'b1': jnp.zeros((NUM_EXPERTS, D), jnp.float32), 'w2': jax.random.normal(ks[3], (NUM_EXPERTS, D, D), jnp.float32) * scale, 'b2': jnp.zeros((NUM_EXPERTS, D), jnp.float32)}
    _L1_ffn_all = _L1_ffn_setup()
    _L1_ffn_in = {k: v for k, v in _L1_ffn_all.items() if k in ('router_w', 'w1', 'b1', 'w2', 'b2', )}
    del _L1_ffn_all

    return {
        "x": x,
        "L0_conv_Wq": _L0_conv_in["Wq"],
        "L0_conv_bq": _L0_conv_in["bq"],
        "L0_conv_Wk": _L0_conv_in["Wk"],
        "L0_conv_bk": _L0_conv_in["bk"],
        "L0_conv_Wv": _L0_conv_in["Wv"],
        "L0_conv_bv": _L0_conv_in["bv"],
        "L0_conv_gamma": _L0_conv_in["gamma"],
        "L1_attn_Wq": _L1_attn_in["Wq"],
        "L1_attn_bq": _L1_attn_in["bq"],
        "L1_attn_Wk": _L1_attn_in["Wk"],
        "L1_attn_bk": _L1_attn_in["bk"],
        "L1_attn_Wv": _L1_attn_in["Wv"],
        "L1_attn_bv": _L1_attn_in["bv"],
        "L1_ffn_router_w": _L1_ffn_in["router_w"],
        "L1_ffn_w1": _L1_ffn_in["w1"],
        "L1_ffn_b1": _L1_ffn_in["b1"],
        "L1_ffn_w2": _L1_ffn_in["w2"],
        "L1_ffn_b2": _L1_ffn_in["b2"],
    }

def reference(x, L0_conv_Wq, L0_conv_bq, L0_conv_Wk, L0_conv_bk, L0_conv_Wv, L0_conv_bv, L0_conv_gamma, L1_attn_Wq, L1_attn_bq, L1_attn_Wk, L1_attn_bk, L1_attn_Wv, L1_attn_bv, L1_ffn_router_w, L1_ffn_w1, L1_ffn_b1, L1_ffn_w2, L1_ffn_b2):
    import jax
    import jax.numpy as jnp
    def _L0_conv_ref(x, Wq, bq, Wk, bk, Wv, bv, gamma):
        import jax, jax.numpy as jnp
        import numpy as np
        B, S, K, D = x.shape
        N = K * S
        xp = jnp.transpose(x, (0, 3, 2, 1)).reshape(B, D, N)
        q = jnp.einsum('cd,bdn->bnc', Wq, xp) + bq
        k = jnp.einsum('cd,bdn->bcn', Wk, xp) + bk[:, None]
        energy = jnp.einsum('bnc,bcm->bnm', q, k)
        attention = jax.nn.softmax(energy, axis=-1)
        v = jnp.einsum('ed,bdn->ben', Wv, xp) + bv[:, None]
        out = jnp.einsum('bdj,bij->bdi', v, attention)
        out = gamma * out + xp
        out = out.reshape(B, D, K, S)
        return jnp.transpose(out, (0, 3, 2, 1))

    def _L1_attn_ref(x, Wq, bq, Wk, bk, Wv, bv):
        import jax, jax.numpy as jnp
        import numpy as np
        B, N, D_IN, E, H = (4, 512, 256, 64, 4)
        NEG = 1000000000.0

        def _sdp(q, k, v):
            logits = jnp.einsum('bne,bme->bnm', q, k) / jnp.sqrt(jnp.asarray(E, q.dtype))
            return jnp.einsum('bnm,bme->bne', jax.nn.softmax(logits, axis=-1), v)

        def _cosine(q, k, v):
            qn = q / jnp.linalg.norm(q, axis=-1, keepdims=True)
            kn = k / jnp.linalg.norm(k, axis=-1, keepdims=True)
            logits = jnp.einsum('bne,bme->bnm', qn, kn)
            return jnp.einsum('bnm,bme->bne', jax.nn.softmax(logits, axis=-1), v)

        def _l1(q, k, v):
            d = jnp.sum(jnp.abs(q[:, :, None, :] - k[:, None, :, :]), axis=-1)
            return jnp.einsum('bnm,bme->bne', jax.nn.softmax(-d, axis=-1), v)

        def _l2(q, k, v):
            d = jnp.sqrt(jnp.sum(jnp.square(q[:, :, None, :] - k[:, None, :, :]), axis=-1))
            return jnp.einsum('bnm,bme->bne', jax.nn.softmax(-d, axis=-1), v)
        _HEAD_FNS = (_sdp, _cosine, _l1, _l2)
        q = jnp.einsum('bnd,hde->bhne', x, Wq) + bq[None, :, None, :]
        k = jnp.einsum('bnd,hde->bhne', x, Wk) + bk[None, :, None, :]
        v = jnp.einsum('bnd,hde->bhne', x, Wv) + bv[None, :, None, :]
        outs = [fn(q[:, h], k[:, h], v[:, h]) for h, fn in enumerate(_HEAD_FNS)]
        return jnp.concatenate(outs, axis=-1)

    def _L1_ffn_ref(input_embeddings, router_w, w1, b1, w2, b2):
        import jax, jax.numpy as jnp
        import numpy as np
        NUM_EXPERTS = 8
        TOP_K = 2
        B, S, D = (8, 8192, 256)

        def _moe(tokens, router_w, w1, b1, w2, b2):
            N = tokens.shape[0]
            E = router_w.shape[0]
            logits = tokens.astype(jnp.float32) @ router_w.astype(jnp.float32).T
            probs = jax.nn.softmax(logits, axis=-1)
            rw, re = jax.lax.top_k(probs, TOP_K)
            if TOP_K > 1:
                rw = rw / jnp.maximum(rw.sum(-1, keepdims=True), 1e-12)
            rw = rw.astype(tokens.dtype)
            combine = jnp.zeros((N, E), tokens.dtype).at[jnp.arange(N)[:, None], re].set(rw)
            out = tokens
            for e in range(E):
                h = jax.nn.gelu(tokens @ w1[e] + b1[e], approximate=False)
                y = h @ w2[e] + b2[e]
                out = out + combine[:, e:e + 1] * y
            return out
        b, s, d = input_embeddings.shape
        tokens = input_embeddings.reshape(b * s, d)
        return _moe(tokens, router_w, w1, b1, w2, b2).reshape(b, s, d)

    def _gn(v, G=32, eps=1e-5):
        B_, H_, W_, C_ = v.shape
        g = v.reshape(B_, H_, W_, G, C_ // G)
        m = jnp.mean(g, axis=(1, 2, 4), keepdims=True)
        s = jnp.var(g, axis=(1, 2, 4), keepdims=True)
        return ((g - m) / jnp.sqrt(s + eps)).reshape(v.shape)

    def _ln_c(v, eps=1e-6):
        m = jnp.mean(v, axis=-1, keepdims=True)
        s = jnp.var(v, axis=-1, keepdims=True)
        return (v - m) / jnp.sqrt(s + eps)

    def _ln_t(v, eps=1e-5):
        m = jnp.mean(v, axis=-1, keepdims=True)
        s = jnp.var(v, axis=-1, keepdims=True)
        return (v - m) / jnp.sqrt(s + eps)

    def _to_tokens(v):
        B_, H_, W_, C_ = v.shape
        return v.reshape(B_, H_ * W_, C_)
    def _from_tokens(t, like):
        return t.reshape(like.shape)

    x = _L0_conv_ref(x, L0_conv_Wq, L0_conv_bq, L0_conv_Wk, L0_conv_bk, L0_conv_Wv, L0_conv_bv, L0_conv_gamma)
    t = _to_tokens(x)
    t = t + _L1_attn_ref(_ln_t(t), L1_attn_Wq, L1_attn_bq, L1_attn_Wk, L1_attn_bk, L1_attn_Wv, L1_attn_bv)
    t = t + _L1_ffn_ref(_ln_t(t), L1_ffn_router_w, L1_ffn_w1, L1_ffn_b1, L1_ffn_w2, L1_ffn_b2)
    x = _from_tokens(t, x)
    return x


_drawn_inputs = setup_inputs


def setup_inputs(seed=0):
    import zlib

    import numpy as np

    out = dict(_drawn_inputs(seed))
    spreads = {'L1_attn_bq': (0.0, 0.1),
     'L1_attn_bk': (0.0, 0.1),
     'L1_attn_bv': (0.0, 0.1),
     'L1_ffn_b1': (0.0, 0.331),
     'L1_ffn_b2': (0.0, 0.1)}
    factors = {'L0_conv_bq': 2.87, 'L0_conv_bk': 8.0, 'L0_conv_bv': 2.983}
    for name, (base, spread) in spreads.items():
        noise = np.random.default_rng([zlib.crc32(name.encode()), seed]).standard_normal(out[name].shape)
        drawn = base * np.exp(spread * noise) if base else spread * noise
        out[name] = jnp.asarray(drawn.astype(out[name].dtype))
    for name, factor in factors.items():
        out[name] = (out[name] * factor).astype(out[name].dtype)
    return out
```

```python
from contextlib import ExitStack

import concourse.bass as bass
from concourse import mybir

P = 128
F32 = mybir.dt.float32
ALU = mybir.AluOpType
ACT = mybir.ActivationFunctionType
AX = mybir.AxisListType

B, N, D = 2, 4096, 256
TOKENS = B * N
C0 = D // 8
H, E = 4, 64
EA = E + 2
DC = D // P
TILES = N // P
PAIRS = TILES // 2
SDP, COS, L1, L2 = range(H)
Q_BLOCK = {SDP: 0, COS: 1, L1: 2, L2: 3}
K_BLOCK = {SDP: 4, COS: 5, L2: 6}
BLOCKS = 7
KS = 2 * E + 4
EXPERTS, TOP = 8, 2
LN_EPS = 1e-5
BANK = 512

VECTOR_SHARE = 30
ON_VECTOR = [(e * VECTOR_SHARE) // E != ((e + 1) * VECTOR_SHARE) // E for e in range(E)]
VECTOR_E = [e for e in range(E) if ON_VECTOR[e]]
SCALAR_E = [e for e in range(E) if not ON_VECTOR[e]]


class Place:

    def __init__(self, nc, ctx, stage):
        self.nc, self.ctx, self.stage = nc, ctx, stage

    def sb(self, name, shape):
        return self.ctx.enter_context(self.nc.sbuf_tensor(f"{self.stage}_{name}", shape, F32))

    def ps(self, name, shape):
        return self.ctx.enter_context(self.nc.psum_tensor(f"{self.stage}_{name}", shape, F32))

    def sem(self, name):
        return self.ctx.enter_context(self.nc.semaphore(f"{self.stage}_{name}"))

    def pair(self, name):
        return [self.sem(f"{name}{par}") for par in range(2)]


def project0(nc, xT, wqk, bqk, wv, bv, qT, kT, v):
    G = BANK
    TG = G // P
    LOOPS = TOKENS // G // 2
    with ExitStack() as ctx:
        a = Place(nc, ctx, "project0")
        x_sb = a.sb("x", [P, 2, DC, G])
        wqk_sb = a.sb("wqk", [P, DC, 2 * C0])
        wv_sb = a.sb("wv", [P, DC, D])
        bqk_sb = a.sb("bqk", [C0, 2])
        bv_sb = a.sb("bv", [P, TG, D])
        q_sb = a.sb("q", [C0, 2, G])
        k_sb = a.sb("k", [C0, 2, G])
        v_sb = a.sb("v", [P, 2, TG, D])
        q_ps = a.ps("q_ps", [P, 2, G])
        k_ps = a.ps("k_ps", [P, 2, G])
        v_ps = a.ps("v_ps", [P, 2, TG, D])
        weights_in = a.sem("weights_in")
        x_in = a.pair("x_in")
        qk_ready = a.sem("qk_ready")
        v_ready = a.sem("v_ready")
        qk_out = a.sem("qk_out")
        v_out = a.sem("v_out")
        q_stored = a.sem("q_stored")
        k_stored = a.sem("k_stored")
        v_stored = a.sem("v_stored")
        out_free = a.sem("out_free")
        WEIGHTS = 16 * (3 + TG)
        x_cols = xT.rearrange("(c p) n -> p c n", p=P)
        v_rows = v.rearrange("(t p) d -> p t d", p=P)
        block = ctx.enter_context(nc.Block())

        @block.sync
        def _(sp):
            sp.dma_start(wqk_sb[:, :, :], wqk.rearrange("(c p) m -> p c m", p=P)).then_inc(weights_in, 16)
            sp.dma_start(wv_sb[:, :, :], wv.rearrange("(c p) m -> p c m", p=P)).then_inc(weights_in, 16)
            sp.dma_start(bqk_sb[:, :], bqk).then_inc(weights_in, 16)
            for t in range(TG):
                sp.dma_start(bv_sb[:, t, :], bv.partition_broadcast(P)).then_inc(weights_in, 16)
            with sp.Fori(0, LOOPS) as i:
                for par in range(2):
                    g = 2 * i + par
                    sp.wait_ge(v_out, g + 1)
                    sp.dma_start(x_sb[:, par, :, :], x_cols[:, :, bass.ds(g * G, G)]).then_inc(x_in[par], 16)

        @block.gpsimd
        def _(pool):
            pool.sem_inc(out_free, 2)
            with pool.Fori(0, LOOPS) as i:
                for par in range(2):
                    g = 2 * i + par
                    pool.wait_ge(qk_out, 2 + g + 1)
                    pool.dma_start(qT[:, bass.ds(g * G, G)], q_sb[:, par, :]).then_inc(q_stored, 16)
                    pool.dma_start(kT[:, bass.ds(g * G, G)], k_sb[:, par, :]).then_inc(k_stored, 16)
                    pool.wait_ge(v_out, 2 + g + 1)
                    pool.dma_start(v_rows[:, bass.ds(g * TG, TG), :], v_sb[:, par, :, :]).then_inc(v_stored, 16)
                    for s in (q_stored, k_stored, v_stored):
                        pool.wait_ge(s, 16 * (g + 1))
                    pool.sem_inc(out_free, 1)

        @block.tensor
        def _(pe):
            pe.sem_inc(qk_ready, 2)
            pe.wait_ge(weights_in, WEIGHTS)
            with pe.Fori(0, LOOPS) as i:
                for par in range(2):
                    g = 2 * i + par
                    pe.wait_ge(x_in[par], 16 * (i + 1))
                    pe.wait_ge(qk_out, g + 1)
                    for which, ps in ((0, q_ps), (1, k_ps)):
                        for c in range(DC):
                            mm = pe.matmul(ps[0:C0, par, :], wqk_sb[:, c, which * C0:(which + 1) * C0],
                                           x_sb[:, par, c, :], start=c == 0, stop=c == DC - 1)
                    mm.then_inc(qk_ready, 1)
                    pe.wait_ge(v_out, g + 1)
                    for t in range(TG):
                        for c in range(DC):
                            mm = pe.matmul(v_ps[:, par, t, :], x_sb[:, par, c, t * P:(t + 1) * P],
                                           wv_sb[:, c, :], start=c == 0, stop=c == DC - 1)
                    mm.then_inc(v_ready, 1)

        @block.scalar
        def _(act):
            act.sem_inc(qk_out, 2)
            act.wait_ge(weights_in, WEIGHTS)
            with act.Fori(0, LOOPS) as i:
                for par in range(2):
                    g = 2 * i + par
                    act.wait_ge(qk_ready, 2 + g + 1)
                    act.wait_ge(out_free, g + 1)
                    act.activation(q_sb[:, par, :], q_ps[0:C0, par, :], ACT.Identity, bias=bqk_sb[:, 0:1])
                    act.activation(k_sb[:, par, :], k_ps[0:C0, par, :], ACT.Identity,
                                   bias=bqk_sb[:, 1:2]).then_inc(qk_out, 1)

        @block.vector
        def _(dve):
            dve.sem_inc(v_out, 2)
            dve.wait_ge(weights_in, WEIGHTS)
            with dve.Fori(0, LOOPS) as i:
                for par in range(2):
                    g = 2 * i + par
                    dve.wait_ge(v_ready, g + 1)
                    dve.wait_ge(out_free, g + 1)
                    dve.tensor_tensor(v_sb[:, par, :, :], v_ps[:, par, :, :], bv_sb[:, :, :],
                                      ALU.add).then_inc(v_out, 1)


def attend(nc, stage, heads, width, qT, q_at, kT, k_at, v, kind, finish, scores=None,
           gamma=None, x=None, out=None, identity=None):
    C = qT.shape[0] if qT is not None else 0
    W = 1024
    SC = N // W
    TC = N // BANK
    KT = BANK // P
    dot, l2, l1 = kind == "dot", kind == "l2", kind == "l1"
    with ExitStack() as ctx:
        a = Place(nc, ctx, stage)
        s_sb = a.sb("s", [P, 2, N])
        t_sb = a.sb("t", [P, 2, BANK])
        v_sb = a.sb("v", [P, TILES, width])
        ident = a.sb("ident", [P, P])
        part = a.sb("part", [P, 2, SC])
        shift = a.sb("shift", [P, 2, 1])
        total = a.sb("total", [P, 2, 1])
        recip = a.sb("recip", [P, 2, 1])
        scale = a.sb("scale", [P, 2, 1])
        gam = a.sb("gam", [P, 1])
        o_sb = a.sb("o", [P, 2, width])
        x_sb = a.sb("x", [P, 2, width])
        if not l1:
            k_sb = a.sb("k", [C, N])
            q_sb = a.sb("q", [C, 2, P])
            s_ps = a.ps("s_ps", [P, 2, W])
        t_ps = a.ps("t_ps", [P, 2, BANK])
        o_ps = a.ps("o_ps", [P, 2, BANK])
        const_in = a.sem("const_in")
        v_in = a.sem("v_in")
        kv_free = a.sem("kv_free")
        q_in = a.pair("q_in")
        if finish == "residual":
            x_in = a.pair("x_in")
        if not l1:
            k_in = a.sem("k_in")
            s_ready = a.sem("s_ready")
            s_copied = a.sem("s_copied")
        m_ready = a.sem("m_ready")
        if l2:
            r_ready = a.sem("r_ready")
        p_ready = a.sem("p_ready")
        t_ready = a.sem("t_ready")
        t_copied = a.sem("t_copied")
        pv_done = a.sem("pv_done")
        rc_ready = a.sem("rc_ready")
        o_done = a.sem("o_done")
        stored = a.sem("stored")
        o_free = a.sem("o_free")
        CONST = 16 * (2 if finish == "residual" else 1)
        block = ctx.enter_context(nc.Block())

        def tiles(eng, first, middle, last):
            with eng.Fori(0, heads) as u:
                k0 = u * PAIRS
                first(u, k0, 0)
                with eng.Fori(0, PAIRS - 1) as j:
                    k = k0 + j
                    middle(u, k, 1, k, 0)
                    middle(u, k + 1, 0, k, 1)
                middle(u, k0 + PAIRS - 1, 1, k0 + PAIRS - 1, 0)
                last(u, k0 + PAIRS - 1, 1)

        @block.sync
        def _(sp):
            sp.dma_start(ident[:, :], identity).then_inc(const_in, 16)
            if finish == "residual":
                sp.dma_start(gam[:, :], gamma.partition_broadcast(P)).then_inc(const_in, 16)

            def q_tile(k, par):
                n = (2 * k + par) * P
                if l1:
                    sp.wait_ge(t_ready, TC * (2 * k + par + 1))
                    sp.dma_start(s_sb[:, par, :], scores[bass.ds(n, P), :]).then_inc(q_in[par], 16)
                else:
                    sp.wait_ge(s_ready, SC * (2 * k + par + 1))
                    sp.dma_start(q_sb[:, par, :], qT[:, bass.ds(q_at + n, P)]).then_inc(q_in[par], 16)
                if finish == "residual":
                    sp.wait_ge(o_done, 2 * k + par + 1)
                    sp.dma_start(x_sb[:, par, :], x[bass.ds(n, P), :]).then_inc(x_in[par], 16)

            with sp.Fori(0, heads) as u:
                sp.wait_ge(kv_free, u + 1)
                if not l1:
                    sp.dma_start(k_sb[:, :], kT[:, bass.ds(k_at + u * N, N)]).then_inc(k_in, 16)
                for half in range(2):
                    sp.dma_start(v_sb[:, half * PAIRS:(half + 1) * PAIRS, :], v.rearrange("(t p) d -> p t d", p=P)[
                        :, bass.ds(u * TILES + half * PAIRS, PAIRS), :]).then_inc(v_in, 16)
                with sp.Fori(0, PAIRS) as j:
                    q_tile(u * PAIRS + j, 0)
                    q_tile(u * PAIRS + j, 1)

        @block.gpsimd
        def _(pool):
            pool.sem_inc(o_free, 2)
            with pool.Fori(0, heads * PAIRS) as k:
                for par in range(2):
                    pool.wait_ge(o_done, 2 + 2 * k + par + 1)
                    pool.dma_start(out[bass.ds((2 * k + par) * P, P), :], o_sb[:, par, :]).then_inc(stored, 16)
                    pool.wait_ge(stored, 16 * (2 * k + par + 1))
                    pool.sem_inc(o_free, 1)

        @block.tensor
        def _(pe):
            if not l1:
                pe.sem_inc(s_ready, 2 * SC)
            pe.sem_inc(t_ready, 2 * TC)
            pe.sem_inc(pv_done, 2)
            pe.sem_inc(kv_free, 1)
            pe.wait_ge(const_in, CONST)

            def make_scores(k, par):
                g = 2 * k + par
                pe.wait_ge(q_in[par], 16 * (k + 1))
                for c in range(SC):
                    pe.wait_ge(s_copied, SC * g + c + 1)
                    for w in range(0, W, BANK):
                        mm = pe.matmul(s_ps[:, c % 2, w:w + BANK], q_sb[:, par, :],
                                       k_sb[:, c * W + w:c * W + w + BANK], start=True, stop=True)
                    mm.then_inc(s_ready, 1)

            def turn(k, par, c):
                i = TC * (2 * k + par) + c
                pe.wait_ge(t_copied, i + 1)
                for j in range(KT):
                    at = c * BANK + j * P
                    mm = pe.transpose(t_ps[:, c % 2, j * P:(j + 1) * P], s_sb[:, par, at:at + P], ident[:, :])
                mm.then_inc(t_ready, 1)

            def times_v(k, par, c):
                i = TC * (2 * k + par) + c
                pe.wait_ge(t_copied, 2 + i + 1)
                for j in range(KT):
                    mm = pe.matmul(o_ps[:, par, 0:width], t_sb[:, c % 2, j * P:(j + 1) * P],
                                   v_sb[:, c * KT + j, :], start=(c == 0 and j == 0),
                                   stop=(c == TC - 1 and j == KT - 1))
                mm.then_inc(pv_done, 1)

            def use_tile(u, k, par):
                g = 2 * k + par
                pe.wait_ge(v_in, 32 * (u + 1))
                pe.wait_ge(p_ready, g + 1)
                pe.wait_ge(o_done, g + 1)
                turn(k, par, 0)
                for c in range(1, TC):
                    turn(k, par, c)
                    times_v(k, par, c - 1)
                times_v(k, par, TC - 1)

            def first(u, k, par):
                if not l1:
                    pe.wait_ge(k_in, 16 * (u + 1))
                    make_scores(k, par)

            def middle(u, k, par, kb, parb):
                if not l1:
                    make_scores(k, par)
                use_tile(u, kb, parb)

            def last(u, k, par):
                use_tile(u, k, par)
                pe.wait_ge(pv_done, 2 + TC * (2 * k + par + 1))
                pe.sem_inc(kv_free, 1)

            tiles(pe, first, middle, last)

        @block.vector
        def _(dve):
            if not l1:
                dve.sem_inc(s_copied, 2)
            dve.sem_inc(t_copied, 2)
            dve.sem_inc(o_done, 2)
            dve.wait_ge(const_in, CONST)

            def take_scores(k, par):
                g = 2 * k + par
                if l1:
                    dve.wait_ge(q_in[par], 16 * (k + 1))
                    dve.wait_ge(t_ready, TC * (g + 1))
                    dve.tensor_reduce(shift[:, par, :], s_sb[:, par, :], AX.X, ALU.min).then_inc(m_ready, 1)
                    return
                dve.wait_ge(t_ready, TC * (g + 1))
                for c in range(SC):
                    dve.wait_ge(s_ready, 2 * SC + SC * g + c + 1)
                    dve.tensor_scalar(s_sb[:, par, c * W:(c + 1) * W], s_ps[:, c % 2, :], 0.0, None,
                                      ALU.max if l2 else ALU.add, ALU.min if l2 else ALU.max,
                                      accum_out=part[:, par, c:c + 1]).then_inc(s_copied, 1)
                dve.wait_ge(s_copied, 2 + SC * (g + 1))
                if l2:
                    dve.tensor_reduce(shift[:, par, :], part[:, par, :], AX.X, ALU.min).then_inc(m_ready, 1)
                else:
                    dve.tensor_reduce(shift[:, par, :], part[:, par, :], AX.X, ALU.max,
                                      negate=True).then_inc(m_ready, 1)

            def use_tile(k, par):
                g = 2 * k + par
                for c in range(TC):
                    i = TC * g + c
                    dve.wait_ge(t_ready, 2 * TC + i + 1)
                    dve.wait_ge(pv_done, i + 1)
                    dve.tensor_copy(t_sb[:, c % 2, :], t_ps[:, c % 2, :]).then_inc(t_copied, 1)
                dve.wait_ge(p_ready, g + 1)
                dve.reciprocal(recip[:, par, :], total[:, par, :]).then_inc(rc_ready, 1)
                dve.wait_ge(o_free, g + 1)
                if finish == "residual":
                    dve.wait_ge(rc_ready, 2 * g + 1)
                    dve.tensor_tensor(scale[:, par, :], recip[:, par, :], gam[:, :], ALU.mult).then_inc(rc_ready, 1)
                    dve.wait_ge(rc_ready, 2 * g + 2)
                    dve.wait_ge(x_in[par], 16 * (k + 1))
                    dve.wait_ge(pv_done, 2 + TC * (g + 1))
                    dve.scalar_tensor_tensor(o_sb[:, par, :], o_ps[:, par, 0:width], scale[:, par, :],
                                             x_sb[:, par, :], ALU.mult, ALU.add).then_inc(o_done, 1)
                else:
                    dve.wait_ge(rc_ready, g + 1)
                    dve.wait_ge(pv_done, 2 + TC * (g + 1))
                    dve.tensor_scalar(o_sb[:, par, :], o_ps[:, par, 0:width], recip[:, par, :], None,
                                      ALU.mult).then_inc(o_done, 1)

            def middle(u, k, par, kb, parb):
                take_scores(k, par)
                use_tile(kb, parb)

            tiles(dve, lambda u, k, par: take_scores(k, par), middle, lambda u, k, par: use_tile(k, par))

        @block.scalar
        def _(act):
            with act.Fori(0, heads * PAIRS) as k:
                for par in range(2):
                    g = 2 * k + par
                    act.wait_ge(m_ready, g + 1)
                    act.wait_ge(o_done, g + 1)
                    if l2:
                        act.activation(s_sb[:, par, :], s_sb[:, par, :], ACT.Sqrt)
                        act.activation(shift[:, par, :], shift[:, par, :], ACT.Sqrt).then_inc(r_ready, 1)
                        act.wait_ge(r_ready, g + 1)
                    act.activation(s_sb[:, par, :], s_sb[:, par, :], ACT.Exp, bias=shift[:, par, :],
                                   scale=1.0 if dot else -1.0,
                                   accum_out=total[:, par, :]).then_inc(p_ready, 1)


def project1(nc, t1, wqkv, bqkv, share, identity, qkT, ks, v):
    HE = H * E
    MT = TOKENS // P
    with ExitStack() as ctx:
        a = Place(nc, ctx, "project1")
        ident = a.sb("ident", [P, P])
        w_sb = a.sb("w", [P, DC, 3 * HE])
        b_sb = a.sb("b", [P, 3 * HE])
        share_sb = a.sb("share", [P, E])
        eps = a.sb("eps", [P, 1])
        x_sb = a.sb("x", [P, 2, D])
        stats = a.sb("stats", [P, 2, 6])
        mean_var = a.sb("mean_var", [P, 2, 2])
        std = a.sb("std", [P, 2, 1])
        rstd = a.sb("rstd", [P, 2, 1])
        n_sb = a.sb("n", [P, 2, D])
        nT_sb = a.sb("nT", [P, 2, DC, P])
        raw = a.sb("raw", [P, 2, 2 * H, E])
        square = a.sb("square", [P, 2, 2 * H, E])
        norm2 = a.sb("norm2", [P, 2, 2 * H])
        norm = a.sb("norm", [P, 2, 2 * H])
        rnorm = a.sb("rnorm", [P, 2, 2 * H])
        forms = a.sb("forms", [P, 2, BLOCKS, EA])
        junk = a.sb("junk", [P, 2, E])
        ks_sb = a.sb("ks", [P, 2, KS])
        v_sb = a.sb("v", [P, 2, H, E])
        fT_sb = a.sb("fT", [EA, 2, BLOCKS, P])
        nT_ps = a.ps("nT_ps", [P, 2, BANK])
        p_ps = a.ps("p_ps", [P, 2, 2 * BANK])
        fT_ps = a.ps("fT_ps", [EA, 2 * BANK])
        const_in = a.sem("const_in")
        preset = a.sem("preset")
        x_in = a.pair("x_in")
        steps = a.sem("steps")
        std_ready = a.sem("std_ready")
        n_ready = a.sem("n_ready")
        nT_ready = a.sem("nT_ready")
        nT_copied = a.sem("nT_copied")
        p_ready = a.sem("p_ready")
        raw_ready = a.sem("raw_ready")
        norm_ready = a.sem("norm_ready")
        rnorm_ready = a.sem("rnorm_ready")
        f_ready = a.sem("f_ready")
        fT_ready = a.sem("fT_ready")
        fT_copied = a.sem("fT_copied")
        stored_f = a.sem("stored_f")
        stored_k = a.sem("stored_k")
        stored_v = a.sem("stored_v")
        out_free = a.sem("out_free")
        CONST = 16 * 4
        qkT_blocks = qkT.rearrange("e (k n) -> e k n", k=BLOCKS)
        v_rows = v.rearrange("(h n) e -> n h e", h=H)
        block = ctx.enter_context(nc.Block())

        @block.sync
        def _(sp):
            sp.dma_start(ident[:, :], identity).then_inc(const_in, 16)
            sp.dma_start(w_sb[:, :, :], wqkv.rearrange("(c p) m -> p c m", p=P)).then_inc(const_in, 16)
            sp.dma_start(b_sb[:, :], bqkv.partition_broadcast(P)).then_inc(const_in, 16)
            sp.dma_start(share_sb[:, :], share.partition_broadcast(P)).then_inc(const_in, 16)
            with sp.Fori(0, MT // 2) as k:
                for par in range(2):
                    g = 2 * k + par
                    sp.wait_ge(n_ready, g + 1)
                    sp.dma_start(x_sb[:, par, :], t1[bass.ds(g * P, P), :]).then_inc(x_in[par], 16)

        @block.gpsimd
        def _(pool):
            pool.sem_inc(out_free, 2)
            with pool.Fori(0, MT // 2) as k:
                for par in range(2):
                    g = 2 * k + par
                    pool.wait_ge(f_ready, 2 + g + 1)
                    pool.dma_start(ks[bass.ds(g * P, P), :], ks_sb[:, par, :]).then_inc(stored_k, 16)
                    pool.dma_start(v_rows[bass.ds(g * P, P), :, :], v_sb[:, par, :, :]).then_inc(stored_v, 16)
                    pool.wait_ge(fT_copied, 1 + g + 1)
                    pool.dma_start(qkT_blocks[:, :, bass.ds(g * P, P)], fT_sb[:, par, :, :]).then_inc(stored_f, 16)
                    for s in (stored_k, stored_v, stored_f):
                        pool.wait_ge(s, 16 * (g + 1))
                    pool.sem_inc(out_free, 1)

        @block.tensor
        def _(pe):
            pe.sem_inc(fT_ready, 2)
            pe.sem_inc(p_ready, 2)
            pe.wait_ge(const_in, CONST)

            def project(k, par):
                g = 2 * k + par
                pe.wait_ge(n_ready, 2 + g + 1)
                pe.wait_ge(nT_copied, g + 1)
                for c in range(DC):
                    mm = pe.transpose(nT_ps[:, par, c * P:(c + 1) * P], n_sb[:, par, c * P:(c + 1) * P], ident[:, :])
                mm.then_inc(nT_ready, 1)
                pe.wait_ge(nT_copied, 2 + g + 1)
                pe.wait_ge(raw_ready, 3 * (g + 1))
                for at, n in ((0, BANK), (BANK, 3 * HE - BANK)):
                    for c in range(DC):
                        mm = pe.matmul(p_ps[:, par, at:at + n], nT_sb[:, par, c, :], w_sb[:, c, at:at + n],
                                       start=c == 0, stop=c == DC - 1)
                mm.then_inc(p_ready, 1)

            def turn_forms(k, par):
                g = 2 * k + par
                pe.wait_ge(f_ready, 2 + g + 1)
                pe.wait_ge(fT_copied, g + 1)
                for m in range(BLOCKS):
                    mm = pe.transpose(fT_ps[:, m * P:(m + 1) * P], forms[:, par, m, :], ident[:, :])
                mm.then_inc(fT_ready, 1)

            with pe.Fori(0, MT // 2) as k:
                project(k, 0)
                project(k, 1)
                turn_forms(k, 0)
                turn_forms(k, 1)

        @block.scalar
        def _(act):
            act.sem_inc(nT_copied, 2)
            act.sem_inc(fT_copied, 1)
            act.wait_ge(preset, 1)

            def norms(k, par):
                g = 2 * k + par
                act.wait_ge(steps, 3 * g + 3)
                act.activation(std[:, par, :], mean_var[:, par, 1:2], ACT.Sqrt, bias=eps[:, :]).then_inc(std_ready, 1)
                act.wait_ge(nT_ready, g + 1)
                act.wait_ge(p_ready, g + 1)
                act.copy(nT_sb[:, par, :, :], nT_ps[:, par, 0:D]).then_inc(nT_copied, 1)

            def head_norms(k, par):
                g = 2 * k + par
                act.wait_ge(raw_ready, 6 + 3 * g + 3)
                act.activation(norm[:, par, :], norm2[:, par, :], ACT.Sqrt).then_inc(norm_ready, 1)

            def take_forms(k, par):
                g = 2 * k + par
                act.wait_ge(fT_ready, 2 + g + 1)
                act.wait_ge(out_free, g + 1)
                act.copy(fT_sb[:, par, :, :], fT_ps[:, 0:BLOCKS * P]).then_inc(fT_copied, 1)

            with act.Fori(0, MT // 2) as k:
                norms(k, 0)
                norms(k, 1)
                head_norms(k, 0)
                head_norms(k, 1)
                take_forms(k, 0)
                take_forms(k, 1)

        @block.vector
        def _(dve):
            dve.sem_inc(n_ready, 2)
            dve.sem_inc(raw_ready, 6)
            dve.sem_inc(f_ready, 2)
            dve.memset(eps[:, :], LN_EPS)
            dve.memset(ks_sb[:, :, :], 0.0)
            dve.memset(forms[:, :, :, E:EA], 0.0).then_inc(steps, 1)
            dve.wait_ge(steps, 1)
            dve.memset(forms[:, :, Q_BLOCK[L2], E + 1:E + 2], 1.0)
            dve.memset(forms[:, :, K_BLOCK[L2], E:E + 1], 1.0).then_inc(preset, 1)
            dve.wait_ge(preset, 1)
            dve.wait_ge(const_in, CONST)

            def normalise(k, par):
                g = 2 * k + par
                dve.wait_ge(x_in[par], 16 * (k + 1))
                dve.bn_stats(stats[:, par, :], x_sb[:, par, :]).then_inc(steps, 1)
                dve.wait_ge(steps, 3 * g + 2)
                dve.memset(junk[:, par, 0:1], 0.0)
                dve.bn_aggr(mean_var[:, par, :], stats[:, par, :]).then_inc(steps, 1)
                dve.wait_ge(std_ready, g + 1)
                dve.reciprocal(rstd[:, par, :], std[:, par, :]).then_inc(steps, 1)
                dve.wait_ge(steps, 3 * g + 4)
                dve.wait_ge(nT_copied, g + 1)
                dve.tensor_scalar(n_sb[:, par, :], x_sb[:, par, :], mean_var[:, par, 0:1], rstd[:, par, :],
                                  ALU.subtract, ALU.mult).then_inc(n_ready, 1)

            def take_products(k, par):
                g = 2 * k + par
                dve.wait_ge(p_ready, 2 + g + 1)
                dve.wait_ge(out_free, g + 1)
                dve.tensor_tensor(raw[:, par, :, :], p_ps[:, par, 0:2 * HE], b_sb[:, 0:2 * HE],
                                  ALU.add).then_inc(raw_ready, 1)
                dve.tensor_tensor(v_sb[:, par, :, :], p_ps[:, par, 2 * HE:3 * HE], b_sb[:, 2 * HE:3 * HE], ALU.add)
                dve.wait_ge(raw_ready, 6 + 3 * g + 1)
                dve.tensor_tensor(square[:, par, :, :], raw[:, par, :, :], raw[:, par, :, :],
                                  ALU.mult).then_inc(raw_ready, 1)
                dve.wait_ge(raw_ready, 6 + 3 * g + 2)
                dve.tensor_reduce(norm2[:, par, :], square[:, par, :, :], AX.X, ALU.add).then_inc(raw_ready, 1)

            def make_forms(k, par):
                g = 2 * k + par
                q, kk, f = raw[:, par, 0:H, :], raw[:, par, H:2 * H, :], forms[:, par, :, :]
                dve.wait_ge(norm_ready, g + 1)
                dve.reciprocal(rnorm[:, par, :], norm[:, par, :]).then_inc(rnorm_ready, 1)
                dve.wait_ge(fT_copied, g)
                dve.tensor_scalar(f[:, Q_BLOCK[SDP], 0:E], q[:, SDP, :], float(E) ** -0.5, None, ALU.mult)
                dve.tensor_scalar(f[:, Q_BLOCK[L1], 0:E], q[:, L1, :], 2.0, None, ALU.mult)
                dve.tensor_scalar(f[:, Q_BLOCK[L2], 0:E], q[:, L2, :], -2.0, None, ALU.mult)
                dve.tensor_copy(f[:, K_BLOCK[SDP], 0:E], kk[:, SDP, :])
                dve.tensor_copy(f[:, K_BLOCK[L2], 0:E], kk[:, L2, :])
                dve.wait_ge(raw_ready, 6 + 3 * g + 3)
                dve.tensor_copy(f[:, Q_BLOCK[L2], E:E + 1], norm2[:, par, L2:L2 + 1])
                dve.tensor_copy(f[:, K_BLOCK[L2], E + 1:E + 2], norm2[:, par, H + L2:H + L2 + 1])
                dve.tensor_scalar(ks_sb[:, par, 0:E], kk[:, L1, :], 2.0, None, ALU.mult)
                dve.tensor_scalar(ks_sb[:, par, E:2 * E], kk[:, L1, :], -1.0, None, ALU.mult)
                dve.tensor_tensor_reduce(junk[:, par, :], kk[:, L1, :], share_sb[:, :], 1.0, 0.0,
                                         ALU.mult, ALU.add, ks_sb[:, par, 2 * E:2 * E + 1])
                dve.wait_ge(rnorm_ready, g + 1)
                dve.tensor_scalar(f[:, Q_BLOCK[COS], 0:E], q[:, COS, :], rnorm[:, par, COS:COS + 1], None, ALU.mult)
                dve.tensor_scalar(f[:, K_BLOCK[COS], 0:E], kk[:, COS, :], rnorm[:, par, H + COS:H + COS + 1], None,
                                  ALU.mult).then_inc(f_ready, 1)

            with dve.Fori(0, MT // 2) as k:
                normalise(k, 0)
                normalise(k, 1)
                take_products(k, 0)
                take_products(k, 1)
                make_forms(k, 0)
                make_forms(k, 1)


def distances(nc, qkT, ks, identity, out):
    QW = BANK
    QT = QW // P
    KT = 4
    STEPS = N // (KT * P)
    HELD = TOKENS // QW
    TURN = 4
    n_abs = len(SCALAR_E) * KT
    n_acc = len(VECTOR_E) * KT
    with ExitStack() as ctx:
        a = Place(nc, ctx, "distances")
        q_sb = a.sb("q", [P, E, QW])
        ks_sb = a.sb("ks", [P, 2, KT, KS])
        ident = a.sb("ident", [P, P])
        acc = a.sb("acc", [P, 2, KT, QW])
        diff = a.sb("diff", [P, TURN, QW])
        d_sb = a.sb("d", [P, 2, QT, KT * P])
        d_ps = a.ps("d_ps", [P, 2, KT, QW])
        const_in = a.sem("const_in")
        q_in = [a.sem(f"q_in{i}") for i in range(E // 8)]
        ks_in = a.pair("ks_in")
        acc_done = a.sem("acc_done")
        abs_done = a.sem("abs_done")
        turned = a.sem("turned")
        d_ready = a.sem("d_ready")
        d_copied = a.sem("d_copied")
        stored = a.pair("stored")
        FLUSH = 6
        first_q = Q_BLOCK[L1] * TOKENS
        PART = E // len(q_in)
        block = ctx.enter_context(nc.Block())

        def steps(eng, body):
            with eng.Fori(0, HELD) as i:
                with eng.Fori(0, STEPS // 2) as j:
                    for par in range(2):
                        body(i, i * (STEPS // 2) + j, par)

        @block.sync
        def _(sp):
            sp.sem_inc(stored[0], 16)
            sp.sem_inc(stored[1], 32)
            sp.dma_start(ident[:, :], identity).then_inc(const_in, 16)
            ks_tiles = ks.rearrange("(t p) m -> p t m", p=P)
            out_tiles = out.rearrange("(t p) n -> p t n", p=P)
            HALF = STEPS // 2

            def load_ks(k, par):
                batch = k // (HALF * HELD // B)
                step = 2 * (k % HALF) + par
                sp.dma_start(ks_sb[:, par, :, :], ks_tiles[:, bass.ds(batch * TILES + step * KT, KT), :]
                             ).then_inc(ks_in[par], 16)

            def store(k, par):
                step = 2 * (k % HALF) + par
                sp.dma_start(out_tiles[:, bass.ds((k // HALF) * QT, QT), bass.ds(step * KT * P, KT * P)],
                             d_sb[:, par, :, :]).then_inc(stored[par], 16)

            load_ks(0, 0)
            load_ks(0, 1)
            with sp.Fori(0, HELD * HALF - 1) as k:
                for par in range(2):
                    sp.wait_ge(d_copied, 2 + 2 * k + par + 1)
                    load_ks(k + 1, par)
                    store(k, par)
            for par in range(2):
                sp.wait_ge(d_copied, 2 + 2 * (HELD * HALF - 1) + par + 1)
                store(HELD * HALF - 1, par)
            sp.wait_ge(stored[0], 16 * (HELD * HALF + 1))
            sp.wait_ge(stored[1], 16 * (HELD * HALF + 2))

        @block.gpsimd
        def _(pool):
            with pool.Fori(0, HELD) as i:
                for part, s in enumerate(q_in):
                    e = part * PART
                    rows_v = sum(ON_VECTOR[:e + PART])
                    pool.wait_ge(acc_done, n_acc * STEPS * i + rows_v * KT)
                    pool.wait_ge(abs_done, n_abs * STEPS * i + (e + PART - rows_v) * KT)
                    pool.dma_start(q_sb[:, e:e + PART, :],
                                   qkT[e:e + PART, bass.ds(first_q + i * QW, QW)].partition_broadcast(P)
                                   ).then_inc(s, 16)

        @block.tensor
        def _(pe):
            pe.sem_inc(turned, TURN)
            pe.sem_inc(d_ready, 2 * KT)
            pe.wait_ge(const_in, 16)

            def turn(tile, par, j, src, start, stop):
                for t in range(QT):
                    mm = pe.matmul(d_ps[:, par, j, t * P:(t + 1) * P], src[:, t * P:(t + 1) * P], ident[:, :],
                                   is_transpose=True, start=start and t == 0, stop=stop, skip_group_check=True)
                return mm

            def body(i, k, par):
                g = 2 * k + par
                pe.wait_ge(d_copied, g + 1)
                for n in range(n_abs):
                    j = n % KT
                    pe.wait_ge(abs_done, n_abs + n_abs * g + n + 1)
                    turn(g, par, j, diff[:, n % TURN, :], n < KT, False).then_inc(turned, 1)
                pe.wait_ge(acc_done, n_acc + n_acc * (g + 1))
                for j in range(KT):
                    turn(g, par, j, acc[:, par, j, :], False, True).then_inc(d_ready, 1)

            steps(pe, body)

        @block.scalar
        def _(act):
            act.sem_inc(abs_done, n_abs)

            def body(i, k, par):
                g = 2 * k + par
                act.wait_ge(ks_in[par], 16 * (k + 1))
                n = 0
                for e in SCALAR_E:
                    act.wait_ge(q_in[e // PART], 16 * (i + 1))
                    for j in range(KT):
                        act.wait_ge(turned, n_abs * g + n + 1)
                        act.activation(diff[:, n % TURN, :], q_sb[:, e, :], ACT.Abs,
                                       bias=ks_sb[:, par, j, E + e:E + e + 1], scale=0.5).then_inc(abs_done, 1)
                        n += 1

            steps(act, body)

        @block.vector
        def _(dve):
            dve.sem_inc(acc_done, n_acc)
            dve.sem_inc(d_copied, 1)
            dve.memset(d_ps[:, 1, :, :], 0.0)

            def take_distances(par, ready):
                for j in range(KT):
                    dve.wait_ge(d_ready, ready + j + 1)
                    ins = dve.tensor_copy(d_sb[:, par, :, j * P:(j + 1) * P], d_ps[:, par, j, :])
                ins.then_inc(d_copied, 1)

            def body(i, k, par):
                g = 2 * k + par
                dve.wait_ge(ks_in[par], 16 * (k + 1))
                dve.wait_ge(d_ready, KT * (g + 1))
                for r, e in enumerate(VECTOR_E):
                    dve.wait_ge(q_in[e // PART], 16 * (i + 1))
                    for j in range(KT):
                        k2 = ks_sb[:, par, j, e:e + 1]
                        if r == 0:
                            dve.tensor_scalar(acc[:, par, j, :], q_sb[:, e, :], k2,
                                              ks_sb[:, par, j, 2 * E:2 * E + 1], ALU.max, ALU.subtract
                                              ).then_inc(acc_done, 1)
                        else:
                            dve.wait_ge(acc_done, n_acc + n_acc * g + KT * (r - 1) + j + 1)
                            dve.scalar_tensor_tensor(acc[:, par, j, :], q_sb[:, e, :], k2,
                                                     acc[:, par, j, :], ALU.max, ALU.add).then_inc(acc_done, 1)
                    if r == FLUSH:
                        dve.wait_ge(stored[1 - par], 16 * (k + 1))
                        take_distances(1 - par, 2 * KT + KT * (g - 1))

            steps(dve, body)
            dve.wait_ge(stored[1], 16 * (HELD * STEPS // 2 + 1))
            take_distances(1, 2 * KT + KT * (HELD * STEPS - 1))


def route(nc, t1, attended, routerT, identity, base, uT, weights):
    MT = TOKENS // P
    with ExitStack() as ctx:
        a = Place(nc, ctx, "route")
        ident = a.sb("ident", [P, P])
        r_sb = a.sb("r", [P, DC, EXPERTS])
        eps = a.sb("eps", [P, 1])
        x_sb = a.sb("x", [P, 2, D])
        att_sb = a.sb("att", [P, 2, H, E])
        t2_sb = a.sb("t2", [P, 2, D])
        stats = a.sb("stats", [P, 2, 6])
        mean_var = a.sb("mean_var", [P, 2, 2])
        std = a.sb("std", [P, 2, 1])
        rstd = a.sb("rstd", [P, 2, 1])
        u_sb = a.sb("u", [P, 2, D])
        junk = a.sb("junk", [P, 1])
        base_sb = a.sb("base", [P, 2, D])
        uT_sb = a.sb("uT", [P, 2, DC, P])
        logits = a.sb("logits", [P, MT, EXPERTS])
        probs = a.sb("probs", [P, MT, EXPERTS])
        rank = a.sb("rank", [P, MT, EXPERTS])
        above = a.sb("above", [P, MT, EXPERTS])
        row = a.sb("row", [P, MT])
        w_sb = a.sb("w", [P, MT, EXPERTS])
        uT_ps = a.ps("uT_ps", [P, 2, BANK])
        l_ps = a.ps("l_ps", [P, 2, BANK])
        const_in = a.sem("const_in")
        preset = a.sem("preset")
        x_in = a.pair("x_in")
        att_in = a.pair("att_in")
        steps = a.sem("steps")
        std_ready = a.sem("std_ready")
        u_ready = a.sem("u_ready")
        base_ready = a.sem("base_ready")
        uT_ready = a.sem("uT_ready")
        uT_copied = a.sem("uT_copied")
        l_ready = a.sem("l_ready")
        l_copied = a.sem("l_copied")
        stored_b = a.sem("stored_b")
        stored_u = a.sem("stored_u")
        out_free = a.sem("out_free")
        choice = a.sem("choice")
        exp_done = a.sem("exp_done")
        w_ready = a.sem("w_ready")
        stored_w = a.sem("stored_w")
        CONST = 16 * 2
        att_rows = attended.rearrange("(h n) e -> n h e", h=H)
        uT_cols = uT.rearrange("(c p) n -> p c n", p=P)
        block = ctx.enter_context(nc.Block())

        @block.sync
        def _(sp):
            sp.dma_start(ident[:, :], identity).then_inc(const_in, 16)
            sp.dma_start(r_sb[:, :, :], routerT.rearrange("(c p) e -> p c e", p=P)).then_inc(const_in, 16)
            with sp.Fori(0, MT // 2) as k:
                for par in range(2):
                    g = 2 * k + par
                    sp.wait_ge(u_ready, g + 1)
                    sp.dma_start(x_sb[:, par, :], t1[bass.ds(g * P, P), :]).then_inc(x_in[par], 16)
                    sp.dma_start(att_sb[:, par, :, :], att_rows[bass.ds(g * P, P), :, :]).then_inc(att_in[par], 16)
            sp.wait_ge(w_ready, 1)
            sp.dma_start(weights.rearrange("(t p) e -> p t e", p=P), w_sb[:, :, :]).then_inc(stored_w, 16)
            sp.wait_ge(stored_w, 16)

        @block.gpsimd
        def _(pool):
            pool.sem_inc(out_free, 2)
            with pool.Fori(0, MT // 2) as k:
                for par in range(2):
                    g = 2 * k + par
                    pool.wait_ge(base_ready, 2 + g + 1)
                    pool.dma_start(base[bass.ds(g * P, P), :], base_sb[:, par, :]).then_inc(stored_b, 16)
                    pool.wait_ge(uT_copied, 2 + g + 1)
                    pool.dma_start(uT_cols[:, :, bass.ds(g * P, P)], uT_sb[:, par, :, :]).then_inc(stored_u, 16)
                    pool.wait_ge(stored_b, 16 * (g + 1))
                    pool.wait_ge(stored_u, 16 * (g + 1))
                    pool.sem_inc(out_free, 1)

        @block.tensor
        def _(pe):
            pe.sem_inc(l_ready, 2)
            pe.wait_ge(const_in, CONST)
            with pe.Fori(0, MT // 2) as k:
                for par in range(2):
                    g = 2 * k + par
                    pe.wait_ge(u_ready, 2 + g + 1)
                    pe.wait_ge(uT_copied, g + 1)
                    for c in range(DC):
                        mm = pe.transpose(uT_ps[:, par, c * P:(c + 1) * P], u_sb[:, par, c * P:(c + 1) * P], ident[:, :])
                    mm.then_inc(uT_ready, 1)
                    pe.wait_ge(uT_copied, 2 + g + 1)
                    pe.wait_ge(l_copied, g + 1)
                    for c in range(DC):
                        mm = pe.matmul(l_ps[:, par, 0:EXPERTS], uT_sb[:, par, c, :], r_sb[:, c, :],
                                       start=c == 0, stop=c == DC - 1)
                    mm.then_inc(l_ready, 1)

        @block.scalar
        def _(act):
            act.sem_inc(uT_copied, 2)
            act.wait_ge(preset, 1)
            with act.Fori(0, MT // 2) as k:
                for par in range(2):
                    g = 2 * k + par
                    act.wait_ge(steps, 4 * g + 3)
                    act.activation(std[:, par, :], mean_var[:, par, 1:2], ACT.Sqrt, bias=eps[:, :]).then_inc(std_ready, 1)
                    act.wait_ge(uT_ready, g + 1)
                    act.wait_ge(l_ready, g + 1)
                    act.wait_ge(out_free, g + 1)
                    act.copy(uT_sb[:, par, :, :], uT_ps[:, par, 0:D]).then_inc(uT_copied, 1)
            act.wait_ge(choice, 2)
            act.activation(probs[:, :, :], logits[:, :, :], ACT.Exp).then_inc(exp_done, 1)

        @block.vector
        def _(dve):
            dve.sem_inc(u_ready, 2)
            dve.sem_inc(base_ready, 2)
            dve.sem_inc(l_copied, 2)
            dve.memset(eps[:, :], LN_EPS).then_inc(preset, 1)

            def take_logits(k, par):
                g = 2 * k + par
                dve.wait_ge(l_ready, 2 + g + 1)
                dve.tensor_copy(logits[:, bass.ds(g, 1), :], l_ps[:, par, 0:EXPERTS]).then_inc(l_copied, 1)

            def normalise(k, par):
                g = 2 * k + par
                dve.wait_ge(x_in[par], 16 * (k + 1))
                dve.wait_ge(att_in[par], 16 * (k + 1))
                dve.tensor_tensor(t2_sb[:, par, :], x_sb[:, par, :], att_sb[:, par, :, :], ALU.add).then_inc(steps, 1)
                dve.wait_ge(steps, 4 * g + 1)
                dve.bn_stats(stats[:, par, :], t2_sb[:, par, :]).then_inc(steps, 1)
                dve.wait_ge(steps, 4 * g + 2)
                dve.memset(junk[:, :], 0.0)
                dve.bn_aggr(mean_var[:, par, :], stats[:, par, :]).then_inc(steps, 1)
                dve.wait_ge(std_ready, g + 1)
                dve.reciprocal(rstd[:, par, :], std[:, par, :]).then_inc(steps, 1)
                dve.wait_ge(steps, 4 * g + 4)
                dve.wait_ge(uT_copied, g + 1)
                dve.tensor_scalar(u_sb[:, par, :], t2_sb[:, par, :], mean_var[:, par, 0:1], rstd[:, par, :],
                                  ALU.subtract, ALU.mult).then_inc(u_ready, 1)
                dve.wait_ge(u_ready, 2 + g + 1)
                dve.wait_ge(out_free, g + 1)
                dve.tensor_tensor(base_sb[:, par, :], t2_sb[:, par, :], u_sb[:, par, :], ALU.add).then_inc(base_ready, 1)

            with dve.Fori(0, MT // 2) as k:
                normalise(k, 0)
                normalise(k, 1)
                take_logits(k, 0)
                take_logits(k, 1)

            done = [0]

            def step(ins):
                done[0] += 1
                ins.then_inc(choice, 1)
                dve.wait_ge(choice, done[0])

            def per_token(x):
                return x[:, :].unsqueeze(2).broadcast_to([P, MT, EXPERTS])

            dve.wait_ge(l_copied, 2 + MT)
            step(dve.tensor_reduce(row[:, :], logits[:, :, :], AX.X, ALU.max))
            step(dve.tensor_tensor(logits[:, :, :], logits[:, :, :], per_token(row), ALU.subtract))
            dve.wait_ge(exp_done, 1)
            step(dve.tensor_reduce(row[:, :], probs[:, :, :], AX.X, ALU.add))
            step(dve.reciprocal(row[:, :], row[:, :]))
            step(dve.tensor_tensor(probs[:, :, :], probs[:, :, :], per_token(row), ALU.mult))
            for j in range(EXPERTS):
                pj = probs[:, :, j:j + 1]
                dst = rank if j == 0 else above
                if j + 1 < EXPERTS:
                    step(dve.tensor_tensor(dst[:, :, j + 1:], pj.broadcast_to([P, MT, EXPERTS - 1 - j]),
                                           probs[:, :, j + 1:], ALU.is_ge))
                step(dve.tensor_tensor(dst[:, :, 0:j + 1], pj.broadcast_to([P, MT, j + 1]),
                                       probs[:, :, 0:j + 1], ALU.is_gt))
                if j:
                    step(dve.tensor_tensor(rank[:, :, :], rank[:, :, :], above[:, :, :], ALU.add))
            step(dve.tensor_scalar(rank[:, :, :], rank[:, :, :], float(TOP), None, ALU.is_lt))
            step(dve.tensor_tensor(probs[:, :, :], probs[:, :, :], rank[:, :, :], ALU.mult))
            step(dve.tensor_reduce(row[:, :], probs[:, :, :], AX.X, ALU.add))
            step(dve.tensor_scalar(row[:, :], row[:, :], 1e-12, None, ALU.max))
            step(dve.reciprocal(row[:, :], row[:, :]))
            dve.tensor_tensor(w_sb[:, :, :], probs[:, :, :], per_token(row), ALU.mult).then_inc(w_ready, 1)


def experts(nc, base, uT, weights, w1, b1, w2, b2, out):
    G = BANK
    TG = G // P
    LOOPS = TOKENS // G // 2
    with ExitStack() as ctx:
        a = Place(nc, ctx, "experts")
        w1_sb = a.sb("w1", [P, EXPERTS, DC, D])
        w2_sb = a.sb("w2", [P, EXPERTS, DC, D])
        b1_sb = a.sb("b1", [P, EXPERTS, DC])
        b2_sb = a.sb("b2", [P, EXPERTS, D])
        u_sb = a.sb("u", [P, 2, DC, G])
        wt_sb = a.sb("wt", [P, 2, TG, EXPERTS])
        acc = a.sb("acc", [P, 2, TG, D])
        h_sb = a.sb("h", [P, 2, DC, G])
        h_ps = a.ps("h_ps", [P, 2, DC, G])
        y_ps = a.ps("y_ps", [P, 2, TG, D])
        w_in = a.sem("w_in")
        u_in = a.pair("u_in")
        wt_in = a.pair("wt_in")
        base_in = a.pair("base_in")
        h_ready = a.sem("h_ready")
        h_done = a.sem("h_done")
        y_ready = a.sem("y_ready")
        b_added = a.sem("b_added")
        y_added = a.sem("y_added")
        acc_free = a.sem("acc_free")
        stored = a.sem("stored")
        CONST = 16 * 4
        block = ctx.enter_context(nc.Block())

        def rows(x, g):
            return x.rearrange("(t p) d -> p t d", p=P)[:, bass.ds(g * TG, TG), :]

        @block.sync
        def _(sp):
            sp.dma_start(w1_sb[:, :, :, :], w1.rearrange("e (c p) f -> p e c f", p=P)).then_inc(w_in, 16)
            sp.dma_start(w2_sb[:, :, :, :], w2.rearrange("e (c p) f -> p e c f", p=P)).then_inc(w_in, 16)
            sp.dma_start(b1_sb[:, :, :], b1).then_inc(w_in, 16)
            sp.dma_start(b2_sb[:, :, :], b2.partition_broadcast(P)).then_inc(w_in, 16)
            with sp.Fori(0, LOOPS) as i:
                for par in range(2):
                    g = 2 * i + par
                    sp.wait_ge(acc_free, g + 1)
                    sp.dma_start(u_sb[:, par, :, :], uT.rearrange("(c p) n -> p c n", p=P)[:, :, bass.ds(g * G, G)]
                                 ).then_inc(u_in[par], 16)
                    sp.dma_start(wt_sb[:, par, :, :], rows(weights, g)).then_inc(wt_in[par], 16)
                    sp.dma_start(acc[:, par, :, :], rows(base, g)).then_inc(base_in[par], 16)

        @block.gpsimd
        def _(pool):
            pool.sem_inc(acc_free, 2)
            with pool.Fori(0, LOOPS) as i:
                for par in range(2):
                    g = 2 * i + par
                    pool.wait_ge(y_added, 2 * TG + EXPERTS * TG * (g + 1))
                    pool.dma_start(rows(out, g), acc[:, par, :, :]).then_inc(stored, 16)
                    pool.wait_ge(stored, 16 * (g + 1))
                    pool.sem_inc(acc_free, 1)

        @block.tensor
        def _(pe):
            pe.sem_inc(h_ready, 2 * DC)
            pe.sem_inc(y_ready, 2)
            pe.wait_ge(w_in, CONST)

            def hidden(g, par, e):
                n = EXPERTS * g + e
                for f in range(DC):
                    pe.wait_ge(h_done, DC * n + f + 1)
                    for c in range(DC):
                        mm = pe.matmul(h_ps[:, e % 2, f, :], w1_sb[:, e, c, f * P:(f + 1) * P],
                                       u_sb[:, par, c, :], start=c == 0, stop=c == DC - 1)
                    mm.then_inc(h_ready, 1)

            def output(g, e):
                n = EXPERTS * g + e
                pe.wait_ge(h_done, 2 * DC + DC * (n + 1))
                pe.wait_ge(y_added, TG * (n + 1))
                for t in range(TG):
                    for f in range(DC):
                        mm = pe.matmul(y_ps[:, e % 2, t, :], h_sb[:, e % 2, f, t * P:(t + 1) * P],
                                       w2_sb[:, e, f, :], start=f == 0, stop=f == DC - 1)
                mm.then_inc(y_ready, 1)

            with pe.Fori(0, LOOPS) as i:
                for par in range(2):
                    g = 2 * i + par
                    pe.wait_ge(u_in[par], 16 * (i + 1))
                    hidden(g, par, 0)
                    for e in range(1, EXPERTS):
                        hidden(g, par, e)
                        output(g, e - 1)
                    output(g, EXPERTS - 1)

        @block.scalar
        def _(act):
            act.sem_inc(h_done, 2 * DC)
            act.wait_ge(w_in, CONST)
            with act.Fori(0, LOOPS) as i:
                for par in range(2):
                    for e in range(EXPERTS):
                        n = EXPERTS * (2 * i + par) + e
                        act.wait_ge(y_ready, n + 1)
                        for f in range(DC):
                            act.wait_ge(h_ready, 2 * DC + DC * n + f + 1)
                            act.activation(h_sb[:, e % 2, f, :], h_ps[:, e % 2, f, :], ACT.Gelu,
                                           bias=b1_sb[:, e, f:f + 1]).then_inc(h_done, 1)

        @block.vector
        def _(dve):
            dve.sem_inc(y_added, 2 * TG)
            dve.wait_ge(w_in, CONST)
            with dve.Fori(0, LOOPS) as i:
                for par in range(2):
                    dve.wait_ge(wt_in[par], 16 * (i + 1))
                    dve.wait_ge(base_in[par], 16 * (i + 1))
                    for e in range(EXPERTS):
                        n = EXPERTS * (2 * i + par) + e
                        for t in range(TG):
                            if e:
                                dve.wait_ge(y_added, 2 * TG + TG * (n - 1) + t + 1)
                            dve.scalar_tensor_tensor(acc[:, par, t, :], b2_sb[:, e, :], wt_sb[:, par, t, e:e + 1],
                                                     acc[:, par, t, :], ALU.mult, ALU.add).then_inc(b_added, 1)
                        dve.wait_ge(y_ready, 2 + n + 1)
                        for t in range(TG):
                            dve.wait_ge(b_added, TG * n + t + 1)
                            dve.scalar_tensor_tensor(acc[:, par, t, :], y_ps[:, e % 2, t, :],
                                                     wt_sb[:, par, t, e:e + 1], acc[:, par, t, :],
                                                     ALU.mult, ALU.add).then_inc(y_added, 1)


def build(nc, t, out):
    def scratch(name, shape):
        return nc.dram_tensor(name, list(shape), F32, kind="Internal").ap()

    identity = t["identity"]
    q0T, k0T, v0 = scratch("q0T", (C0, TOKENS)), scratch("k0T", (C0, TOKENS)), scratch("v0", (TOKENS, D))
    t1 = scratch("t1", (TOKENS, D))
    qkT = scratch("qkT", (EA, BLOCKS * TOKENS))
    ks, v = scratch("ks", (TOKENS, KS)), scratch("v", (H * TOKENS, E))
    dist = scratch("dist", (TOKENS, N))
    attended = scratch("attended", (H * TOKENS, E))
    base, uT, weights = scratch("base", (TOKENS, D)), scratch("uT", (D, TOKENS)), scratch("weights", (TOKENS, EXPERTS))

    project0(nc, t["xT"], t["wqk0"], t["bqk0"], t["wv0"], t["bv0"], q0T, k0T, v0)
    attend(nc, "attend0", B, D, q0T, 0, k0T, 0, v0, "dot", "residual", gamma=t["gamma"], x=t["x"],
           out=t1, identity=identity)
    project1(nc, t1, t["wqkv"], t["bqkv"], t["share"], identity, qkT, ks, v)
    distances(nc, qkT, ks, identity, dist)

    def rows(x, head, heads):
        return x[head * TOKENS:(head + heads) * TOKENS, :]

    attend(nc, "products", 2 * B, E, qkT, Q_BLOCK[SDP] * TOKENS, qkT, K_BLOCK[SDP] * TOKENS, rows(v, SDP, 2),
           "dot", "plain", out=rows(attended, SDP, 2), identity=identity)
    attend(nc, "l1", B, E, None, 0, None, 0, rows(v, L1, 1), "l1", "plain", scores=dist,
           out=rows(attended, L1, 1), identity=identity)
    attend(nc, "l2", B, E, qkT, Q_BLOCK[L2] * TOKENS, qkT, K_BLOCK[L2] * TOKENS, rows(v, L2, 1),
           "l2", "plain", out=rows(attended, L2, 1), identity=identity)
    route(nc, t1, attended, t["routerT"], identity, base, uT, weights)
    experts(nc, base, uT, weights, t["w1"], t["b1"], t["w2"], t["b2"], out)


def lay_out(inputs):
    import numpy as np

    def heads(w):
        return w.transpose(1, 0, 2).reshape(D, H * E)

    i = {name: np.asarray(x) for name, x in inputs.items()}
    x = i["x"].reshape(TOKENS, D)
    arrays = {
        "x": x, "xT": x.T, "identity": np.eye(P, dtype=np.float32),
        "wqk0": np.concatenate([i["L0_conv_Wq"], i["L0_conv_Wk"]]).T,
        "bqk0": np.stack([i["L0_conv_bq"], i["L0_conv_bk"]], axis=1),
        "wv0": i["L0_conv_Wv"].T, "bv0": i["L0_conv_bv"], "gamma": i["L0_conv_gamma"],
        "wqkv": np.concatenate([heads(i[f"L1_attn_W{c}"]) for c in "qkv"], axis=1),
        "bqkv": np.concatenate([i[f"L1_attn_b{c}"].reshape(-1) for c in "qkv"]),
        "share": np.array(ON_VECTOR, np.float32),
        "routerT": i["L1_ffn_router_w"].T,
        "w1": i["L1_ffn_w1"], "b1": i["L1_ffn_b1"].reshape(EXPERTS, DC, P).transpose(2, 0, 1),
        "w2": i["L1_ffn_w2"], "b2": i["L1_ffn_b2"],
    }
    return {name: np.ascontiguousarray(x) for name, x in arrays.items()}


def kernel(**inputs):
    import concourse.bacc as bacc
    from concourse.bass_utils import run_bass_kernel_spmd

    nc = bacc.Bacc("TRN2", target_bir_lowering=False, num_devices=1)
    arrays = lay_out(inputs)
    tensors = {name: nc.dram_tensor(name, x.shape, mybir.dt.from_np(x.dtype), kind="ExternalInput").ap()
               for name, x in arrays.items()}
    out = nc.dram_tensor("out", (TOKENS, D), F32, kind="ExternalOutput").ap()
    build(nc, tensors, out)
    result = run_bass_kernel_spmd(nc, [arrays], core_ids=[0])
    return result.results[0]["out"].reshape(inputs["x"].shape)
```

```python
from contextlib import ExitStack

import concourse.bass as bass
from concourse import mybir

P = 128
F32 = mybir.dt.float32
F32R = mybir.dt.float32r
ALU = mybir.AluOpType
ACT = mybir.ActivationFunctionType
AX = mybir.AxisListType

B, N, D = 2, 4096, 256
TOKENS = B * N
C0 = D // 8
H, E = 4, 64
DC = D // P
TILES = N // P
PAIRS = TILES // 2
SDP, COS, L1, L2 = range(H)
PRODUCT_HEADS = [SDP, COS, L2]
PH = len(PRODUCT_HEADS)
KS = 2 * E + 4
NORM_AT = 2 * E + 1
EXPERTS, TOP = 8, 2
LN_EPS = 1e-5
BANK = 512


def spread(count, among):
    n = len(among)
    return [x for i, x in enumerate(among) if (i * count) // n != ((i + 1) * count) // n]


def merged(*queues):
    return [(q, n) for _, q, n in sorted(((n + 0.5) / length, q, n)
                                         for q, length in enumerate(queues) for n in range(length))]


ON_SCALAR, ON_MAX = 31, 12
SCALAR_E = spread(ON_SCALAR, range(E))
VECTOR_E = [e for e in range(E) if e not in SCALAR_E]
MAX_E = spread(ON_MAX, VECTOR_E)
SUM_E = [e for e in VECTOR_E if e not in MAX_E]


class Place:

    def __init__(self, nc, ctx, stage):
        self.nc, self.ctx, self.stage = nc, ctx, stage

    def sb(self, name, shape, dtype=F32):
        return self.ctx.enter_context(self.nc.sbuf_tensor(f"{self.stage}_{name}", shape, dtype))

    def ps(self, name, shape):
        return self.ctx.enter_context(self.nc.psum_tensor(f"{self.stage}_{name}", shape, F32))

    def sem(self, name):
        return self.ctx.enter_context(self.nc.semaphore(f"{self.stage}_{name}"))

    def pair(self, name):
        return [self.sem(f"{name}{par}") for par in range(2)]


def project0(nc, xT, wqk, bqk, signs, wv, bv, identity, ident, qT, kT, v):
    G = BANK
    TG = G // P
    LOOPS = TOKENS // G // 2
    with ExitStack() as ctx:
        a = Place(nc, ctx, "project0")
        x_sb = a.sb("x", [P, 2, DC, G])
        wqk_sb = a.sb("wqk", [P, DC, 2 * P])
        wv_sb = a.sb("wv", [P, DC, D])
        bqk_sb = a.sb("bqk", [P, 4])
        signs_sb = a.sb("signs", [P, 4])
        bv_sb = a.sb("bv", [P, TG, D])
        high = a.sb("high", [P, 2, 2, G], F32R)
        full = a.sb("full", [P, 2, 2, G])
        q_sb = a.sb("q", [P, 2, G], F32R)
        k_sb = a.sb("k", [P, 2, G], F32R)
        v_sb = a.sb("v", [P, 2, TG, D])
        q_ps = a.ps("q_ps", [P, 2, G])
        k_ps = a.ps("k_ps", [P, 2, G])
        v_ps = a.ps("v_ps", [P, 2, TG, D])
        weights_in = a.sem("weights_in")
        x_in = a.pair("x_in")
        qk_ready = a.sem("qk_ready")
        v_ready = a.sem("v_ready")
        qk_copied = a.sem("qk_copied")
        qk_out = a.sem("qk_out")
        v_out = a.sem("v_out")
        stored = a.sem("stored")
        out_free = a.sem("out_free")
        WEIGHTS = 16 * (5 + TG)
        x_cols = xT.rearrange("(c p) n -> p c n", p=P)
        v_rows = v.rearrange("(t p) d -> p t d", p=P)
        block = ctx.enter_context(nc.Block())

        @block.sync
        def _(sp):
            sp.dma_start(wqk_sb[:, :, :], wqk.rearrange("(c p) m -> p c m", p=P)).then_inc(weights_in, 16)
            sp.dma_start(wv_sb[:, :, :], wv.rearrange("(c p) m -> p c m", p=P)).then_inc(weights_in, 16)
            sp.dma_start(bqk_sb[:, :], bqk).then_inc(weights_in, 16)
            sp.dma_start(signs_sb[:, :], signs).then_inc(weights_in, 16)
            sp.dma_start(ident[:, :], identity).then_inc(weights_in, 16)
            for t in range(TG):
                sp.dma_start(bv_sb[:, t, :], bv.partition_broadcast(P)).then_inc(weights_in, 16)
            with sp.Fori(0, LOOPS) as i:
                for par in range(2):
                    g = 2 * i + par
                    sp.wait_ge(v_out, g + 1)
                    sp.dma_start(x_sb[:, par, :, :], x_cols[:, :, bass.ds(g * G, G)]).then_inc(x_in[par], 16)

        @block.gpsimd
        def _(pool):
            pool.sem_inc(out_free, 2)
            with pool.Fori(0, LOOPS) as i:
                for par in range(2):
                    g = 2 * i + par
                    pool.wait_ge(qk_out, 2 + g + 1)
                    pool.dma_start(qT[:, bass.ds(g * G, G)], q_sb.bitcast(F32)[:, par, :]).then_inc(stored, 16)
                    pool.dma_start(kT[:, bass.ds(g * G, G)], k_sb.bitcast(F32)[:, par, :]).then_inc(stored, 16)
                    pool.wait_ge(v_out, 2 + g + 1)
                    pool.dma_start(v_rows[:, bass.ds(g * TG, TG), :], v_sb[:, par, :, :]).then_inc(stored, 16)
                    pool.wait_ge(stored, 48 * (g + 1))
                    pool.sem_inc(out_free, 1)

        @block.tensor
        def _(pe):
            pe.sem_inc(qk_ready, 2)
            pe.wait_ge(weights_in, WEIGHTS)
            with pe.Fori(0, LOOPS) as i:
                for par in range(2):
                    g = 2 * i + par
                    pe.wait_ge(x_in[par], 16 * (i + 1))
                    pe.wait_ge(qk_copied, g + 1)
                    for which, ps in ((0, q_ps), (1, k_ps)):
                        for c in range(DC):
                            mm = pe.matmul(ps[:, par, :], wqk_sb[:, c, which * P:(which + 1) * P],
                                           x_sb[:, par, c, :], start=c == 0, stop=c == DC - 1)
                    mm.then_inc(qk_ready, 1)
                    pe.wait_ge(v_out, g + 1)
                    for t in range(TG):
                        for c in range(DC):
                            mm = pe.matmul(v_ps[:, par, t, :], x_sb[:, par, c, t * P:(t + 1) * P],
                                           wv_sb[:, c, :], start=c == 0, stop=c == DC - 1)
                    mm.then_inc(v_ready, 1)

        @block.scalar
        def _(act):
            act.sem_inc(qk_copied, 2)
            act.wait_ge(weights_in, WEIGHTS)
            with act.Fori(0, LOOPS) as i:
                for par in range(2):
                    g = 2 * i + par
                    act.wait_ge(qk_ready, 2 + g + 1)
                    act.wait_ge(qk_out, g + 1)
                    for which, ps in ((0, q_ps), (1, k_ps)):
                        act.activation(high[:, par, which, :], ps[:, par, :], ACT.Identity,
                                       bias=bqk_sb[:, 2 * which:2 * which + 1])
                        ins = act.activation(full[:, par, which, :], ps[:, par, :], ACT.Identity,
                                             bias=bqk_sb[:, 2 * which + 1:2 * which + 2],
                                             scale=signs_sb[:, 2 * which + 1:2 * which + 2])
                    ins.then_inc(qk_copied, 1)

        @block.vector
        def _(dve):
            dve.sem_inc(v_out, 2)
            dve.sem_inc(qk_out, 2)
            dve.wait_ge(weights_in, WEIGHTS)
            with dve.Fori(0, LOOPS) as i:
                for par in range(2):
                    g = 2 * i + par
                    dve.wait_ge(out_free, g + 1)
                    dve.wait_ge(qk_copied, 2 + g + 1)
                    for which, sb in ((0, q_sb), (1, k_sb)):
                        ins = dve.scalar_tensor_tensor(sb[:, par, :], high.bitcast(F32)[:, par, which, :],
                                                       signs_sb[:, 2 * which:2 * which + 1],
                                                       full[:, par, which, :], ALU.mult, ALU.add)
                    ins.then_inc(qk_out, 1)
                    dve.wait_ge(v_ready, g + 1)
                    dve.tensor_tensor(v_sb[:, par, :, :], v_ps[:, par, :, :], bv_sb[:, :, :],
                                      ALU.add).then_inc(v_out, 1)


def attend(nc, stage, heads, width, qT, kT, v, kind, finish, ident, out, scores=None, norms=None,
           norm_rows=None, gamma=None, x=None):
    R = 4
    LAG = 2
    GROUPS = TILES // R
    W = 1024
    SC = N // W
    TC = N // BANK
    KT = BANK // P
    TB = 4
    BY_SCALAR = (1, 4, 7)
    dot, l2, l1 = kind == "dot", kind == "l2", kind == "l1"
    with ExitStack() as ctx:
        a = Place(nc, ctx, stage)
        s_sb = a.sb("s", [P, R, N])
        t_sb = a.sb("t", [P, TB, BANK])
        v_sb = a.sb("v", [P, TILES, width])
        part = a.sb("part", [P, R, SC])
        shift = a.sb("shift", [P, R, 1])
        sums = a.sb("sums", [P, R, SC])
        total = a.sb("total", [P, R, 1])
        recip = a.sb("recip", [P, R, 1])
        o_sb = a.sb("o", [P, 2, width])
        if finish == "residual":
            scale = a.sb("scale", [P, R, 1])
            gam = a.sb("gam", [P, 1])
            x_sb = a.sb("x", [P, R, width])
        if not l1:
            k_sb = [a.sb(f"k{n}", [P, N], F32R) for n in range(len(kT))]
            q_sb = a.sb("q", [P, R, P], F32R)
            s_ps = a.ps("s_ps", [P, 2, W])
        if l2:
            ones = a.sb("ones", [2, P], F32R)
            kn_sb = a.sb("kn", [2, N], F32R)
            qn_sb = a.sb("qn", [P, R, 2])
            root = a.sb("root", [P, R, 1])
        t_ps = a.ps("t_ps", [P, 2, BANK])
        o_ps = a.ps("o_ps", [P, 2, BANK])
        if finish == "residual":
            const_in = a.sem("const_in")
        v_in = a.sem("v_in")
        kv_free = a.sem("kv_free")
        q_in = [a.sem(f"q_in{r}") for r in range(R)]
        if not l1:
            k_in = a.sem("k_in")
            s_ready = a.sem("s_ready")
            s_copied = a.sem("s_copied")
        else:
            e_ready = a.sem("e_ready")
        m_ready = a.sem("m_ready")
        if l2:
            r_ready = a.sem("r_ready")
            ones_ready = a.sem("ones_ready")
        p_ready = a.sem("p_ready")
        t_ready = a.sem("t_ready")
        by_vector = a.sem("by_vector")
        by_scalar = a.sem("by_scalar")
        pv_done = a.sem("pv_done")
        rc_ready = a.sem("rc_ready")
        o_done = a.sem("o_done")
        stored = a.sem("stored")
        o_free = a.sem("o_free")
        TILE_IN = 16 * (2 if l2 or finish == "residual" else 1)
        HEAD_IN = 16 * (len(kT) + (1 if l2 else 0)) if not l1 else 0
        block = ctx.enter_context(nc.Block())

        def copied(g, c):
            by_scalar_here = c in BY_SCALAR
            mine = [x for x in range(TC) if (x in BY_SCALAR) == by_scalar_here]
            return (by_scalar if by_scalar_here else by_vector), len(mine) * g + mine.index(c) + 1

        def tiles(eng, body, behind=None):
            def step(u, k, n, first, end):
                new, mid, old = ((k + m // R, m % R) if first <= m < end else None
                                 for m in (n, n - 1, n - LAG))
                body(u, new, mid, old)

            with eng.Fori(0, heads) as u:
                k0 = u * GROUPS
                for n in range(LAG):
                    step(u, k0, n, 0, R)
                with eng.Fori(0, GROUPS - 1) as j:
                    for n in range(LAG, R + LAG):
                        step(u, k0 + j, n, 0, R + LAG)
                k = k0 + GROUPS - 1
                for n in range(LAG, R + LAG):
                    step(u, k, n, 0, R)
                if behind:
                    behind(k)

        @block.sync
        def _(sp):
            if finish == "residual":
                sp.dma_start(gam[:, :], gamma.partition_broadcast(P)).then_inc(const_in, 16)
            with sp.Fori(0, heads) as u:
                sp.wait_ge(kv_free, u + 1)
                if not l1:
                    for sb, dram in zip(k_sb, kT):
                        sp.dma_start(sb.bitcast(F32)[:, :], dram[:, bass.ds(u * N, N)]).then_inc(k_in, 16)
                if l2:
                    sp.dma_start(kn_sb.bitcast(F32)[:, :], norm_rows[:, bass.ds(u * N, N)]).then_inc(k_in, 16)
                for half in range(2):
                    sp.dma_start(v_sb[:, half * TILES // 2:(half + 1) * TILES // 2, :],
                                 v.rearrange("(t p) d -> p t d", p=P)[
                                     :, bass.ds(u * TILES + half * TILES // 2, TILES // 2), :]).then_inc(v_in, 16)
                with sp.Fori(0, GROUPS) as j:
                    for r in range(R):
                        k = u * GROUPS + j
                        g = R * k + r
                        rows = bass.ds(g * P, P)
                        if l1:
                            sp.wait_ge(t_ready, TC * (g + 1))
                            sp.dma_start(s_sb[:, r, :], scores[rows, :]).then_inc(q_in[r], 16)
                        else:
                            if l2:
                                sp.wait_ge(t_ready, TC * (g + 1))
                            else:
                                sp.wait_ge(s_ready, SC * (g + 1))
                            if l2:
                                sp.dma_start(qn_sb[:, r, :], norms[rows, :]).then_inc(q_in[r], 16)
                            sp.dma_start(q_sb.bitcast(F32)[:, r, :], qT[:, rows]).then_inc(q_in[r], 16)
                        if finish == "residual":
                            sp.wait_ge(o_done, g + 1)
                            sp.dma_start(x_sb[:, r, :], x[rows, :]).then_inc(q_in[r], 16)

        @block.gpsimd
        def _(pool):
            pool.sem_inc(o_free, 2)
            with pool.Fori(0, heads * TILES // 2) as k:
                for par in range(2):
                    pool.wait_ge(o_done, R + 2 * k + par + 1)
                    pool.dma_start(out[bass.ds((2 * k + par) * P, P), :], o_sb[:, par, :]).then_inc(stored, 16)
                    pool.wait_ge(stored, 16 * (2 * k + par + 1))
                    pool.sem_inc(o_free, 1)

        @block.tensor
        def _(pe):
            if not l1:
                pe.sem_inc(s_ready, R * SC)
            pe.sem_inc(t_ready, R * TC)
            pe.sem_inc(pv_done, TB)
            pe.sem_inc(kv_free, 1)
            if l2:
                pe.wait_ge(ones_ready, 1)

            def body(u, new, mid, old):
                def make_scores(c):
                    if not new or l1:
                        return
                    k, r = new
                    if c == 0:
                        pe.wait_ge(k_in, HEAD_IN * (u + 1))
                        pe.wait_ge(q_in[r], TILE_IN * (k + 1))
                    pe.wait_ge(s_copied, SC * (R * k + r) + c + 1)
                    for w in range(0, W, BANK):
                        at = slice(c * W + w, c * W + w + BANK)
                        for n, sb in enumerate(k_sb):
                            mm = pe.matmul(s_ps[:, c % 2, w:w + BANK], q_sb[:, r, :], sb[:, at],
                                           start=n == 0, stop=not l2 and n == len(k_sb) - 1)
                        if l2:
                            mm = pe.matmul(s_ps[:, c % 2, w:w + BANK], ones[:, :], kn_sb[:, at],
                                           start=False, stop=True)
                    mm.then_inc(s_ready, 1)

                def turn(c):
                    k, r = old
                    pe.wait_ge(*copied(R * k + r + (c >= 2), (c - 2) % TC))
                    if c % 2 == 0:
                        pe.wait_ge(p_ready, SC * (R * k + r) + c // 2 + 1)
                    for j in range(KT):
                        at = c * BANK + j * P
                        mm = pe.transpose(t_ps[:, c % 2, j * P:(j + 1) * P], s_sb[:, r, at:at + P], ident[:, :])
                    mm.then_inc(t_ready, 1)

                def times_v(c):
                    k, r = old
                    pe.wait_ge(*copied(R * k + r + 1, c))
                    for j in range(KT):
                        mm = pe.matmul(o_ps[:, r % 2, 0:width], t_sb[:, c % TB, j * P:(j + 1) * P],
                                       v_sb[:, c * KT + j, :], start=(c == 0 and j == 0),
                                       stop=(c == TC - 1 and j == KT - 1))
                    mm.then_inc(pv_done, 1)

                make_scores(0)
                if old:
                    k, r = old
                    pe.wait_ge(v_in, 32 * (u + 1))
                    pe.wait_ge(o_done, R * k + r + R - 1)
                for c in range(TC):
                    if c in (2, 4):
                        make_scores(c // 2)
                    if old:
                        turn(c)
                        if c >= 2:
                            times_v(c - 2)
                make_scores(SC - 1)
                if old:
                    times_v(TC - 2)
                    times_v(TC - 1)

            def behind(k):
                pe.wait_ge(pv_done, TB + TC * R * (k + 1))
                pe.sem_inc(kv_free, 1)

            tiles(pe, body, behind)

        @block.vector
        def _(dve):
            if not l1:
                dve.sem_inc(s_copied, 2)
            dve.sem_inc(by_vector, TC - len(BY_SCALAR))
            dve.sem_inc(o_done, R)
            if l2:
                dve.memset(root[:, :, :], 1.0).then_inc(rc_ready, 1)
                dve.wait_ge(rc_ready, 1)
                dve.tensor_copy(ones[:, :], root[0:2, 0, 0:1].broadcast_to([2, P])).then_inc(ones_ready, 1)
            if finish == "residual":
                dve.wait_ge(const_in, 16)
            RC = 1 if l2 else 0
            RC_STEPS = 3 if finish == "residual" else 2

            def body(u, new, mid, old):
                def take_scores(c):
                    if not new:
                        return
                    k, r = new
                    g = R * k + r
                    at = slice(c * W, (c + 1) * W)
                    if c == 0:
                        dve.wait_ge(t_ready, TC * (g + 1))
                        if l1 or l2:
                            dve.wait_ge(q_in[r], TILE_IN * (k + 1))
                    if l1:
                        dve.tensor_reduce(part[:, r, c:c + 1], s_sb[:, r, at], AX.X, ALU.min).then_inc(e_ready, 1)
                        return
                    dve.wait_ge(s_ready, R * SC + SC * g + c + 1)
                    dve.tensor_scalar(s_sb[:, r, at], s_ps[:, c % 2, :], qn_sb[:, r, 1:2] if l2 else 0.0, None,
                                      ALU.max if l2 else ALU.add, ALU.min if l2 else ALU.max,
                                      accum_out=part[:, r, c:c + 1]).then_inc(s_copied, 1)

                def extreme():
                    if not new:
                        return
                    k, r = new
                    g = R * k + r
                    if l1:
                        dve.wait_ge(e_ready, SC * (g + 1))
                    else:
                        dve.wait_ge(s_copied, 2 + SC * (g + 1))
                    dve.tensor_reduce(shift[:, r, :], part[:, r, :], AX.X, ALU.max if dot else ALU.min,
                                      negate=dot).then_inc(m_ready, 1)

                def take_turned(c):
                    k, r = old
                    i = TC * (R * k + r) + c
                    dve.wait_ge(t_ready, R * TC + i + 1)
                    dve.wait_ge(pv_done, i + 1)
                    dve.tensor_copy(t_sb[:, c % TB, :], t_ps[:, c % 2, :]).then_inc(by_vector, 1)

                def finish_tile():
                    k, r = old
                    g = R * k + r
                    n = RC + RC_STEPS * g
                    dve.wait_ge(p_ready, SC * (g + 1))
                    dve.tensor_reduce(total[:, r, :], sums[:, r, :], AX.X, ALU.add).then_inc(rc_ready, 1)
                    dve.wait_ge(rc_ready, n + 1)
                    dve.reciprocal(recip[:, r, :], total[:, r, :]).then_inc(rc_ready, 1)
                    dve.wait_ge(rc_ready, n + 2)
                    dve.wait_ge(o_free, g + 1)
                    if finish == "residual":
                        dve.tensor_tensor(scale[:, r, :], recip[:, r, :], gam[:, :], ALU.mult).then_inc(rc_ready, 1)
                        dve.wait_ge(rc_ready, n + 3)
                        dve.wait_ge(q_in[r], TILE_IN * (k + 1))
                        dve.wait_ge(pv_done, TB + TC * (g + 1))
                        dve.scalar_tensor_tensor(o_sb[:, r % 2, :], o_ps[:, r % 2, 0:width], scale[:, r, :],
                                                 x_sb[:, r, :], ALU.mult, ALU.add).then_inc(o_done, 1)
                    else:
                        dve.wait_ge(pv_done, TB + TC * (g + 1))
                        dve.tensor_scalar(o_sb[:, r % 2, :], o_ps[:, r % 2, 0:width], recip[:, r, :], None,
                                          ALU.mult).then_inc(o_done, 1)

                take_scores(0)
                for c in range(TC):
                    if c in (2, 4):
                        take_scores(c // 2)
                    if old and c not in BY_SCALAR:
                        take_turned(c)
                take_scores(SC - 1)
                extreme()
                if old:
                    finish_tile()

            tiles(dve, body)

        @block.scalar
        def _(act):
            act.sem_inc(by_scalar, len(BY_SCALAR))

            def body(u, new, mid, old):
                def piece(c):
                    return slice(c * W, (c + 1) * W)

                def take_turned(c):
                    k, r = old
                    i = TC * (R * k + r) + c
                    act.wait_ge(t_ready, R * TC + i + 1)
                    act.wait_ge(pv_done, i + 1)
                    act.copy(t_sb[:, c % TB, :], t_ps[:, c % 2, :]).then_inc(by_scalar, 1)

                def exponentiate(c):
                    k, r = mid
                    act.activation(s_sb[:, r, piece(c)], s_sb[:, r, piece(c)], ACT.Exp,
                                   bias=(root if l2 else shift)[:, r, :], scale=1.0 if dot else -1.0,
                                   accum_out=sums[:, r, c:c + 1]).then_inc(p_ready, 1)

                if mid:
                    k, r = mid
                    g = R * k + r
                    act.wait_ge(m_ready, g + 1)
                    act.wait_ge(o_done, g + 1)
                    if l2:
                        act.activation(root[:, r, :], shift[:, r, :], ACT.Sqrt,
                                       bias=qn_sb[:, r, 0:1]).then_inc(r_ready, 1)
                for c in range(TC):
                    if mid and l2:
                        if c < SC:
                            act.activation(s_sb[:, r, piece(c)], s_sb[:, r, piece(c)], ACT.Sqrt,
                                           bias=qn_sb[:, r, 0:1]).then_inc(r_ready, 1)
                        else:
                            act.wait_ge(r_ready, (SC + 1) * g + c - SC + 2)
                            exponentiate(c - SC)
                    elif mid and c % 2 == 0:
                        exponentiate(c // 2)
                    if old and c in BY_SCALAR:
                        take_turned(c)

            tiles(act, body)


def project1(nc, t1, wqkv, bqkv, share, ident, parts, rows2, ks, v):
    HE = H * E
    MT = TOKENS // P
    PAIRS1 = MT // 2
    with ExitStack() as ctx:
        a = Place(nc, ctx, "project1")
        w_sb = a.sb("w", [P, DC, 3 * HE])
        b_sb = a.sb("b", [P, 3 * HE])
        share_sb = a.sb("share", [P, E])
        eps = a.sb("eps", [P, 1])
        x_sb = a.sb("x", [P, 2, D])
        stats = a.sb("stats", [P, 2, 6])
        mean_var = a.sb("mean_var", [P, 2, 2])
        std = a.sb("std", [P, 2, 1])
        rstd = a.sb("rstd", [P, 2, 1])
        n_sb = a.sb("n", [P, 2, D])
        nT_sb = a.sb("nT", [P, 2, DC, P])
        raw = a.sb("raw", [P, 2, 2, H, E])
        square = a.sb("square", [P, 2, 2, 2, E])
        norm2 = a.sb("norm2", [P, 2, 4])
        norm = a.sb("norm", [P, 2, 4])
        rnorm = a.sb("rnorm", [P, 2, 4])
        forms = a.sb("forms", [P, 2, 2, PH, E])
        split = a.sb("split", [P, 2, 3 * PH, 2, E], F32R)
        last = a.sb("last", [P, 2, E + 2])
        junk = a.sb("junk", [P, 2, E])
        ks_sb = a.sb("ks", [P, 2, KS])
        v_sb = a.sb("v", [P, 2, H, E])
        sT_sb = a.sb("sT", [P, 2, 3 * PH, P], F32R)
        lT_sb = a.sb("lT", [E + 2, 2, P])
        nT_ps = a.ps("nT_ps", [P, 2, D])
        p_ps = a.ps("p_ps", [P, 2, 2 * BANK])
        sT_ps = a.ps("sT_ps", [P, 3 * BANK])
        LAST = 3 * PH * P
        const_in = a.sem("const_in")
        preset = a.sem("preset")
        x_in = a.pair("x_in")
        stats_ready = a.sem("stats_ready")
        mean_ready = a.sem("mean_ready")
        std_ready = a.sem("std_ready")
        rstd_ready = a.sem("rstd_ready")
        n_ready = a.sem("n_ready")
        nT_ready = a.sem("nT_ready")
        nT_copied = a.sem("nT_copied")
        p_ready = a.sem("p_ready")
        raw_ready = a.sem("raw_ready")
        norm2_ready = a.sem("norm2_ready")
        norm_ready = a.sem("norm_ready")
        rnorm_ready = a.sem("rnorm_ready")
        forms_ready = a.sem("forms_ready")
        high_ready = a.sem("high_ready")
        split_ready = a.sem("split_ready")
        sT_ready = a.sem("sT_ready")
        sT_copied = a.sem("sT_copied")
        stored = a.sem("stored")
        v_free = a.sem("v_free")
        ks_free = a.sem("ks_free")
        CONST = 16 * 3
        part_blocks = parts.rearrange("e (k n) -> e k n", k=3 * PH)
        v_rows = v.rearrange("(h n) e -> n h e", h=H)
        Q, K = 0, 1
        block = ctx.enter_context(nc.Block())

        def pipelined(eng, early, late):
            early(0)
            with eng.Fori(0, PAIRS1 - 1) as k:
                early(k + 1)
                late(k)
            late(PAIRS1 - 1)

        @block.sync
        def _(sp):
            sp.dma_start(w_sb[:, :, :], wqkv.rearrange("(c p) m -> p c m", p=P)).then_inc(const_in, 16)
            sp.dma_start(b_sb[:, :], bqkv.partition_broadcast(P)).then_inc(const_in, 16)
            sp.dma_start(share_sb[:, :], share.partition_broadcast(P)).then_inc(const_in, 16)
            with sp.Fori(0, PAIRS1) as k:
                for par in range(2):
                    g = 2 * k + par
                    sp.wait_ge(n_ready, g + 1)
                    sp.dma_start(x_sb[:, par, :], t1[bass.ds(g * P, P), :]).then_inc(x_in[par], 16)

        @block.gpsimd
        def _(pool):
            pool.sem_inc(v_free, 1)
            pool.sem_inc(ks_free, 1)
            with pool.Fori(0, PAIRS1) as k:
                def tile(par):
                    return bass.ds((2 * k + par) * P, P)

                for par in range(2):
                    pool.wait_ge(raw_ready, 2 + 2 * k + par + 1)
                    pool.dma_start(v_rows[tile(par), :, :], v_sb[:, par, :, :]).then_inc(stored, 16)
                pool.wait_ge(stored, 16 * 8 * k + 16 * 2)
                pool.sem_inc(v_free, 1)
                for par in range(2):
                    pool.wait_ge(split_ready, 2 + 2 * k + par + 1)
                    pool.dma_start(ks[tile(par), :], ks_sb[:, par, :]).then_inc(stored, 16)
                pool.wait_ge(stored, 16 * 8 * k + 16 * 4)
                pool.sem_inc(ks_free, 1)
                for par in range(2):
                    pool.wait_ge(sT_copied, 1 + 2 * k + par + 1)
                    pool.dma_start(part_blocks[:, :, tile(par)], sT_sb.bitcast(F32)[:, par, :, :]).then_inc(stored, 16)
                    pool.dma_start(rows2[:, tile(par)], lT_sb[:, par, :]).then_inc(stored, 16)
            pool.wait_ge(stored, 16 * 8 * PAIRS1)

        @block.tensor
        def _(pe):
            pe.sem_inc(sT_ready, 2)
            pe.sem_inc(p_ready, 2)
            pe.wait_ge(const_in, CONST)

            def project(k):
                for par in range(2):
                    g = 2 * k + par
                    pe.wait_ge(n_ready, 2 + g + 1)
                    if par == 0:
                        pe.wait_ge(nT_copied, k + 1)
                    for c in range(DC):
                        mm = pe.transpose(nT_ps[:, par, c * P:(c + 1) * P], n_sb[:, par, c * P:(c + 1) * P],
                                          ident[:, :])
                mm.then_inc(nT_ready, 1)
                for par in range(2):
                    g = 2 * k + par
                    if par == 0:
                        pe.wait_ge(nT_copied, 1 + k + 1)
                    pe.wait_ge(raw_ready, g + 1)
                    for at, n in ((0, BANK), (BANK, 3 * HE - BANK)):
                        for c in range(DC):
                            mm = pe.matmul(p_ps[:, par, at:at + n], nT_sb[:, par, c, :], w_sb[:, c, at:at + n],
                                           start=c == 0, stop=c == DC - 1)
                    mm.then_inc(p_ready, 1)

            def turn(k):
                for par in range(2):
                    g = 2 * k + par
                    pe.wait_ge(split_ready, 2 + g + 1)
                    pe.wait_ge(sT_copied, g + 1)
                    for m in range(3 * PH):
                        pe.transpose(sT_ps[:, m * P:(m + 1) * P], split.bitcast(F32)[:, par, m, :, :], ident[:, :])
                    pe.transpose(sT_ps[0:E + 2, LAST:LAST + P], last[:, par, :], ident[:, :]).then_inc(sT_ready, 1)

            pipelined(pe, project, turn)

        @block.scalar
        def _(act):
            act.sem_inc(nT_copied, 1)
            act.sem_inc(sT_copied, 1)
            act.wait_ge(preset, 1)

            def early(k):
                for par in range(2):
                    g = 2 * k + par
                    act.wait_ge(mean_ready, g + 1)
                    act.activation(std[:, par, :], mean_var[:, par, 1:2], ACT.Sqrt, bias=eps[:, :]).then_inc(std_ready, 1)
                act.wait_ge(nT_ready, k + 1)
                act.wait_ge(p_ready, 2 + 2 * k)
                act.copy(nT_sb[:, :, :, :], nT_ps[:, :, :]).then_inc(nT_copied, 1)

            def late(k):
                for par in range(2):
                    g = 2 * k + par
                    act.wait_ge(norm2_ready, 2 * (g + 1))
                    act.activation(norm[:, par, :], norm2[:, par, :], ACT.Sqrt).then_inc(norm_ready, 1)
                for par in range(2):
                    g = 2 * k + par
                    act.wait_ge(sT_ready, g + 1)
                    act.wait_ge(forms_ready, g + 1)
                    act.copy(split[:, par, 0:PH, 0, :], forms[:, par, Q, :, :])
                    act.copy(split[:, par, PH:2 * PH, :, :],
                             forms[:, par, K, :, :].unsqueeze(2).broadcast_to([P, PH, 2, E])).then_inc(high_ready, 1)
                for par in range(2):
                    g = 2 * k + par
                    act.wait_ge(sT_ready, 2 + g + 1)
                    if par == 0:
                        act.wait_ge(v_free, 1 + k + 1)
                    act.copy(sT_sb[:, par, :, :], sT_ps[:, 0:LAST])
                    act.copy(lT_sb[:, par, :], sT_ps[0:E + 2, LAST:LAST + P]).then_inc(sT_copied, 1)

            pipelined(act, early, late)

        @block.vector
        def _(dve):
            dve.sem_inc(n_ready, 2)
            dve.sem_inc(raw_ready, 2)
            dve.sem_inc(split_ready, 2)
            dve.memset(eps[:, :], LN_EPS)
            dve.memset(ks_sb[:, :, :], 0.0).then_inc(preset, 1)
            dve.wait_ge(preset, 1)
            dve.wait_ge(const_in, CONST)

            def early(k):
                for par in range(2):
                    dve.wait_ge(x_in[par], 16 * (k + 1))
                    dve.bn_stats(stats[:, par, :], x_sb[:, par, :]).then_inc(stats_ready, 1)
                dve.wait_ge(stats_ready, 2 * k + 2)
                dve.memset(junk[:, 0, 0:1], 0.0)
                for par in range(2):
                    dve.bn_aggr(mean_var[:, par, :], stats[:, par, :]).then_inc(mean_ready, 1)

            def normalise(k):
                for par in range(2):
                    dve.wait_ge(std_ready, 2 * k + par + 1)
                    dve.reciprocal(rstd[:, par, :], std[:, par, :]).then_inc(rstd_ready, 1)
                for par in range(2):
                    g = 2 * k + par
                    dve.wait_ge(rstd_ready, g + 1)
                    dve.wait_ge(nT_copied, k + 1)
                    dve.tensor_scalar(n_sb[:, par, :], x_sb[:, par, :], mean_var[:, par, 0:1], rstd[:, par, :],
                                      ALU.subtract, ALU.mult).then_inc(n_ready, 1)

            def take_products(k):
                for par in range(2):
                    g = 2 * k + par
                    dve.wait_ge(p_ready, 2 + g + 1)
                    dve.wait_ge(v_free, k + 1)
                    dve.tensor_tensor(v_sb[:, par, :, :], p_ps[:, par, 2 * HE:3 * HE], b_sb[:, 2 * HE:3 * HE],
                                      ALU.add)
                    dve.tensor_tensor(raw[:, par, :, :, :], p_ps[:, par, 0:2 * HE], b_sb[:, 0:2 * HE],
                                      ALU.add).then_inc(raw_ready, 1)

            def square_sums(k):
                for par in range(2):
                    g = 2 * k + par
                    normed = raw[:, par, :, COS:L2 + 1:L2 - COS, :]
                    dve.wait_ge(raw_ready, 2 + g + 1)
                    dve.tensor_tensor(square[:, par, :, :, :], normed, normed, ALU.mult).then_inc(norm2_ready, 1)
                    dve.wait_ge(norm2_ready, 2 * g + 1)
                    dve.tensor_reduce(norm2[:, par, :].rearrange("p (a b) -> p a b", a=2), square[:, par, :, :, :],
                                      AX.X, ALU.add).then_inc(norm2_ready, 1)

            def make_forms(k):
                for par in range(2):
                    g = 2 * k + par
                    q, kk = raw[:, par, Q, :, :], raw[:, par, K, :, :]
                    f = forms[:, par, :, :, :]
                    dve.wait_ge(sT_ready, g + 1)
                    dve.wait_ge(ks_free, k + 1)
                    dve.tensor_scalar(f[:, Q, 0, :], q[:, SDP, :], float(E) ** -0.5, None, ALU.mult)
                    dve.tensor_scalar(f[:, Q, 2, :], q[:, L2, :], -2.0, None, ALU.mult)
                    dve.tensor_copy(f[:, K, 0:PH:2, :], kk[:, SDP:L2 + 1:L2 - SDP, :])
                    dve.tensor_scalar(last[:, par, 0:E], q[:, L1, :], 2.0, None, ALU.mult)
                    dve.tensor_scalar(ks_sb[:, par, 0:E], kk[:, L1, :], 2.0, None, ALU.mult)
                    dve.tensor_scalar(ks_sb[:, par, E:2 * E], kk[:, L1, :], -1.0, None, ALU.mult)
                    dve.tensor_tensor_reduce(junk[:, par, :], kk[:, L1, :], share_sb[:, :], 1.0, 0.0,
                                             ALU.mult, ALU.add, ks_sb[:, par, 2 * E:2 * E + 1])
                    dve.wait_ge(norm2_ready, 2 * (g + 1))
                    dve.tensor_copy(last.bitcast(F32R)[:, par, E:E + 1], norm2[:, par, 3:4])
                    dve.tensor_copy(ks_sb[:, par, NORM_AT:NORM_AT + 1], norm2[:, par, 1:2])
                    dve.tensor_scalar(ks_sb[:, par, NORM_AT + 1:NORM_AT + 2], norm2[:, par, 1:2], -1.0, None, ALU.mult)
                    dve.wait_ge(norm_ready, g + 1)
                    dve.reciprocal(rnorm[:, par, :], norm[:, par, :]).then_inc(rnorm_ready, 1)
                for par in range(2):
                    g = 2 * k + par
                    f = forms[:, par, :, :, :]
                    dve.wait_ge(rnorm_ready, g + 1)
                    dve.tensor_scalar(f[:, Q, 1, :], raw[:, par, Q, COS, :], rnorm[:, par, 0:1], None, ALU.mult)
                    dve.tensor_scalar(f[:, K, 1, :], raw[:, par, K, COS, :], rnorm[:, par, 2:3], None,
                                      ALU.mult).then_inc(forms_ready, 1)

            def split_forms(k):
                for par in range(2):
                    g = 2 * k + par
                    high = split.bitcast(F32)[:, par, :, :, :]
                    dve.wait_ge(rnorm_ready, g + 1)
                    dve.tensor_tensor(last[:, par, E + 1:E + 2], norm2[:, par, 3:4], last[:, par, E:E + 1],
                                      ALU.subtract)
                    dve.wait_ge(high_ready, g + 1)
                    dve.tensor_tensor(split[:, par, 0:PH, 1, :], forms[:, par, Q, :, :], high[:, 0:PH, 0, :],
                                      ALU.subtract)
                    dve.tensor_tensor(split[:, par, 2 * PH:3 * PH, :, :],
                                      forms[:, par, K, :, :].unsqueeze(2).broadcast_to([P, PH, 2, E]),
                                      high[:, PH:2 * PH, :, :], ALU.subtract).then_inc(split_ready, 1)

            early(0)
            normalise(0)
            with dve.Fori(0, PAIRS1 - 1) as k:
                early(k + 1)
                take_products(k)
                normalise(k + 1)
                square_sums(k)
                make_forms(k)
                split_forms(k)
            take_products(PAIRS1 - 1)
            square_sums(PAIRS1 - 1)
            make_forms(PAIRS1 - 1)
            split_forms(PAIRS1 - 1)


def distances(nc, rows2, ks, ident, out):
    QW = BANK
    QT = QW // P
    KT = 4
    STEPS = N // (KT * P)
    HELD = TOKENS // QW
    TURN = 4
    n_abs = len(SCALAR_E) * KT
    n_max = len(MAX_E) * KT
    n_acc = len(SUM_E) * KT
    with ExitStack() as ctx:
        a = Place(nc, ctx, "distances")
        q_sb = a.sb("q", [P, E, QW])
        ks_sb = a.sb("ks", [P, 2, KT, KS])
        acc = a.sb("acc", [P, 2, KT, QW])
        diff = a.sb("diff", [P, TURN, QW])
        larger = a.sb("larger", [P, TURN, QW])
        d_sb = a.sb("d", [P, 2, QT, KT * P])
        d_ps = a.ps("d_ps", [P, 2, KT, QW])
        q_in = [a.sem(f"q_in{i}") for i in range(E // 16)]
        ks_in = a.pair("ks_in")
        acc_done = a.sem("acc_done")
        abs_done = a.sem("abs_done")
        max_done = a.sem("max_done")
        turned = a.sem("turned")
        max_turned = a.sem("max_turned")
        d_ready = a.sem("d_ready")
        d_copied = a.sem("d_copied")
        stored = a.pair("stored")
        FLUSH = 20
        PART = E // len(q_in)
        block = ctx.enter_context(nc.Block())

        def steps(eng, body):
            with eng.Fori(0, HELD) as i:
                with eng.Fori(0, STEPS // 2) as j:
                    for par in range(2):
                        body(i, i * (STEPS // 2) + j, par)

        @block.sync
        def _(sp):
            sp.sem_inc(stored[0], 16)
            sp.sem_inc(stored[1], 32)
            ks_tiles = ks.rearrange("(t p) m -> p t m", p=P)
            out_tiles = out.rearrange("(t p) n -> p t n", p=P)
            HALF = STEPS // 2

            def load_ks(k, par):
                batch = k // (HALF * HELD // B)
                step = 2 * (k % HALF) + par
                sp.dma_start(ks_sb[:, par, :, :], ks_tiles[:, bass.ds(batch * TILES + step * KT, KT), :]
                             ).then_inc(ks_in[par], 16)

            def store(k, par):
                step = 2 * (k % HALF) + par
                sp.dma_start(out_tiles[:, bass.ds((k // HALF) * QT, QT), bass.ds(step * KT * P, KT * P)],
                             d_sb[:, par, :, :]).then_inc(stored[par], 16)

            load_ks(0, 0)
            load_ks(0, 1)
            with sp.Fori(0, HELD * HALF - 1) as k:
                for par in range(2):
                    sp.wait_ge(d_copied, 2 + 2 * k + par + 1)
                    load_ks(k + 1, par)
                    store(k, par)
            for par in range(2):
                sp.wait_ge(d_copied, 2 + 2 * (HELD * HALF - 1) + par + 1)
                store(HELD * HALF - 1, par)
            sp.wait_ge(stored[0], 16 * (HELD * HALF + 1))
            sp.wait_ge(stored[1], 16 * (HELD * HALF + 2))

        @block.gpsimd
        def _(pool):
            with pool.Fori(0, HELD) as i:
                for part, s in enumerate(q_in):
                    e = part * PART
                    for done, share in ((acc_done, SUM_E), (max_done, MAX_E), (abs_done, SCALAR_E)):
                        pool.wait_ge(done, len(share) * KT * STEPS * i + sum(x < e + PART for x in share) * KT)
                    pool.dma_start(q_sb[:, e:e + PART, :],
                                   rows2[e:e + PART, bass.ds(i * QW, QW)].partition_broadcast(P)
                                   ).then_inc(s, 16)

        @block.tensor
        def _(pe):
            pe.sem_inc(turned, TURN)
            pe.sem_inc(max_turned, TURN)
            pe.sem_inc(d_ready, 2 * KT)

            def turn(par, j, src, start, stop):
                for t in range(QT):
                    mm = pe.matmul(d_ps[:, par, j, t * P:(t + 1) * P], src[:, t * P:(t + 1) * P], ident[:, :],
                                   is_transpose=True, start=start and t == 0, stop=stop, skip_group_check=True)
                return mm

            def body(i, k, par):
                g = 2 * k + par
                pe.wait_ge(d_copied, g + 1)
                started = [False] * KT
                for is_max, n in merged(n_abs, n_max):
                    j = n % KT
                    if is_max:
                        pe.wait_ge(max_done, n_max + n_max * g + n + 1)
                        turn(par, j, larger[:, n % TURN, :], not started[j], False).then_inc(max_turned, 1)
                    else:
                        pe.wait_ge(abs_done, n_abs + n_abs * g + n + 1)
                        turn(par, j, diff[:, n % TURN, :], not started[j], False).then_inc(turned, 1)
                    started[j] = True
                pe.wait_ge(acc_done, n_acc + n_acc * (g + 1))
                for j in range(KT):
                    turn(par, j, acc[:, par, j, :], False, True).then_inc(d_ready, 1)

            steps(pe, body)

        @block.scalar
        def _(act):
            act.sem_inc(abs_done, n_abs)

            def body(i, k, par):
                g = 2 * k + par
                act.wait_ge(ks_in[par], 16 * (k + 1))
                n = 0
                for e in SCALAR_E:
                    act.wait_ge(q_in[e // PART], 16 * (i + 1))
                    for j in range(KT):
                        act.wait_ge(turned, n_abs * g + n + 1)
                        act.activation(diff[:, n % TURN, :], q_sb[:, e, :], ACT.Abs,
                                       bias=ks_sb[:, par, j, E + e:E + e + 1], scale=0.5).then_inc(abs_done, 1)
                        n += 1

            steps(act, body)

        @block.vector
        def _(dve):
            dve.sem_inc(acc_done, n_acc)
            dve.sem_inc(max_done, n_max)
            dve.sem_inc(d_copied, 1)
            dve.memset(d_ps[:, 1, :, :], 0.0)

            def take_distances(par, ready):
                for j in range(KT):
                    dve.wait_ge(d_ready, ready + j + 1)
                    ins = dve.tensor_copy(d_sb[:, par, :, j * P:(j + 1) * P], d_ps[:, par, j, :])
                ins.then_inc(d_copied, 1)

            def body(i, k, par):
                g = 2 * k + par
                dve.wait_ge(ks_in[par], 16 * (k + 1))
                dve.wait_ge(d_ready, KT * (g + 1))
                for is_max, n in merged(n_acc, n_max):
                    r, j = n // KT, n % KT
                    e = (MAX_E if is_max else SUM_E)[r]
                    k2 = ks_sb[:, par, j, e:e + 1]
                    if j == 0:
                        dve.wait_ge(q_in[e // PART], 16 * (i + 1))
                    if is_max:
                        dve.wait_ge(max_turned, n_max * g + n + 1)
                        dve.tensor_scalar(larger[:, n % TURN, :], q_sb[:, e, :], k2, None, ALU.max
                                          ).then_inc(max_done, 1)
                    elif r == 0:
                        dve.tensor_scalar(acc[:, par, j, :], q_sb[:, e, :], k2,
                                          ks_sb[:, par, j, 2 * E:2 * E + 1], ALU.max, ALU.subtract
                                          ).then_inc(acc_done, 1)
                    else:
                        dve.wait_ge(acc_done, n_acc + n_acc * g + n - KT + 1)
                        dve.scalar_tensor_tensor(acc[:, par, j, :], q_sb[:, e, :], k2,
                                                 acc[:, par, j, :], ALU.max, ALU.add).then_inc(acc_done, 1)
                    if not is_max and n == FLUSH:
                        dve.wait_ge(stored[1 - par], 16 * (k + 1))
                        take_distances(1 - par, 2 * KT + KT * (g - 1))

            steps(dve, body)
            dve.wait_ge(stored[1], 16 * (HELD * STEPS // 2 + 1))
            take_distances(1, 2 * KT + KT * (HELD * STEPS - 1))


def route(nc, t1, attended, routerT, ident, base, uT, weights):
    MT = TOKENS // P
    with ExitStack() as ctx:
        a = Place(nc, ctx, "route")
        r_sb = a.sb("r", [P, DC, EXPERTS])
        eps = a.sb("eps", [P, 1])
        x_sb = a.sb("x", [P, 2, D])
        att_sb = a.sb("att", [P, 2, H, E])
        t2_sb = a.sb("t2", [P, 2, D])
        stats = a.sb("stats", [P, 2, 6])
        mean_var = a.sb("mean_var", [P, 2, 2])
        std = a.sb("std", [P, 2, 1])
        rstd = a.sb("rstd", [P, 2, 1])
        u_sb = a.sb("u", [P, 2, D])
        junk = a.sb("junk", [P, 1])
        base_sb = a.sb("base", [P, 2, D])
        uT_sb = a.sb("uT", [P, 2, DC, P])
        logits = a.sb("logits", [P, MT, EXPERTS])
        probs = a.sb("probs", [P, MT, EXPERTS])
        rank = a.sb("rank", [P, MT, EXPERTS])
        above = a.sb("above", [P, MT, EXPERTS])
        row = a.sb("row", [P, MT])
        w_sb = a.sb("w", [P, MT, EXPERTS])
        uT_ps = a.ps("uT_ps", [P, 2, BANK])
        l_ps = a.ps("l_ps", [P, 2, BANK])
        const_in = a.sem("const_in")
        preset = a.sem("preset")
        x_in = a.pair("x_in")
        steps = a.sem("steps")
        std_ready = a.sem("std_ready")
        u_ready = a.sem("u_ready")
        base_ready = a.sem("base_ready")
        uT_ready = a.sem("uT_ready")
        uT_copied = a.sem("uT_copied")
        l_ready = a.sem("l_ready")
        l_copied = a.sem("l_copied")
        stored = a.sem("stored")
        out_free = a.sem("out_free")
        choice = a.sem("choice")
        exp_done = a.sem("exp_done")
        w_ready = a.sem("w_ready")
        stored_w = a.sem("stored_w")
        CONST = 16
        att_rows = attended.rearrange("(h n) e -> n h e", h=H)
        uT_cols = uT.rearrange("(c p) n -> p c n", p=P)
        block = ctx.enter_context(nc.Block())

        @block.sync
        def _(sp):
            sp.dma_start(r_sb[:, :, :], routerT.rearrange("(c p) e -> p c e", p=P)).then_inc(const_in, 16)
            with sp.Fori(0, MT // 2) as k:
                for par in range(2):
                    g = 2 * k + par
                    sp.wait_ge(u_ready, g + 1)
                    sp.dma_start(x_sb[:, par, :], t1[bass.ds(g * P, P), :]).then_inc(x_in[par], 16)
                    sp.dma_start(att_sb[:, par, :, :], att_rows[bass.ds(g * P, P), :, :]).then_inc(x_in[par], 16)
            sp.wait_ge(w_ready, 1)
            sp.dma_start(weights.rearrange("(t p) e -> p t e", p=P), w_sb[:, :, :]).then_inc(stored_w, 16)
            sp.wait_ge(stored_w, 16)

        @block.gpsimd
        def _(pool):
            pool.sem_inc(out_free, 2)
            with pool.Fori(0, MT // 2) as k:
                for par in range(2):
                    g = 2 * k + par
                    pool.wait_ge(base_ready, 2 + g + 1)
                    pool.dma_start(base[bass.ds(g * P, P), :], base_sb[:, par, :]).then_inc(stored, 16)
                    pool.wait_ge(uT_copied, 2 + g + 1)
                    pool.dma_start(uT_cols[:, :, bass.ds(g * P, P)], uT_sb[:, par, :, :]).then_inc(stored, 16)
                    pool.wait_ge(stored, 32 * (g + 1))
                    pool.sem_inc(out_free, 1)

        @block.tensor
        def _(pe):
            pe.sem_inc(l_ready, 2)
            pe.wait_ge(const_in, CONST)
            with pe.Fori(0, MT // 2) as k:
                for par in range(2):
                    g = 2 * k + par
                    pe.wait_ge(u_ready, 2 + g + 1)
                    pe.wait_ge(uT_copied, g + 1)
                    for c in range(DC):
                        mm = pe.transpose(uT_ps[:, par, c * P:(c + 1) * P], u_sb[:, par, c * P:(c + 1) * P], ident[:, :])
                    mm.then_inc(uT_ready, 1)
                    pe.wait_ge(uT_copied, 2 + g + 1)
                    pe.wait_ge(l_copied, g + 1)
                    for c in range(DC):
                        mm = pe.matmul(l_ps[:, par, 0:EXPERTS], uT_sb[:, par, c, :], r_sb[:, c, :],
                                       start=c == 0, stop=c == DC - 1)
                    mm.then_inc(l_ready, 1)

        @block.scalar
        def _(act):
            act.sem_inc(uT_copied, 2)
            act.wait_ge(preset, 1)
            with act.Fori(0, MT // 2) as k:
                for par in range(2):
                    g = 2 * k + par
                    act.wait_ge(steps, 4 * g + 3)
                    act.activation(std[:, par, :], mean_var[:, par, 1:2], ACT.Sqrt, bias=eps[:, :]).then_inc(std_ready, 1)
                    act.wait_ge(uT_ready, g + 1)
                    act.wait_ge(l_ready, g + 1)
                    act.wait_ge(out_free, g + 1)
                    act.copy(uT_sb[:, par, :, :], uT_ps[:, par, 0:D]).then_inc(uT_copied, 1)
            act.wait_ge(choice, 2)
            act.activation(probs[:, :, :], logits[:, :, :], ACT.Exp).then_inc(exp_done, 1)

        @block.vector
        def _(dve):
            dve.sem_inc(u_ready, 2)
            dve.sem_inc(base_ready, 2)
            dve.sem_inc(l_copied, 2)
            dve.memset(eps[:, :], LN_EPS).then_inc(preset, 1)

            def take_logits(k, par):
                g = 2 * k + par
                dve.wait_ge(l_ready, 2 + g + 1)
                dve.tensor_copy(logits[:, bass.ds(g, 1), :], l_ps[:, par, 0:EXPERTS]).then_inc(l_copied, 1)

            def normalise(k, par):
                g = 2 * k + par
                dve.wait_ge(x_in[par], 32 * (k + 1))
                dve.tensor_tensor(t2_sb[:, par, :], x_sb[:, par, :], att_sb[:, par, :, :], ALU.add).then_inc(steps, 1)
                dve.wait_ge(steps, 4 * g + 1)
                dve.bn_stats(stats[:, par, :], t2_sb[:, par, :]).then_inc(steps, 1)
                dve.wait_ge(steps, 4 * g + 2)
                dve.memset(junk[:, :], 0.0)
                dve.bn_aggr(mean_var[:, par, :], stats[:, par, :]).then_inc(steps, 1)
                dve.wait_ge(std_ready, g + 1)
                dve.reciprocal(rstd[:, par, :], std[:, par, :]).then_inc(steps, 1)
                dve.wait_ge(steps, 4 * g + 4)
                dve.wait_ge(uT_copied, g + 1)
                dve.tensor_scalar(u_sb[:, par, :], t2_sb[:, par, :], mean_var[:, par, 0:1], rstd[:, par, :],
                                  ALU.subtract, ALU.mult).then_inc(u_ready, 1)
                dve.wait_ge(u_ready, 2 + g + 1)
                dve.wait_ge(out_free, g + 1)
                dve.tensor_tensor(base_sb[:, par, :], t2_sb[:, par, :], u_sb[:, par, :], ALU.add).then_inc(base_ready, 1)

            with dve.Fori(0, MT // 2) as k:
                normalise(k, 0)
                normalise(k, 1)
                take_logits(k, 0)
                take_logits(k, 1)

            done = [0]

            def step(ins):
                done[0] += 1
                ins.then_inc(choice, 1)
                dve.wait_ge(choice, done[0])

            def per_token(x):
                return x[:, :].unsqueeze(2).broadcast_to([P, MT, EXPERTS])

            dve.wait_ge(l_copied, 2 + MT)
            step(dve.tensor_reduce(row[:, :], logits[:, :, :], AX.X, ALU.max))
            step(dve.tensor_tensor(logits[:, :, :], logits[:, :, :], per_token(row), ALU.subtract))
            dve.wait_ge(exp_done, 1)
            step(dve.tensor_reduce(row[:, :], probs[:, :, :], AX.X, ALU.add))
            step(dve.reciprocal(row[:, :], row[:, :]))
            step(dve.tensor_tensor(probs[:, :, :], probs[:, :, :], per_token(row), ALU.mult))
            for j in range(EXPERTS):
                pj = probs[:, :, j:j + 1]
                dst = rank if j == 0 else above
                if j + 1 < EXPERTS:
                    step(dve.tensor_tensor(dst[:, :, j + 1:], pj.broadcast_to([P, MT, EXPERTS - 1 - j]),
                                           probs[:, :, j + 1:], ALU.is_ge))
                step(dve.tensor_tensor(dst[:, :, 0:j + 1], pj.broadcast_to([P, MT, j + 1]),
                                       probs[:, :, 0:j + 1], ALU.is_gt))
                if j:
                    step(dve.tensor_tensor(rank[:, :, :], rank[:, :, :], above[:, :, :], ALU.add))
            step(dve.tensor_scalar(rank[:, :, :], rank[:, :, :], float(TOP), None, ALU.is_lt))
            step(dve.tensor_tensor(probs[:, :, :], probs[:, :, :], rank[:, :, :], ALU.mult))
            step(dve.tensor_reduce(row[:, :], probs[:, :, :], AX.X, ALU.add))
            step(dve.tensor_scalar(row[:, :], row[:, :], 1e-12, None, ALU.max))
            step(dve.reciprocal(row[:, :], row[:, :]))
            dve.tensor_tensor(w_sb[:, :, :], probs[:, :, :], per_token(row), ALU.mult).then_inc(w_ready, 1)


def experts(nc, base, uT, weights, w1, b1, w2, b2, out):
    G = BANK
    TG = G // P
    LOOPS = TOKENS // G // 2
    with ExitStack() as ctx:
        a = Place(nc, ctx, "experts")
        w1_sb = a.sb("w1", [P, EXPERTS, DC, D])
        w2_sb = a.sb("w2", [P, EXPERTS, DC, D])
        b1_sb = a.sb("b1", [P, EXPERTS, DC])
        b2_sb = a.sb("b2", [P, EXPERTS, D])
        u_sb = a.sb("u", [P, 2, DC, G])
        wt_sb = a.sb("wt", [P, 2, TG, EXPERTS])
        acc = a.sb("acc", [P, 2, TG, D])
        h_sb = a.sb("h", [P, 2, DC, G])
        h_ps = a.ps("h_ps", [P, 2, DC, G])
        y_ps = a.ps("y_ps", [P, 2, TG, D])
        w_in = a.sem("w_in")
        group_in = a.pair("group_in")
        h_ready = a.sem("h_ready")
        h_done = a.sem("h_done")
        y_ready = a.sem("y_ready")
        b_added = a.sem("b_added")
        y_added = a.sem("y_added")
        acc_free = a.sem("acc_free")
        stored = a.sem("stored")
        CONST = 16 * 4
        block = ctx.enter_context(nc.Block())

        def rows(x, g):
            return x.rearrange("(t p) d -> p t d", p=P)[:, bass.ds(g * TG, TG), :]

        @block.sync
        def _(sp):
            sp.dma_start(w1_sb[:, :, :, :], w1.rearrange("e (c p) f -> p e c f", p=P)).then_inc(w_in, 16)
            sp.dma_start(w2_sb[:, :, :, :], w2.rearrange("e (c p) f -> p e c f", p=P)).then_inc(w_in, 16)
            sp.dma_start(b1_sb[:, :, :], b1).then_inc(w_in, 16)
            sp.dma_start(b2_sb[:, :, :], b2.partition_broadcast(P)).then_inc(w_in, 16)
            with sp.Fori(0, LOOPS) as i:
                for par in range(2):
                    g = 2 * i + par
                    sp.wait_ge(acc_free, g + 1)
                    sp.dma_start(u_sb[:, par, :, :], uT.rearrange("(c p) n -> p c n", p=P)[:, :, bass.ds(g * G, G)]
                                 ).then_inc(group_in[par], 16)
                    sp.dma_start(wt_sb[:, par, :, :], rows(weights, g)).then_inc(group_in[par], 16)
                    sp.dma_start(acc[:, par, :, :], rows(base, g)).then_inc(group_in[par], 16)

        @block.gpsimd
        def _(pool):
            pool.sem_inc(acc_free, 2)
            with pool.Fori(0, LOOPS) as i:
                for par in range(2):
                    g = 2 * i + par
                    pool.wait_ge(y_added, 2 * TG + EXPERTS * TG * (g + 1))
                    pool.dma_start(rows(out, g), acc[:, par, :, :]).then_inc(stored, 16)
                    pool.wait_ge(stored, 16 * (g + 1))
                    pool.sem_inc(acc_free, 1)

        @block.tensor
        def _(pe):
            pe.sem_inc(h_ready, 2 * DC)
            pe.sem_inc(y_ready, 2)
            pe.wait_ge(w_in, CONST)

            def hidden(g, par, e):
                n = EXPERTS * g + e
                for f in range(DC):
                    pe.wait_ge(h_done, DC * n + f + 1)
                    for c in range(DC):
                        mm = pe.matmul(h_ps[:, e % 2, f, :], w1_sb[:, e, c, f * P:(f + 1) * P],
                                       u_sb[:, par, c, :], start=c == 0, stop=c == DC - 1)
                    mm.then_inc(h_ready, 1)

            def output(g, e):
                n = EXPERTS * g + e
                pe.wait_ge(h_done, 2 * DC + DC * (n + 1))
                pe.wait_ge(y_added, TG * (n + 1))
                for t in range(TG):
                    for f in range(DC):
                        mm = pe.matmul(y_ps[:, e % 2, t, :], h_sb[:, e % 2, f, t * P:(t + 1) * P],
                                       w2_sb[:, e, f, :], start=f == 0, stop=f == DC - 1)
                mm.then_inc(y_ready, 1)

            with pe.Fori(0, LOOPS) as i:
                for par in range(2):
                    g = 2 * i + par
                    pe.wait_ge(group_in[par], 48 * (i + 1))
                    hidden(g, par, 0)
                    for e in range(1, EXPERTS):
                        hidden(g, par, e)
                        output(g, e - 1)
                    output(g, EXPERTS - 1)

        @block.scalar
        def _(act):
            act.sem_inc(h_done, 2 * DC)
            act.wait_ge(w_in, CONST)
            with act.Fori(0, LOOPS) as i:
                for par in range(2):
                    for e in range(EXPERTS):
                        n = EXPERTS * (2 * i + par) + e
                        act.wait_ge(y_ready, n + 1)
                        for f in range(DC):
                            act.wait_ge(h_ready, 2 * DC + DC * n + f + 1)
                            act.activation(h_sb[:, e % 2, f, :], h_ps[:, e % 2, f, :], ACT.Gelu,
                                           bias=b1_sb[:, e, f:f + 1]).then_inc(h_done, 1)

        @block.vector
        def _(dve):
            dve.sem_inc(y_added, 2 * TG)
            dve.wait_ge(w_in, CONST)
            with dve.Fori(0, LOOPS) as i:
                for par in range(2):
                    dve.wait_ge(group_in[par], 48 * (i + 1))
                    for e in range(EXPERTS):
                        n = EXPERTS * (2 * i + par) + e
                        for t in range(TG):
                            if e:
                                dve.wait_ge(y_added, 2 * TG + TG * (n - 1) + t + 1)
                            dve.scalar_tensor_tensor(acc[:, par, t, :], b2_sb[:, e, :], wt_sb[:, par, t, e:e + 1],
                                                     acc[:, par, t, :], ALU.mult, ALU.add).then_inc(b_added, 1)
                        dve.wait_ge(y_ready, 2 + n + 1)
                        for t in range(TG):
                            dve.wait_ge(b_added, TG * n + t + 1)
                            dve.scalar_tensor_tensor(acc[:, par, t, :], y_ps[:, e % 2, t, :],
                                                     wt_sb[:, par, t, e:e + 1], acc[:, par, t, :],
                                                     ALU.mult, ALU.add).then_inc(y_added, 1)


def build(nc, t, out):
    with nc.sbuf_tensor("ident", [P, P], F32) as ident:
        stages(nc, t, ident, out)


def stages(nc, t, ident, out):
    def scratch(name, shape):
        return nc.dram_tensor(name, list(shape), F32, kind="Internal").ap()

    q0T, k0T = scratch("q0T", (P, TOKENS)), scratch("k0T", (P, TOKENS))
    v0, t1 = scratch("v0", (TOKENS, D)), scratch("t1", (TOKENS, D))
    parts = scratch("parts", (P, 3 * PH * TOKENS))
    rows2 = scratch("rows2", (E + 2, TOKENS))
    ks, v = scratch("ks", (TOKENS, KS)), scratch("v", (H * TOKENS, E))
    dist = scratch("dist", (TOKENS, N))
    attended = scratch("attended", (H * TOKENS, E))
    base, uT, weights = scratch("base", (TOKENS, D)), scratch("uT", (D, TOKENS)), scratch("weights", (TOKENS, EXPERTS))

    project0(nc, t["xT"], t["wqk0"], t["bqk0"], t["signs0"], t["wv0"], t["bv0"], t["identity"], ident,
             q0T, k0T, v0)
    attend(nc, "attend0", B, D, q0T, [k0T], v0, "dot", "residual", ident, t1, gamma=t["gamma"], x=t["x"])
    project1(nc, t1, t["wqkv"], t["bqkv"], t["share"], ident, parts, rows2, ks, v)
    distances(nc, rows2, ks, ident, dist)

    def rows(x, head, heads):
        return x[head * TOKENS:(head + heads) * TOKENS, :]

    def products(stage, first, heads, kind, **more):
        at = PRODUCT_HEADS.index(first)
        q, k_high, k_low = (parts[:, (at + m * PH) * TOKENS:(at + m * PH + heads) * TOKENS] for m in range(3))
        attend(nc, stage, heads * B, E, q, [k_high, k_low], rows(v, first, heads), kind, "plain", ident,
               rows(attended, first, heads), **more)

    products("products", SDP, 2, "dot")
    attend(nc, "l1", B, E, None, [], rows(v, L1, 1), "l1", "plain", ident, rows(attended, L1, 1), scores=dist)
    products("l2", L2, 1, "l2", norms=ks[:, NORM_AT:NORM_AT + 2], norm_rows=rows2[E:E + 2, :])
    route(nc, t1, attended, t["routerT"], ident, base, uT, weights)
    experts(nc, base, uT, weights, t["w1"], t["b1"], t["w2"], t["b2"], out)


def lay_out(inputs):
    import numpy as np

    def heads(w):
        return w.transpose(1, 0, 2).reshape(D, H * E)

    QUADS, Q_LOW, K_LOW = P // C0, (1, 3), (2, 3)

    def quads(b, *where):
        out = np.zeros((QUADS, C0), np.float32)
        out[list(where)] = b
        return out.reshape(P)

    q_low, k_low = (quads(np.ones(C0, np.float32), *where) for where in (Q_LOW, K_LOW))
    i = {name: np.asarray(x) for name, x in inputs.items()}
    x = i["x"].reshape(TOKENS, D)
    arrays = {
        "x": x, "xT": x.T, "identity": np.eye(P, dtype=np.float32),
        "wqk0": np.concatenate([i["L0_conv_Wq"]] * QUADS + [i["L0_conv_Wk"]] * QUADS).T,
        "bqk0": np.stack([quads(i["L0_conv_bq"], 0, 1, 2, 3), quads(i["L0_conv_bq"], *Q_LOW),
                          quads(i["L0_conv_bk"], 0, 1, 2, 3), quads(i["L0_conv_bk"], *K_LOW)], axis=1),
        "signs0": np.stack([1 - 2 * q_low, q_low, 1 - 2 * k_low, k_low], axis=1),
        "wv0": i["L0_conv_Wv"].T, "bv0": i["L0_conv_bv"], "gamma": i["L0_conv_gamma"],
        "wqkv": np.concatenate([heads(i[f"L1_attn_W{c}"]) for c in "qkv"], axis=1),
        "bqkv": np.concatenate([i[f"L1_attn_b{c}"].reshape(-1) for c in "qkv"]),
        "share": np.array([e in VECTOR_E for e in range(E)], np.float32),
        "routerT": i["L1_ffn_router_w"].T,
        "w1": i["L1_ffn_w1"], "b1": i["L1_ffn_b1"].reshape(EXPERTS, DC, P).transpose(2, 0, 1),
        "w2": i["L1_ffn_w2"], "b2": i["L1_ffn_b2"],
    }
    return {name: np.ascontiguousarray(x) for name, x in arrays.items()}


def kernel(**inputs):
    import concourse.bacc as bacc
    from concourse.bass_utils import run_bass_kernel_spmd

    nc = bacc.Bacc("TRN2", target_bir_lowering=False, num_devices=1)
    arrays = lay_out(inputs)
    tensors = {name: nc.dram_tensor(name, x.shape, mybir.dt.from_np(x.dtype), kind="ExternalInput").ap()
               for name, x in arrays.items()}
    out = nc.dram_tensor("out", (TOKENS, D), F32, kind="ExternalOutput").ap()
    build(nc, tensors, out)
    result = run_bass_kernel_spmd(nc, [arrays], core_ids=[0])
    return result.results[0]["out"].reshape(inputs["x"].shape)
```

```python
from contextlib import ExitStack

import concourse.bass as bass
from concourse import mybir

P = 128
F32 = mybir.dt.float32
F32R = mybir.dt.float32r
ALU = mybir.AluOpType
ACT = mybir.ActivationFunctionType
AX = mybir.AxisListType

B, N, D = 2, 4096, 256
TOKENS = B * N
C0 = D // 8
H, E = 4, 64
DC = D // P
TILES = N // P
PAIRS = TILES // 2
SDP, COS, L1, L2 = range(H)
PRODUCT_HEADS = [SDP, COS, L2]
PH = len(PRODUCT_HEADS)
KS = 2 * E + 4
NORM_AT = 2 * E + 1
EXPERTS, TOP = 8, 2
LN_EPS = 1e-5
BANK = 512


def spread(count, among):
    n = len(among)
    return [x for i, x in enumerate(among) if (i * count) // n != ((i + 1) * count) // n]


def merged(*queues):
    return [(q, n) for _, q, n in sorted(((n + 0.5) / length, q, n)
                                         for q, length in enumerate(queues) for n in range(length))]


HALF_E = E // 2
ON_SCALAR, ON_MAX = 17, 2
SCALAR_E = spread(ON_SCALAR, range(HALF_E))
VECTOR_E = [e for e in range(HALF_E) if e not in SCALAR_E]
MAX_E = spread(ON_MAX, VECTOR_E)
SUM_E = [e for e in VECTOR_E if e not in MAX_E]


class Place:

    def __init__(self, nc, ctx, stage):
        self.nc, self.ctx, self.stage = nc, ctx, stage

    def sb(self, name, shape, dtype=F32):
        return self.ctx.enter_context(self.nc.sbuf_tensor(f"{self.stage}_{name}", shape, dtype))

    def ps(self, name, shape):
        return self.ctx.enter_context(self.nc.psum_tensor(f"{self.stage}_{name}", shape, F32))

    def sem(self, name):
        return self.ctx.enter_context(self.nc.semaphore(f"{self.stage}_{name}"))

    def pair(self, name):
        return [self.sem(f"{name}{par}") for par in range(2)]


def project0(nc, xT, wqk, bqk, signs, wv, bv, identity, ident, qT, kT, v):
    G = BANK
    TG = G // P
    LOOPS = TOKENS // G // 2
    with ExitStack() as ctx:
        a = Place(nc, ctx, "project0")
        x_sb = a.sb("x", [P, 2, DC, G])
        wqk_sb = a.sb("wqk", [P, DC, 2 * P])
        wv_sb = a.sb("wv", [P, DC, D])
        bqk_sb = a.sb("bqk", [P, 4])
        signs_sb = a.sb("signs", [P, 4])
        bv_sb = a.sb("bv", [P, TG, D])
        high = a.sb("high", [P, 2, 2, G], F32R)
        full = a.sb("full", [P, 2, 2, G])
        q_sb = a.sb("q", [P, 2, G], F32R)
        k_sb = a.sb("k", [P, 2, G], F32R)
        v_sb = a.sb("v", [P, 2, TG, D])
        q_ps = a.ps("q_ps", [P, 2, G])
        k_ps = a.ps("k_ps", [P, 2, G])
        v_ps = a.ps("v_ps", [P, 2, TG, D])
        weights_in = a.sem("weights_in")
        x_in = a.pair("x_in")
        qk_ready = a.sem("qk_ready")
        v_ready = a.sem("v_ready")
        qk_copied = a.sem("qk_copied")
        qk_out = a.sem("qk_out")
        v_out = a.sem("v_out")
        stored = a.sem("stored")
        out_free = a.sem("out_free")
        WEIGHTS = 16 * (5 + TG)
        x_cols = xT.rearrange("(c p) n -> p c n", p=P)
        v_rows = v.rearrange("(t p) d -> p t d", p=P)
        block = ctx.enter_context(nc.Block())

        @block.sync
        def _(sp):
            sp.dma_start(wqk_sb[:, :, :], wqk.rearrange("(c p) m -> p c m", p=P)).then_inc(weights_in, 16)
            sp.dma_start(wv_sb[:, :, :], wv.rearrange("(c p) m -> p c m", p=P)).then_inc(weights_in, 16)
            sp.dma_start(bqk_sb[:, :], bqk).then_inc(weights_in, 16)
            sp.dma_start(signs_sb[:, :], signs).then_inc(weights_in, 16)
            sp.dma_start(ident[:, :], identity).then_inc(weights_in, 16)
            for t in range(TG):
                sp.dma_start(bv_sb[:, t, :], bv.partition_broadcast(P)).then_inc(weights_in, 16)
            with sp.Fori(0, LOOPS) as i:
                for par in range(2):
                    g = 2 * i + par
                    sp.wait_ge(v_out, g + 1)
                    sp.dma_start(x_sb[:, par, :, :], x_cols[:, :, bass.ds(g * G, G)]).then_inc(x_in[par], 16)

        @block.gpsimd
        def _(pool):
            pool.sem_inc(out_free, 2)
            with pool.Fori(0, LOOPS) as i:
                for par in range(2):
                    g = 2 * i + par
                    pool.wait_ge(qk_out, 2 + g + 1)
                    pool.dma_start(qT[:, bass.ds(g * G, G)], q_sb.bitcast(F32)[:, par, :]).then_inc(stored, 16)
                    pool.dma_start(kT[:, bass.ds(g * G, G)], k_sb.bitcast(F32)[:, par, :]).then_inc(stored, 16)
                    pool.wait_ge(v_out, 2 + g + 1)
                    pool.dma_start(v_rows[:, bass.ds(g * TG, TG), :], v_sb[:, par, :, :]).then_inc(stored, 16)
                    pool.wait_ge(stored, 48 * (g + 1))
                    pool.sem_inc(out_free, 1)

        @block.tensor
        def _(pe):
            pe.sem_inc(qk_ready, 2)
            pe.wait_ge(weights_in, WEIGHTS)
            with pe.Fori(0, LOOPS) as i:
                for par in range(2):
                    g = 2 * i + par
                    pe.wait_ge(x_in[par], 16 * (i + 1))
                    pe.wait_ge(qk_copied, g + 1)
                    for which, ps in ((0, q_ps), (1, k_ps)):
                        for c in range(DC):
                            mm = pe.matmul(ps[:, par, :], wqk_sb[:, c, which * P:(which + 1) * P],
                                           x_sb[:, par, c, :], start=c == 0, stop=c == DC - 1)
                    mm.then_inc(qk_ready, 1)
                    pe.wait_ge(v_out, g + 1)
                    for t in range(TG):
                        for c in range(DC):
                            mm = pe.matmul(v_ps[:, par, t, :], x_sb[:, par, c, t * P:(t + 1) * P],
                                           wv_sb[:, c, :], start=c == 0, stop=c == DC - 1)
                    mm.then_inc(v_ready, 1)

        @block.scalar
        def _(act):
            act.sem_inc(qk_copied, 2)
            act.wait_ge(weights_in, WEIGHTS)
            with act.Fori(0, LOOPS) as i:
                for par in range(2):
                    g = 2 * i + par
                    act.wait_ge(qk_ready, 2 + g + 1)
                    act.wait_ge(qk_out, g + 1)
                    for which, ps in ((0, q_ps), (1, k_ps)):
                        act.activation(high[:, par, which, :], ps[:, par, :], ACT.Identity,
                                       bias=bqk_sb[:, 2 * which:2 * which + 1])
                        ins = act.activation(full[:, par, which, :], ps[:, par, :], ACT.Identity,
                                             bias=bqk_sb[:, 2 * which + 1:2 * which + 2],
                                             scale=signs_sb[:, 2 * which + 1:2 * which + 2])
                    ins.then_inc(qk_copied, 1)

        @block.vector
        def _(dve):
            dve.sem_inc(v_out, 2)
            dve.sem_inc(qk_out, 2)
            dve.wait_ge(weights_in, WEIGHTS)
            with dve.Fori(0, LOOPS) as i:
                for par in range(2):
                    g = 2 * i + par
                    dve.wait_ge(out_free, g + 1)
                    dve.wait_ge(qk_copied, 2 + g + 1)
                    for which, sb in ((0, q_sb), (1, k_sb)):
                        ins = dve.scalar_tensor_tensor(sb[:, par, :], high.bitcast(F32)[:, par, which, :],
                                                       signs_sb[:, 2 * which:2 * which + 1],
                                                       full[:, par, which, :], ALU.mult, ALU.add)
                    ins.then_inc(qk_out, 1)
                    dve.wait_ge(v_ready, g + 1)
                    dve.tensor_tensor(v_sb[:, par, :, :], v_ps[:, par, :, :], bv_sb[:, :, :],
                                      ALU.add).then_inc(v_out, 1)


def attend0(nc, qT, kT, v, ident, gamma, x, out):
    R = 4
    LAG = 2
    GROUPS = TILES // R
    W = 1024
    SC = N // W
    TC = N // BANK
    KT = BANK // P
    TB = 4
    BY_SCALAR = (1, 4, 7)
    with ExitStack() as ctx:
        a = Place(nc, ctx, "attend0")
        s_sb = a.sb("s", [P, R, N])
        t_sb = a.sb("t", [P, TB, BANK])
        v_sb = a.sb("v", [P, TILES, D])
        part = a.sb("part", [P, R, SC])
        shift = a.sb("shift", [P, R])
        sums = a.sb("sums", [P, R, SC])
        total = a.sb("total", [P, R])
        recip = a.sb("recip", [P, R])
        o_sb = a.sb("o", [P, 2, D])
        scale = a.sb("scale", [P, R])
        gam = a.sb("gam", [P, 1])
        x_sb = a.sb("x", [P, R, D])
        k_sb = a.sb("k", [P, N], F32R)
        q_sb = a.sb("q", [P, R, P], F32R)
        s_ps = a.ps("s_ps", [P, 2, W])
        t_ps = a.ps("t_ps", [P, 2, BANK])
        o_ps = a.ps("o_ps", [P, 2, BANK])
        gamma_in = a.sem("gamma_in")
        v_in = a.sem("v_in")
        kv_free = a.sem("kv_free")
        q_in = [a.sem(f"q_in{r}") for r in range(R)]
        k_in = a.sem("k_in")
        s_ready = a.sem("s_ready")
        s_copied = a.sem("s_copied")
        m_ready = a.sem("m_ready")
        p_ready = a.sem("p_ready")
        t_ready = a.sem("t_ready")
        by_vector = a.sem("by_vector")
        by_scalar = a.sem("by_scalar")
        pv_done = a.sem("pv_done")
        rc_ready = a.sem("rc_ready")
        o_done = a.sem("o_done")
        stored = a.sem("stored")
        o_free = a.sem("o_free")
        TILE_IN = 16 * 2
        block = ctx.enter_context(nc.Block())

        def copied(g, c):
            by_scalar_here = c in BY_SCALAR
            mine = [x for x in range(TC) if (x in BY_SCALAR) == by_scalar_here]
            return (by_scalar if by_scalar_here else by_vector), len(mine) * g + mine.index(c) + 1

        def tiles(eng, body, behind=None):
            def step(u, k, n, first, end):
                new, mid, old = ((k + m // R, m % R) if first <= m < end else None
                                 for m in (n, n - 1, n - LAG))
                body(u, new, mid, old)

            with eng.Fori(0, B) as u:
                k0 = u * GROUPS
                for n in range(LAG):
                    step(u, k0, n, 0, R)
                with eng.Fori(0, GROUPS - 1) as j:
                    for n in range(LAG, R + LAG):
                        step(u, k0 + j, n, 0, R + LAG)
                k = k0 + GROUPS - 1
                for n in range(LAG, R + LAG):
                    step(u, k, n, 0, R)
                if behind:
                    behind(k)

        @block.sync
        def _(sp):
            sp.dma_start(gam[:, :], gamma.partition_broadcast(P)).then_inc(gamma_in, 16)
            with sp.Fori(0, B) as u:
                sp.wait_ge(kv_free, u + 1)
                sp.dma_start(k_sb.bitcast(F32)[:, :], kT[:, bass.ds(u * N, N)]).then_inc(k_in, 16)
                for half in range(2):
                    sp.dma_start(v_sb[:, half * TILES // 2:(half + 1) * TILES // 2, :],
                                 v.rearrange("(t p) d -> p t d", p=P)[
                                     :, bass.ds(u * TILES + half * TILES // 2, TILES // 2), :]).then_inc(v_in, 16)
                with sp.Fori(0, GROUPS) as j:
                    for r in range(R):
                        k = u * GROUPS + j
                        g = R * k + r
                        rows = bass.ds(g * P, P)
                        sp.wait_ge(s_ready, SC * (g + 1))
                        sp.dma_start(q_sb.bitcast(F32)[:, r, :], qT[:, rows]).then_inc(q_in[r], 16)
                        sp.wait_ge(o_done, g + 1)
                        sp.dma_start(x_sb[:, r, :], x[rows, :]).then_inc(q_in[r], 16)

        @block.gpsimd
        def _(pool):
            pool.sem_inc(o_free, 2)
            with pool.Fori(0, B * TILES // 2) as k:
                for par in range(2):
                    pool.wait_ge(o_done, R + 2 * k + par + 1)
                    pool.dma_start(out[bass.ds((2 * k + par) * P, P), :], o_sb[:, par, :]).then_inc(stored, 16)
                    pool.wait_ge(stored, 16 * (2 * k + par + 1))
                    pool.sem_inc(o_free, 1)

        @block.tensor
        def _(pe):
            pe.sem_inc(s_ready, R * SC)
            pe.sem_inc(t_ready, R * TC)
            pe.sem_inc(pv_done, TB)
            pe.sem_inc(kv_free, 1)

            def body(u, new, mid, old):
                def make_scores(c):
                    if not new:
                        return
                    k, r = new
                    if c == 0:
                        pe.wait_ge(k_in, 16 * (u + 1))
                        pe.wait_ge(q_in[r], TILE_IN * (k + 1))
                    pe.wait_ge(s_copied, SC * (R * k + r) + c + 1)
                    for w in range(0, W, BANK):
                        at = slice(c * W + w, c * W + w + BANK)
                        mm = pe.matmul(s_ps[:, c % 2, w:w + BANK], q_sb[:, r, :], k_sb[:, at],
                                       start=True, stop=True)
                    mm.then_inc(s_ready, 1)

                def turn(c):
                    k, r = old
                    pe.wait_ge(*copied(R * k + r + (c >= 2), (c - 2) % TC))
                    if c % 2 == 0:
                        pe.wait_ge(p_ready, SC * (R * k + r) + c // 2 + 1)
                    for j in range(KT):
                        at = c * BANK + j * P
                        mm = pe.transpose(t_ps[:, c % 2, j * P:(j + 1) * P], s_sb[:, r, at:at + P], ident[:, :])
                    mm.then_inc(t_ready, 1)

                def times_v(c):
                    k, r = old
                    pe.wait_ge(*copied(R * k + r + 1, c))
                    for j in range(KT):
                        mm = pe.matmul(o_ps[:, r % 2, 0:D], t_sb[:, c % TB, j * P:(j + 1) * P],
                                       v_sb[:, c * KT + j, :], start=(c == 0 and j == 0),
                                       stop=(c == TC - 1 and j == KT - 1))
                    mm.then_inc(pv_done, 1)

                make_scores(0)
                if old:
                    k, r = old
                    pe.wait_ge(v_in, 32 * (u + 1))
                    pe.wait_ge(o_done, R * k + r + R - 1)
                for c in range(TC):
                    if c in (2, 4):
                        make_scores(c // 2)
                    if old:
                        turn(c)
                        if c >= 2:
                            times_v(c - 2)
                make_scores(SC - 1)
                if old:
                    times_v(TC - 2)
                    times_v(TC - 1)

            def behind(k):
                pe.wait_ge(pv_done, TB + TC * R * (k + 1))
                pe.sem_inc(kv_free, 1)

            tiles(pe, body, behind)

        @block.vector
        def _(dve):
            dve.sem_inc(s_copied, 2)
            dve.sem_inc(by_vector, TC - len(BY_SCALAR))
            dve.sem_inc(o_done, R)
            dve.wait_ge(gamma_in, 16)

            def body(u, new, mid, old):
                def take_scores(c):
                    if not new:
                        return
                    k, r = new
                    g = R * k + r
                    at = slice(c * W, (c + 1) * W)
                    if c == 0:
                        dve.wait_ge(t_ready, TC * (g + 1))
                    dve.wait_ge(s_ready, R * SC + SC * g + c + 1)
                    dve.tensor_scalar(s_sb[:, r, at], s_ps[:, c % 2, :], 0.0, None, ALU.add, ALU.max,
                                      accum_out=part[:, r, c:c + 1]).then_inc(s_copied, 1)

                def extreme():
                    if not new:
                        return
                    k, r = new
                    g = R * k + r
                    dve.wait_ge(s_copied, 2 + SC * (g + 1))
                    dve.tensor_reduce(shift[:, r:r + 1], part[:, r, :], AX.X, ALU.max,
                                      negate=True).then_inc(m_ready, 1)

                def take_turned(c):
                    k, r = old
                    i = TC * (R * k + r) + c
                    dve.wait_ge(t_ready, R * TC + i + 1)
                    dve.wait_ge(pv_done, i + 1)
                    dve.tensor_copy(t_sb[:, c % TB, :], t_ps[:, c % 2, :]).then_inc(by_vector, 1)

                def finish_tile():
                    k, r = old
                    g = R * k + r
                    n = 3 * g
                    dve.wait_ge(p_ready, SC * (g + 1))
                    dve.tensor_reduce(total[:, r:r + 1], sums[:, r, :], AX.X, ALU.add).then_inc(rc_ready, 1)
                    dve.wait_ge(rc_ready, n + 1)
                    dve.reciprocal(recip[:, r:r + 1], total[:, r:r + 1]).then_inc(rc_ready, 1)
                    dve.wait_ge(rc_ready, n + 2)
                    dve.wait_ge(o_free, g + 1)
                    dve.tensor_tensor(scale[:, r:r + 1], recip[:, r:r + 1], gam[:, :], ALU.mult).then_inc(rc_ready, 1)
                    dve.wait_ge(rc_ready, n + 3)
                    dve.wait_ge(q_in[r], TILE_IN * (k + 1))
                    dve.wait_ge(pv_done, TB + TC * (g + 1))
                    dve.scalar_tensor_tensor(o_sb[:, r % 2, :], o_ps[:, r % 2, 0:D], scale[:, r:r + 1],
                                             x_sb[:, r, :], ALU.mult, ALU.add).then_inc(o_done, 1)

                take_scores(0)
                for c in range(TC):
                    if c in (2, 4):
                        take_scores(c // 2)
                    if old and c not in BY_SCALAR:
                        take_turned(c)
                take_scores(SC - 1)
                extreme()
                if old:
                    finish_tile()

            tiles(dve, body)

        @block.scalar
        def _(act):
            act.sem_inc(by_scalar, len(BY_SCALAR))

            def body(u, new, mid, old):
                def piece(c):
                    return slice(c * W, (c + 1) * W)

                def take_turned(c):
                    k, r = old
                    i = TC * (R * k + r) + c
                    act.wait_ge(t_ready, R * TC + i + 1)
                    act.wait_ge(pv_done, i + 1)
                    act.copy(t_sb[:, c % TB, :], t_ps[:, c % 2, :]).then_inc(by_scalar, 1)

                def exponentiate(c):
                    k, r = mid
                    act.activation(s_sb[:, r, piece(c)], s_sb[:, r, piece(c)], ACT.Exp,
                                   bias=shift[:, r:r + 1],
                                   accum_out=sums[:, r, c:c + 1]).then_inc(p_ready, 1)

                if mid:
                    k, r = mid
                    g = R * k + r
                    act.wait_ge(m_ready, g + 1)
                    act.wait_ge(o_done, g + 1)
                for c in range(TC):
                    if mid and c % 2 == 0:
                        exponentiate(c // 2)
                    if old and c in BY_SCALAR:
                        take_turned(c)

            tiles(act, body)


def attend1(nc, stage, heads, qT, kT, v, kind, ident, out, scores=None, norms=None, norm_rows=None):
    R = 4
    LAG = 2
    GROUPS = PAIRS // R
    QW = 2 * P
    W = 1024
    SC = N // W
    PIECES = 2 * SC
    KT = BANK // QW
    UNITS = TILES // KT
    dot, l2, l1 = kind == "dot", kind == "l2", kind == "l1"
    TB = 2 if l2 else 4
    with ExitStack() as ctx:
        a = Place(nc, ctx, stage)
        s_sb = a.sb("s", [P, R, 2, N])
        t_sb = a.sb("t", [P, TB, 2, BANK], F32R)
        v_sb = a.sb("v", [P, TILES, 2 * E], F32R)
        part = a.sb("part", [P, R, 2, SC])
        shift = a.sb("shift", [P, R, 2])
        sums = a.sb("sums", [P, R, 2, SC])
        total = a.sb("total", [P, R, 2])
        recip = a.sb("recip", [P, R, 2])
        oT_sb = a.sb("oT", [P, QW])
        o_sb = a.sb("o", [P, 2, 2, E])
        if not l1:
            k_sb = [a.sb(f"k{n}", [P, N], F32R) for n in range(len(kT))]
            q_sb = a.sb("q", [P, 2, QW], F32R)
            s_ps = a.ps("s_ps", [P, 2, W])
        if l2:
            ones = a.sb("ones", [2, P], F32R)
            kn_sb = a.sb("kn", [2, N], F32R)
            qn_sb = a.sb("qn", [P, R, 2, 2])
            root = a.sb("root", [P, R, 2])
        t_ps = a.ps("t_ps", [P, 2, BANK])
        o_ps = a.ps("o_ps", [P, 2, BANK])
        O_AT = QW
        v_in = a.pair("v_in")
        q_in = [a.sem(f"q_in{r}") for r in range(R if l1 else 2)]
        if not l1:
            k_in = a.pair("k_in")
            s_ready = a.sem("s_ready")
            s_copied = a.sem("s_copied")
        else:
            e_ready = a.sem("e_ready")
        m_ready = a.sem("m_ready")
        if l2:
            r_ready = a.sem("r_ready")
            ones_ready = a.sem("ones_ready")
        p_ready = a.sem("p_ready")
        t_ready = a.sem("t_ready")
        high_ready = a.sem("high_ready")
        low_ready = a.sem("low_ready")
        pv_done = a.sem("pv_done")
        o_turned = a.sem("o_turned")
        steps = a.sem("steps")
        o_done = a.sem("o_done")
        stored = a.sem("stored")
        o_free = a.sem("o_free")
        PAIR_IN = 16 * (2 if l2 else 1)
        K_IN = 16 * (len(kT) + (1 if l2 else 0))
        CHUNKS = SC
        TV = TILES // CHUNKS
        FIRST = 1 if l2 else 0
        block = ctx.enter_context(nc.Block())

        def q_read(k, r):
            if l1:
                return q_in[r], 16 * (k + 1)
            return q_in[r % 2], PAIR_IN * (2 * k + r // 2 + 1)

        def chunk_in(sems, each, head, c):
            return sems[c % 2], each * (CHUNKS // 2 * head + c // 2 + 1)

        def pairs(eng, body):
            def step(k, n, end):
                body(*((k + m // R, m % R) if 0 <= m < end else None
                       for m in (n, n - 1, n - LAG, n - LAG - 1)))

            for n in range(LAG + 1):
                step(0, n, R)
            with eng.Fori(0, heads * GROUPS - 1) as k:
                for n in range(LAG + 1, R + LAG + 1):
                    step(k, n, R + LAG + 1)
            for n in range(LAG + 1, R + LAG + 1):
                step(heads * GROUPS - 1, n, R)

        @block.sync
        def _(sp):
            def load_pair(k, r):
                g = R * k + r
                tiles = bass.ds(2 * g, 2)
                if l1:
                    sp.wait_ge(t_ready, UNITS * (g + 1))
                    sp.dma_start(s_sb[:, r, :, :], scores.rearrange("(t p) n -> p t n", p=P)[:, tiles, :]
                                 ).then_inc(q_in[r], 16)
                else:
                    sp.wait_ge(s_ready, PIECES * (g + 1))
                    if l2:
                        sp.dma_start(qn_sb[:, r, :, :], norms.rearrange("(t p) c -> p t c", p=P)[:, tiles, :]
                                     ).then_inc(q_in[r % 2], 16)
                    sp.dma_start(q_sb.bitcast(F32)[:, r % 2, :], qT[:, bass.ds(g * QW, QW)]
                                 ).then_inc(q_in[r % 2], 16)

            def load_k(u, c):
                if c < 2:
                    sp.wait_ge(s_ready, PIECES * (PAIRS * u + 1) + 2 * (c + 1))
                else:
                    sp.wait_ge(s_ready, PIECES * (PAIRS * u + 2) + 2 * (c - 1))
                for sb, dram in zip(k_sb, kT):
                    sp.dma_start(sb.bitcast(F32)[:, c * W:(c + 1) * W], dram[:, bass.ds(u * N + c * W, W)]
                                 ).then_inc(k_in[c % 2], 16)
                if l2:
                    sp.dma_start(kn_sb.bitcast(F32)[:, c * W:(c + 1) * W], norm_rows[:, bass.ds(u * N + c * W, W)]
                                 ).then_inc(k_in[c % 2], 16)

            with sp.Fori(0, heads) as u:
                for r in range(R):
                    load_pair(u * GROUPS, r)
                    if r == 0 and not l1:
                        for c in range(CHUNKS):
                            load_k(u, c)
                with sp.Fori(1, GROUPS) as j:
                    for r in range(R):
                        load_pair(u * GROUPS + j, r)

        @block.gpsimd
        def _(pool):
            pool.sem_inc(o_free, 2)
            out_tiles = out.rearrange("(t p) d -> p t d", p=P)
            v_tiles = v.rearrange("(t p) d -> p t d", p=P)

            def load_v(u, c):
                pool.dma_start(v_sb.bitcast(F32)[:, c * TV:(c + 1) * TV, :],
                               v_tiles[:, bass.ds(u * TILES + c * TV, TV), :]).then_inc(v_in[c % 2], 16)

            def store(g, par):
                pool.wait_ge(o_done, R + g + 1)
                pool.dma_start(out_tiles[:, bass.ds(2 * g, 2), :], o_sb[:, par, :, :]).then_inc(stored, 16)
                pool.wait_ge(stored, 16 * (g + 1))
                pool.sem_inc(o_free, 1)

            def store_head(u, next_v):
                with pool.Fori(0, PAIRS // 2 - 1) as k:
                    for par in range(2):
                        store(u * PAIRS + 2 * k + par, par)
                store(u * PAIRS + PAIRS - 2, 0)
                if next_v:
                    for c in range(CHUNKS):
                        pool.wait_ge(pv_done, TB + UNITS * (PAIRS * (u + 1) - 1) + UNITS // CHUNKS * (c + 1))
                        if c >= 2:
                            pool.wait_ge(*chunk_in(v_in, 16, u + 1, c - 2))
                        load_v(u + 1, c)
                store(u * PAIRS + PAIRS - 1, 1)

            for c in range(CHUNKS):
                if c >= 2:
                    pool.wait_ge(*chunk_in(v_in, 16, 0, c - 2))
                load_v(0, c)
            with pool.Fori(0, heads - 1) as u:
                store_head(u, True)
            store_head(heads - 1, False)

        @block.tensor
        def _(pe):
            if not l1:
                pe.sem_inc(s_ready, 2 * PIECES)
            pe.sem_inc(t_ready, R * UNITS)
            pe.sem_inc(pv_done, TB)
            if l2:
                pe.wait_ge(ones_ready, 1)

            def body(new, mid, old, last):
                def make_scores(piece):
                    if not new or l1:
                        return
                    k, r = new
                    c, t = piece // 2, piece % 2
                    if piece == 0:
                        pe.wait_ge(*q_read(k, r))
                    if t == 0:
                        pe.wait_ge(*chunk_in(k_in, K_IN, k // GROUPS, c))
                    pe.wait_ge(s_copied, PIECES * (R * k + r) + piece + 1)
                    query = q_sb[:, r % 2, t * P:(t + 1) * P]
                    for w in range(0, W, BANK):
                        at = slice(c * W + w, c * W + w + BANK)
                        for n, sb in enumerate(k_sb):
                            mm = pe.matmul(s_ps[:, t, w:w + BANK], query, sb[:, at],
                                           start=n == 0, stop=not l2 and n == len(k_sb) - 1)
                        if l2:
                            mm = pe.matmul(s_ps[:, t, w:w + BANK], ones[:, :], kn_sb[:, at],
                                           start=False, stop=True)
                    mm.then_inc(s_ready, 1)

                def turn(c):
                    k, r = old
                    g = R * k + r
                    if c * KT * P % W == 0:
                        pe.wait_ge(p_ready, PIECES * g + 2 * (c * KT * P // W + 1))
                    pe.wait_ge(low_ready, UNITS * g + c + 1)
                    for j in range(KT):
                        for t in range(2):
                            at = (c * KT + j) * P
                            mm = pe.transpose(t_ps[:, c % 2, j * QW + t * P:j * QW + (t + 1) * P],
                                              s_sb[:, r, t, at:at + P], ident[:, :])
                    mm.then_inc(t_ready, 1)

                def times_v(c):
                    k, r = old
                    g = R * k + r
                    if c == 0:
                        pe.wait_ge(o_done, R + g - 1)
                    if c * KT % TV == 0:
                        pe.wait_ge(*chunk_in(v_in, 16, k // GROUPS, c * KT // TV))
                    pe.wait_ge(low_ready, 2 + UNITS * g + c + 1)
                    for j in range(KT):
                        for which in range(2):
                            mm = pe.matmul(o_ps[:, r % 2, 0:QW], v_sb[:, c * KT + j, :],
                                           t_sb[:, c % TB, which, j * QW:(j + 1) * QW],
                                           start=(c == 0 and j == 0 and which == 0),
                                           stop=(c == UNITS - 1 and j == KT - 1 and which == 1))
                    mm.then_inc(pv_done, 1)

                def turn_back():
                    k, r = last
                    pe.wait_ge(steps, FIRST + 3 * (R * k + r) + 1)
                    for t in range(2):
                        for half in range(2):
                            mm = pe.matmul(o_ps[:, r % 2, O_AT + t * E:O_AT + (t + 1) * E],
                                           oT_sb[:, t * P:(t + 1) * P], ident[:, half * E:(half + 1) * E],
                                           start=half == 0, stop=half == 1)
                    mm.then_inc(o_turned, 1)

                for c in range(UNITS):
                    if old:
                        turn(c)
                    if old and c >= 2:
                        times_v(c - 2)
                    if c % 2 == 0:
                        make_scores(c // 2)
                    if last and c == 3:
                        turn_back()
                if old:
                    times_v(UNITS - 2)
                    times_v(UNITS - 1)

            pairs(pe, body)

        @block.vector
        def _(dve):
            if not l1:
                dve.sem_inc(s_copied, 2)
            dve.sem_inc(low_ready, 2)
            dve.sem_inc(o_done, R)
            if l2:
                dve.memset(part[:, :, :, :], 1.0).then_inc(steps, 1)
                dve.wait_ge(steps, 1)
                dve.tensor_copy(ones[:, :], part[0:2, 0, 0, 0:1].broadcast_to([2, P])).then_inc(ones_ready, 1)
                dve.wait_ge(ones_ready, 1)

            def body(new, mid, old, last):
                def take_scores(piece):
                    k, r = new
                    g = R * k + r
                    c, t = piece // 2, piece % 2
                    at = slice(c * W, (c + 1) * W)
                    if piece == 0:
                        dve.wait_ge(t_ready, UNITS * (g + 1))
                        if l1 or l2:
                            dve.wait_ge(*q_read(k, r))
                    if l1:
                        dve.tensor_reduce(part[:, r, t, c:c + 1], s_sb[:, r, t, at], AX.X, ALU.min).then_inc(e_ready, 1)
                        return
                    dve.wait_ge(s_ready, 2 * PIECES + PIECES * g + piece + 1)
                    dve.tensor_scalar(s_sb[:, r, t, at], s_ps[:, t, :], qn_sb[:, r, t, 1:2] if l2 else 0.0, None,
                                      ALU.max if l2 else ALU.add, ALU.min if l2 else ALU.max,
                                      accum_out=part[:, r, t, c:c + 1]).then_inc(s_copied, 1)

                def extremes():
                    k, r = new
                    n = PIECES * (R * k + r + 1)
                    if l1:
                        dve.wait_ge(e_ready, n)
                    else:
                        dve.wait_ge(s_copied, 2 + n)
                    dve.tensor_reduce(shift[:, r, :], part[:, r, :, :], AX.X, ALU.max if dot else ALU.min,
                                      negate=dot).then_inc(m_ready, 1)

                def make_low(c):
                    k, r = old
                    dve.wait_ge(high_ready, UNITS * (R * k + r) + c + 1)
                    dve.tensor_tensor(t_sb[:, c % TB, 1, :], t_ps[:, c % 2, :], t_sb.bitcast(F32)[:, c % TB, 0, :],
                                      ALU.subtract).then_inc(low_ready, 1)

                def take_output():
                    k, r = last
                    g = R * k + r
                    dve.wait_ge(pv_done, TB + UNITS * (g + 1))
                    dve.wait_ge(o_done, R + g)
                    dve.tensor_copy(oT_sb[:, :], o_ps[:, r % 2, 0:QW]).then_inc(steps, 1)
                    dve.wait_ge(p_ready, PIECES * (g + 1))
                    dve.tensor_reduce(total[:, r, :], sums[:, r, :, :], AX.X, ALU.add).then_inc(steps, 1)
                    dve.wait_ge(steps, FIRST + 3 * g + 2)
                    dve.reciprocal(recip[:, r, :], total[:, r, :]).then_inc(steps, 1)

                def finish():
                    k, r = last
                    g = R * k + r
                    dve.wait_ge(steps, FIRST + 3 * g + 3)
                    dve.wait_ge(o_free, g + 1)
                    dve.wait_ge(o_turned, g + 1)
                    dve.tensor_tensor(o_sb[:, r % 2, :, :], o_ps[:, r % 2, O_AT:O_AT + 2 * E],
                                      recip[:, r, :].unsqueeze(2).broadcast_to([P, 2, E]), ALU.mult
                                      ).then_inc(o_done, 1)

                for c in range(UNITS):
                    if old:
                        make_low(c)
                    if new and c % 2:
                        take_scores(c // 2)
                    if last and c == 1:
                        take_output()
                    if last and c == 5:
                        finish()
                if new:
                    extremes()

            pairs(dve, body)

        @block.scalar
        def _(act):
            def body(new, mid, old, last):
                def piece_of(m):
                    return m % 2, slice(m // 2 * W, (m // 2 + 1) * W)

                def make_high(c):
                    k, r = old
                    i = UNITS * (R * k + r) + c
                    act.wait_ge(t_ready, R * UNITS + i + 1)
                    act.wait_ge(pv_done, i + 1)
                    act.copy(t_sb[:, c % TB, 0, :], t_ps[:, c % 2, :]).then_inc(high_ready, 1)

                def exponentiate(m):
                    k, r = mid
                    t, at = piece_of(m)
                    act.activation(s_sb[:, r, t, at], s_sb[:, r, t, at], ACT.Exp,
                                   bias=(root if l2 else shift)[:, r, t:t + 1], scale=1.0 if dot else -1.0,
                                   accum_out=sums[:, r, t, m // 2:m // 2 + 1]).then_inc(p_ready, 1)

                def take_root(m):
                    k, r = mid
                    t, at = piece_of(m)
                    act.activation(s_sb[:, r, t, at], s_sb[:, r, t, at], ACT.Sqrt,
                                   bias=qn_sb[:, r, t, 0:1]).then_inc(r_ready, 1)

                if mid:
                    k, r = mid
                    g = R * k + r
                    act.wait_ge(m_ready, g + 1)
                    act.wait_ge(o_done, g + 1)
                    if l2:
                        for t in range(2):
                            act.activation(root[:, r, t:t + 1], shift[:, r, t:t + 1], ACT.Sqrt,
                                           bias=qn_sb[:, r, t, 0:1]).then_inc(r_ready, 1)
                for c in range(UNITS):
                    if old:
                        make_high(c)
                    if mid and l2:
                        if c < PIECES:
                            take_root(c)
                        else:
                            act.wait_ge(r_ready, (PIECES + 2) * g + 2 + c - PIECES + 1)
                            exponentiate(c - PIECES)
                    elif mid and c % 2:
                        exponentiate(c // 2)

            pairs(act, body)


def project1(nc, t1, wqkv, bqkv, share, ident, parts, rows2, ks, v):
    HE = H * E
    MT = TOKENS // P
    PAIRS1 = MT // 2
    with ExitStack() as ctx:
        a = Place(nc, ctx, "project1")
        w_sb = a.sb("w", [P, DC, 3 * HE])
        b_sb = a.sb("b", [P, 3 * HE])
        share_sb = a.sb("share", [P, E])
        eps = a.sb("eps", [P, 1])
        x_sb = a.sb("x", [P, 2, D])
        stats = a.sb("stats", [P, 2, 6])
        mean_var = a.sb("mean_var", [P, 2, 2])
        std = a.sb("std", [P, 2, 1])
        rstd = a.sb("rstd", [P, 2, 1])
        n_sb = a.sb("n", [P, 2, D])
        nT_sb = a.sb("nT", [P, 2, DC, P])
        raw = a.sb("raw", [P, 2, 2, H, E])
        square = a.sb("square", [P, 2, 2, 2, E])
        norm2 = a.sb("norm2", [P, 2, 4])
        norm = a.sb("norm", [P, 2, 4])
        rnorm = a.sb("rnorm", [P, 2, 4])
        forms = a.sb("forms", [P, 2, 2, PH, E])
        split = a.sb("split", [P, 2, 3 * PH, 2, E], F32R)
        last = a.sb("last", [P, 2, E + 2])
        junk = a.sb("junk", [P, 2, E])
        ks_sb = a.sb("ks", [P, 2, KS])
        v_full = a.sb("v_full", [P, 2, H, E])
        v_sb = a.sb("v", [P, 2, H, 2, E], F32R)
        sT_sb = a.sb("sT", [P, 2, 3 * PH, P], F32R)
        lT_sb = a.sb("lT", [E + 2, 2, P])
        nT_ps = a.ps("nT_ps", [P, 2, D])
        p_ps = a.ps("p_ps", [P, 2, 2 * BANK])
        sT_ps = a.ps("sT_ps", [P, 3 * BANK])
        LAST = 3 * PH * P
        const_in = a.sem("const_in")
        preset = a.sem("preset")
        x_in = a.pair("x_in")
        stats_ready = a.sem("stats_ready")
        std_ready = a.sem("std_ready")
        rstd_ready = a.sem("rstd_ready")
        n_ready = a.sem("n_ready")
        nT_ready = a.sem("nT_ready")
        nT_copied = a.sem("nT_copied")
        p_ready = a.sem("p_ready")
        raw_ready = a.sem("raw_ready")
        norm2_ready = a.sem("norm2_ready")
        norm_ready = a.sem("norm_ready")
        rnorm_ready = a.sem("rnorm_ready")
        forms_ready = a.sem("forms_ready")
        high_ready = a.sem("high_ready")
        split_ready = a.sem("split_ready")
        sT_ready = a.sem("sT_ready")
        sT_copied = a.sem("sT_copied")
        stored = a.sem("stored")
        parts_free = a.sem("parts_free")
        kv_free = a.sem("kv_free")
        CONST = 16 * 3
        part_blocks = parts.rearrange("e (k n) -> e k n", k=3 * PH)
        v_rows = v.rearrange("(h n) e -> n h e", h=H)
        Q, K = 0, 1
        block = ctx.enter_context(nc.Block())

        def pipelined(eng, early, late):
            early(0)
            with eng.Fori(0, PAIRS1 - 1) as k:
                early(k + 1)
                late(k)
            late(PAIRS1 - 1)

        @block.sync
        def _(sp):
            sp.dma_start(w_sb[:, :, :], wqkv.rearrange("(c p) m -> p c m", p=P)).then_inc(const_in, 16)
            sp.dma_start(b_sb[:, :], bqkv.partition_broadcast(P)).then_inc(const_in, 16)
            sp.dma_start(share_sb[:, :], share.partition_broadcast(P)).then_inc(const_in, 16)
            with sp.Fori(0, PAIRS1) as k:
                for par in range(2):
                    g = 2 * k + par
                    sp.wait_ge(n_ready, g + 1)
                    sp.dma_start(x_sb[:, par, :], t1[bass.ds(g * P, P), :]).then_inc(x_in[par], 16)

        @block.gpsimd
        def _(pool):
            pool.sem_inc(kv_free, 1)

            def store(k, after_first):
                def tile(par):
                    return bass.ds((2 * k + par) * P, P)

                if after_first:
                    pool.wait_ge(stored, 16 * 8 * k)
                pool.sem_inc(parts_free, 1)
                for par in range(2):
                    pool.wait_ge(split_ready, 2 + 2 * k + par + 1)
                    pool.dma_start(ks[tile(par), :], ks_sb[:, par, :]).then_inc(stored, 16)
                    pool.dma_start(v_rows[tile(par), :, :], v_sb.bitcast(F32)[:, par, :, :, :]).then_inc(stored, 16)
                pool.wait_ge(stored, 16 * (8 * k + 4))
                pool.sem_inc(kv_free, 1)
                for par in range(2):
                    pool.wait_ge(sT_copied, 1 + 2 * k + par + 1)
                    pool.dma_start(part_blocks[:, :, tile(par)], sT_sb.bitcast(F32)[:, par, :, :]).then_inc(stored, 16)
                    pool.dma_start(rows2[:, tile(par)], lT_sb[:, par, :]).then_inc(stored, 16)

            store(0, False)
            with pool.Fori(0, PAIRS1 - 1) as k:
                store(k + 1, True)
            pool.wait_ge(stored, 16 * 8 * PAIRS1)

        @block.tensor
        def _(pe):
            pe.sem_inc(sT_ready, 2)
            pe.sem_inc(p_ready, 2)
            pe.wait_ge(const_in, CONST)

            def project(k):
                for par in range(2):
                    g = 2 * k + par
                    pe.wait_ge(n_ready, 2 + g + 1)
                    if par == 0:
                        pe.wait_ge(nT_copied, k + 1)
                    for c in range(DC):
                        mm = pe.transpose(nT_ps[:, par, c * P:(c + 1) * P], n_sb[:, par, c * P:(c + 1) * P],
                                          ident[:, :])
                mm.then_inc(nT_ready, 1)
                for par in range(2):
                    g = 2 * k + par
                    if par == 0:
                        pe.wait_ge(nT_copied, 1 + k + 1)
                    pe.wait_ge(raw_ready, g + 1)
                    for at, n in ((0, BANK), (BANK, 3 * HE - BANK)):
                        for c in range(DC):
                            mm = pe.matmul(p_ps[:, par, at:at + n], nT_sb[:, par, c, :], w_sb[:, c, at:at + n],
                                           start=c == 0, stop=c == DC - 1)
                    mm.then_inc(p_ready, 1)

            def turn(k):
                for par in range(2):
                    g = 2 * k + par
                    pe.wait_ge(split_ready, 2 + g + 1)
                    pe.wait_ge(sT_copied, g + 1)
                    for m in range(3 * PH):
                        pe.transpose(sT_ps[:, m * P:(m + 1) * P], split.bitcast(F32)[:, par, m, :, :], ident[:, :])
                    pe.transpose(sT_ps[0:E + 2, LAST:LAST + P], last[:, par, :], ident[:, :]).then_inc(sT_ready, 1)

            pipelined(pe, project, turn)

        @block.scalar
        def _(act):
            act.sem_inc(nT_copied, 1)
            act.sem_inc(sT_copied, 1)
            act.wait_ge(preset, 1)

            def early(k):
                for par in range(2):
                    g = 2 * k + par
                    act.wait_ge(stats_ready, 4 * k + 2 + par + 1)
                    act.activation(std[:, par, :], mean_var[:, par, 1:2], ACT.Sqrt, bias=eps[:, :]).then_inc(std_ready, 1)
                act.wait_ge(nT_ready, k + 1)
                act.wait_ge(p_ready, 2 + 2 * k)
                act.copy(nT_sb[:, :, :, :], nT_ps[:, :, :]).then_inc(nT_copied, 1)

            def late(k):
                for par in range(2):
                    g = 2 * k + par
                    act.wait_ge(norm2_ready, 2 * (g + 1))
                    act.activation(norm[:, par, :], norm2[:, par, :], ACT.Sqrt).then_inc(norm_ready, 1)
                for par in range(2):
                    g = 2 * k + par
                    act.wait_ge(sT_ready, g + 1)
                    act.wait_ge(forms_ready, g + 1)
                    act.copy(split[:, par, 0:PH, 0, :], forms[:, par, Q, :, :])
                    if par == 0:
                        act.wait_ge(kv_free, k + 1)
                    act.copy(v_sb[:, par, :, 0, :], v_full[:, par, :, :])
                    act.copy(split[:, par, PH:2 * PH, :, :],
                             forms[:, par, K, :, :].unsqueeze(2).broadcast_to([P, PH, 2, E])).then_inc(high_ready, 1)
                for par in range(2):
                    g = 2 * k + par
                    act.wait_ge(sT_ready, 2 + g + 1)
                    if par == 0:
                        act.wait_ge(parts_free, k + 1)
                    act.copy(sT_sb[:, par, :, :], sT_ps[:, 0:LAST])
                    act.copy(lT_sb[:, par, :], sT_ps[0:E + 2, LAST:LAST + P]).then_inc(sT_copied, 1)

            pipelined(act, early, late)

        @block.vector
        def _(dve):
            dve.sem_inc(n_ready, 2)
            dve.sem_inc(raw_ready, 2)
            dve.sem_inc(split_ready, 2)
            dve.memset(eps[:, :], LN_EPS)
            dve.memset(ks_sb[:, :, :], 0.0).then_inc(preset, 1)
            dve.wait_ge(preset, 1)
            dve.wait_ge(const_in, CONST)

            def early(k):
                for par in range(2):
                    dve.wait_ge(x_in[par], 16 * (k + 1))
                    dve.bn_stats(stats[:, par, :], x_sb[:, par, :]).then_inc(stats_ready, 1)
                dve.wait_ge(stats_ready, 4 * k + 2)
                dve.memset(junk[:, 0, 0:1], 0.0)
                for par in range(2):
                    dve.bn_aggr(mean_var[:, par, :], stats[:, par, :]).then_inc(stats_ready, 1)

            def normalise(k):
                for par in range(2):
                    dve.wait_ge(std_ready, 2 * k + par + 1)
                    dve.reciprocal(rstd[:, par, :], std[:, par, :]).then_inc(rstd_ready, 1)
                for par in range(2):
                    g = 2 * k + par
                    dve.wait_ge(rstd_ready, g + 1)
                    dve.wait_ge(nT_copied, k + 1)
                    dve.tensor_scalar(n_sb[:, par, :], x_sb[:, par, :], mean_var[:, par, 0:1], rstd[:, par, :],
                                      ALU.subtract, ALU.mult).then_inc(n_ready, 1)

            def take_products(k):
                for par in range(2):
                    g = 2 * k + par
                    dve.wait_ge(p_ready, 2 + g + 1)
                    dve.wait_ge(split_ready, g + 1)
                    dve.tensor_tensor(v_full[:, par, :, :], p_ps[:, par, 2 * HE:3 * HE], b_sb[:, 2 * HE:3 * HE],
                                      ALU.add)
                    dve.tensor_tensor(raw[:, par, :, :, :], p_ps[:, par, 0:2 * HE], b_sb[:, 0:2 * HE],
                                      ALU.add).then_inc(raw_ready, 1)

            def square_sums(k):
                for par in range(2):
                    g = 2 * k + par
                    normed = raw[:, par, :, COS:L2 + 1:L2 - COS, :]
                    dve.wait_ge(raw_ready, 2 + g + 1)
                    dve.tensor_tensor(square[:, par, :, :, :], normed, normed, ALU.mult).then_inc(norm2_ready, 1)
                    dve.wait_ge(norm2_ready, 2 * g + 1)
                    dve.tensor_reduce(norm2[:, par, :].rearrange("p (a b) -> p a b", a=2), square[:, par, :, :, :],
                                      AX.X, ALU.add).then_inc(norm2_ready, 1)

            def make_forms(k):
                for par in range(2):
                    g = 2 * k + par
                    q, kk = raw[:, par, Q, :, :], raw[:, par, K, :, :]
                    f = forms[:, par, :, :, :]
                    dve.wait_ge(sT_ready, g + 1)
                    dve.wait_ge(kv_free, k + 1)
                    dve.tensor_scalar(f[:, Q, 0, :], q[:, SDP, :], float(E) ** -0.5, None, ALU.mult)
                    dve.tensor_scalar(f[:, Q, 2, :], q[:, L2, :], -2.0, None, ALU.mult)
                    dve.tensor_copy(f[:, K, 0:PH:2, :], kk[:, SDP:L2 + 1:L2 - SDP, :])
                    dve.tensor_scalar(last[:, par, 0:E], q[:, L1, :], 2.0, None, ALU.mult)
                    dve.tensor_scalar(ks_sb[:, par, 0:E], kk[:, L1, :], 2.0, None, ALU.mult)
                    dve.tensor_scalar(ks_sb[:, par, E:2 * E], kk[:, L1, :], -1.0, None, ALU.mult)
                    dve.tensor_tensor_reduce(junk[:, par, :], kk[:, L1, :], share_sb[:, :], 1.0, 0.0,
                                             ALU.mult, ALU.add, ks_sb[:, par, 2 * E:2 * E + 1])
                    dve.wait_ge(norm2_ready, 2 * (g + 1))
                    dve.tensor_copy(last.bitcast(F32R)[:, par, E:E + 1], norm2[:, par, 3:4])
                    dve.tensor_copy(ks_sb[:, par, NORM_AT:NORM_AT + 1], norm2[:, par, 1:2])
                    dve.tensor_scalar(ks_sb[:, par, NORM_AT + 1:NORM_AT + 2], norm2[:, par, 1:2], -1.0, None, ALU.mult)
                    dve.wait_ge(norm_ready, g + 1)
                    dve.reciprocal(rnorm[:, par, :], norm[:, par, :]).then_inc(rnorm_ready, 1)
                for par in range(2):
                    g = 2 * k + par
                    f = forms[:, par, :, :, :]
                    dve.wait_ge(rnorm_ready, g + 1)
                    dve.tensor_scalar(f[:, Q, 1, :], raw[:, par, Q, COS, :], rnorm[:, par, 0:1], None, ALU.mult)
                    dve.tensor_scalar(f[:, K, 1, :], raw[:, par, K, COS, :], rnorm[:, par, 2:3], None,
                                      ALU.mult).then_inc(forms_ready, 1)

            def split_forms(k):
                for par in range(2):
                    g = 2 * k + par
                    high = split.bitcast(F32)[:, par, :, :, :]
                    dve.wait_ge(rnorm_ready, g + 1)
                    dve.tensor_tensor(last[:, par, E + 1:E + 2], norm2[:, par, 3:4], last[:, par, E:E + 1],
                                      ALU.subtract)
                    dve.wait_ge(high_ready, g + 1)
                    dve.tensor_tensor(v_sb[:, par, :, 1, :], v_full[:, par, :, :], v_sb.bitcast(F32)[:, par, :, 0, :],
                                      ALU.subtract)
                    dve.tensor_tensor(split[:, par, 0:PH, 1, :], forms[:, par, Q, :, :], high[:, 0:PH, 0, :],
                                      ALU.subtract)
                    dve.tensor_tensor(split[:, par, 2 * PH:3 * PH, :, :],
                                      forms[:, par, K, :, :].unsqueeze(2).broadcast_to([P, PH, 2, E]),
                                      high[:, PH:2 * PH, :, :], ALU.subtract).then_inc(split_ready, 1)

            early(0)
            normalise(0)
            with dve.Fori(0, PAIRS1 - 1) as k:
                early(k + 1)
                take_products(k)
                normalise(k + 1)
                square_sums(k)
                make_forms(k)
                split_forms(k)
            take_products(PAIRS1 - 1)
            square_sums(PAIRS1 - 1)
            make_forms(PAIRS1 - 1)
            split_forms(PAIRS1 - 1)


def distances(nc, rows2, ks, ident, out):
    QW = 2 * BANK
    QT = QW // P
    KT = 2
    STEPS = N // (KT * P)
    HELD = TOKENS // QW
    TURN = 4
    n_abs = len(SCALAR_E) * KT
    n_max = len(MAX_E) * KT
    n_acc = len(SUM_E) * KT
    with ExitStack() as ctx:
        a = Place(nc, ctx, "distances")
        q_sb = a.sb("q", [P, HALF_E, QW])
        ks_sb = a.sb("ks", [P, 2, KT, KS])
        acc = a.sb("acc", [P, 2, KT, QW])
        diff = a.sb("diff", [P, TURN, QW])
        larger = a.sb("larger", [P, TURN, QW])
        d_sb = a.sb("d", [P, 2, QT, KT * P])
        d_ps = a.ps("d_ps", [P, 2, KT, QW])
        q_in = [a.sem(f"q_in{i}") for i in range(4)]
        ks_in = a.pair("ks_in")
        acc_done = a.sem("acc_done")
        abs_done = a.sem("abs_done")
        max_done = a.sem("max_done")
        turned = a.sem("turned")
        max_turned = a.sem("max_turned")
        d_ready = a.sem("d_ready")
        d_copied = a.sem("d_copied")
        stored = a.pair("stored")
        back_in = a.pair("back_in")
        FLUSH = 5
        PART = HALF_E // len(q_in)
        LOOP = STEPS // 2
        assert 2 * n_abs % TURN == 0 and 2 * n_max % TURN == 0
        block = ctx.enter_context(nc.Block())

        def steps(eng, body):
            with eng.Fori(0, HELD) as i:
                for half in range(2):
                    with eng.Fori(0, LOOP) as j:
                        for par in range(2):
                            body(2 * i + half, half, (2 * i + half) * LOOP + j, par)

        @block.sync
        def _(sp):
            sp.sem_inc(stored[0], 16)
            sp.sem_inc(stored[1], 32)
            sp.sem_inc(back_in[1], 16)
            ks_tiles = ks.rearrange("(t p) m -> p t m", p=P)
            out_tiles = out.rearrange("(t p) n -> p t n", p=P)

            def load_ks(batch, j, par):
                sp.dma_start(ks_sb[:, par, :, :], ks_tiles[:, bass.ds(batch * TILES + (2 * j + par) * KT, KT), :]
                             ).then_inc(ks_in[par], 16)

            def place(i, j, par):
                return out_tiles[:, bass.ds(i * QT, QT), bass.ds((2 * j + par) * KT * P, KT * P)]

            def turn_over(i, half, j, next_ks, next_half):
                for par in range(2):
                    k = (2 * i + half) * LOOP + j
                    sp.wait_ge(d_copied, 2 + 2 * k + par + 1)
                    if next_ks and next_half == half:
                        load_ks(*next_ks, par)
                    sp.dma_start(place(i, j, par), d_sb[:, par, :, :]).then_inc(stored[par], 16)
                    if next_half == 1:
                        sp.wait_ge(stored[par], 16 * (k + 2 + par))
                    if next_ks and next_half != half:
                        load_ks(*next_ks, par)
                    if next_half == 1:
                        sp.dma_start(d_sb[:, par, :, :], place(i, 0 if half == 0 else j + 1, par)
                                     ).then_inc(back_in[par], 16)

            load_ks(0, 0, 0)
            load_ks(0, 0, 1)

            def held(i, batch, next_batch):
                for half in range(2):
                    with sp.Fori(0, LOOP - 1) as j:
                        turn_over(i, half, j, (batch, j + 1), half)
                    turn_over(i, half, LOOP - 1, (batch, 0) if half == 0 else next_batch, 1 - half)

            for batch in range(B):
                with sp.Fori(0, HELD // B - 1) as i:
                    held(batch * HELD // B + i, batch, (batch, 0))
                held((batch + 1) * HELD // B - 1, batch, (batch + 1, 0) if batch < B - 1 else None)
            sp.wait_ge(stored[0], 16 * (HELD * STEPS + 1))
            sp.wait_ge(stored[1], 16 * (HELD * STEPS + 2))

        @block.gpsimd
        def _(pool):
            with pool.Fori(0, HELD) as i:
                for half in range(2):
                    h = 2 * i + half
                    for part, s in enumerate(q_in):
                        e = part * PART
                        for done, share in ((acc_done, SUM_E), (max_done, MAX_E), (abs_done, SCALAR_E)):
                            pool.wait_ge(done, len(share) * KT * STEPS * h + sum(x < e + PART for x in share) * KT)
                        pool.dma_start(q_sb[:, e:e + PART, :],
                                       rows2[half * HALF_E + e:half * HALF_E + e + PART, bass.ds(i * QW, QW)]
                                       .partition_broadcast(P)).then_inc(s, 16)

        @block.tensor
        def _(pe):
            pe.sem_inc(turned, TURN)
            pe.sem_inc(max_turned, TURN)
            pe.sem_inc(d_ready, 2 * KT)

            def turn(par, j, src, start, stop):
                for t in range(QT):
                    mm = pe.matmul(d_ps[:, par, j, t * P:(t + 1) * P], src[:, t * P:(t + 1) * P], ident[:, :],
                                   is_transpose=True, start=start and t * P % BANK == 0, stop=stop,
                                   skip_group_check=True)
                return mm

            def body(h, half, k, par):
                g = 2 * k + par
                pe.wait_ge(d_copied, g + 1)
                started = [False] * KT
                for is_max, n in merged(n_abs, n_max):
                    j = n % KT
                    if is_max:
                        pe.wait_ge(max_done, n_max + n_max * g + n + 1)
                        turn(par, j, larger[:, (par * n_max + n) % TURN, :], not started[j], False).then_inc(max_turned, 1)
                    else:
                        pe.wait_ge(abs_done, n_abs + n_abs * g + n + 1)
                        turn(par, j, diff[:, (par * n_abs + n) % TURN, :], not started[j], False).then_inc(turned, 1)
                    started[j] = True
                pe.wait_ge(acc_done, n_acc + n_acc * (g + 1))
                for j in range(KT):
                    turn(par, j, acc[:, par, j, :], False, True).then_inc(d_ready, 1)

            steps(pe, body)

        @block.scalar
        def _(act):
            act.sem_inc(abs_done, n_abs)

            def body(h, half, k, par):
                g = 2 * k + par
                act.wait_ge(ks_in[par], 16 * (k + 1))
                n = 0
                for e in SCALAR_E:
                    act.wait_ge(q_in[e // PART], 16 * (h + 1))
                    for j in range(KT):
                        act.wait_ge(turned, n_abs * g + n + 1)
                        minus_k = E + half * HALF_E + e
                        act.activation(diff[:, (par * n_abs + n) % TURN, :], q_sb[:, e, :], ACT.Abs,
                                       bias=ks_sb[:, par, j, minus_k:minus_k + 1], scale=0.5).then_inc(abs_done, 1)
                        n += 1

            steps(act, body)

        @block.vector
        def _(dve):
            dve.sem_inc(max_done, n_max)
            dve.sem_inc(d_copied, 1)
            dve.memset(d_sb[:, 1, :, :], 0.0)
            dve.memset(d_ps[:, 1, :, :], 0.0).then_inc(acc_done, n_acc)
            dve.wait_ge(acc_done, n_acc)

            def take_distances(par, ready, half):
                for j in range(KT):
                    dve.wait_ge(d_ready, ready + j + 1)
                    at = d_sb[:, par, :, j * P:(j + 1) * P]
                    if half == 0:
                        ins = dve.tensor_copy(at, d_ps[:, par, j, :])
                    else:
                        ins = dve.tensor_tensor(at, d_ps[:, par, j, :], at, ALU.add)
                ins.then_inc(d_copied, 1)

            def body(i, half, j, par, half_before):
                h = 2 * i + half
                k = h * LOOP + j
                g = 2 * k + par
                dve.wait_ge(ks_in[par], 16 * (k + 1))
                dve.wait_ge(d_ready, KT * (g + 1))
                for is_max, n in merged(n_acc, n_max):
                    r, t = n // KT, n % KT
                    e = (MAX_E if is_max else SUM_E)[r]
                    q = q_sb[:, e, :]
                    k2 = ks_sb[:, par, t, half * HALF_E + e:half * HALF_E + e + 1]
                    sums = acc[:, par, t, :]
                    if t == 0:
                        dve.wait_ge(q_in[e // PART], 16 * (h + 1))
                    if is_max:
                        dve.wait_ge(max_turned, n_max * g + n + 1)
                        dve.tensor_scalar(larger[:, (par * n_max + n) % TURN, :], q, k2, None, ALU.max).then_inc(max_done, 1)
                    elif r == 0 and half == 0:
                        dve.tensor_scalar(sums, q, k2, ks_sb[:, par, t, 2 * E:2 * E + 1], ALU.max, ALU.subtract
                                          ).then_inc(acc_done, 1)
                    elif r == 0:
                        dve.tensor_scalar(sums, q, k2, None, ALU.max).then_inc(acc_done, 1)
                    else:
                        dve.wait_ge(acc_done, n_acc + n_acc * g + n - KT + 1)
                        dve.scalar_tensor_tensor(sums, q, k2, sums, ALU.max, ALU.add).then_inc(acc_done, 1)
                    if not is_max and n == FLUSH:
                        dve.wait_ge(stored[1 - par], 16 * (k + 1))
                        if half_before == 1:
                            dve.wait_ge(back_in[1 - par], 16 * (LOOP * i + j + 1))
                        take_distances(1 - par, 2 * KT + KT * (g - 1), half_before)

            with dve.Fori(0, HELD) as i:
                for half in range(2):
                    body(i, half, 0, 0, 1 - half)
                    body(i, half, 0, 1, half)
                    with dve.Fori(1, LOOP) as j:
                        for par in range(2):
                            body(i, half, j, par, half)
            dve.wait_ge(stored[1], 16 * (HELD * STEPS + 1))
            dve.wait_ge(back_in[1], 16 * (LOOP * HELD + 1))
            take_distances(1, 2 * KT + KT * (2 * HELD * STEPS - 1), 1)


def route(nc, t1, attended, routerT, ident, base, uT, weights):
    MT = TOKENS // P
    with ExitStack() as ctx:
        a = Place(nc, ctx, "route")
        r_sb = a.sb("r", [P, DC, EXPERTS])
        eps = a.sb("eps", [P, 1])
        x_sb = a.sb("x", [P, 2, D])
        att_sb = a.sb("att", [P, 2, H, E])
        t2_sb = a.sb("t2", [P, 2, D])
        stats = a.sb("stats", [P, 2, 6])
        mean_var = a.sb("mean_var", [P, 2, 2])
        std = a.sb("std", [P, 2, 1])
        rstd = a.sb("rstd", [P, 2, 1])
        u_sb = a.sb("u", [P, 2, D])
        junk = a.sb("junk", [P, 1])
        base_sb = a.sb("base", [P, 2, D])
        uT_sb = a.sb("uT", [P, 2, DC, P])
        logits = a.sb("logits", [P, MT, EXPERTS])
        probs = a.sb("probs", [P, MT, EXPERTS])
        rank = a.sb("rank", [P, MT, EXPERTS])
        above = a.sb("above", [P, MT, EXPERTS])
        row = a.sb("row", [P, MT])
        w_sb = a.sb("w", [P, MT, EXPERTS])
        uT_ps = a.ps("uT_ps", [P, 2, BANK])
        l_ps = a.ps("l_ps", [P, 2, BANK])
        const_in = a.sem("const_in")
        preset = a.sem("preset")
        x_in = a.pair("x_in")
        steps = a.sem("steps")
        std_ready = a.sem("std_ready")
        u_ready = a.sem("u_ready")
        base_ready = a.sem("base_ready")
        uT_ready = a.sem("uT_ready")
        uT_copied = a.sem("uT_copied")
        l_ready = a.sem("l_ready")
        l_copied = a.sem("l_copied")
        stored = a.sem("stored")
        out_free = a.sem("out_free")
        choice = a.sem("choice")
        exp_done = a.sem("exp_done")
        w_ready = a.sem("w_ready")
        stored_w = a.sem("stored_w")
        CONST = 16
        att_rows = attended.rearrange("(h n) e -> n h e", h=H)
        uT_cols = uT.rearrange("(c p) n -> p c n", p=P)
        block = ctx.enter_context(nc.Block())

        @block.sync
        def _(sp):
            sp.dma_start(r_sb[:, :, :], routerT.rearrange("(c p) e -> p c e", p=P)).then_inc(const_in, 16)
            with sp.Fori(0, MT // 2) as k:
                for par in range(2):
                    g = 2 * k + par
                    sp.wait_ge(u_ready, g + 1)
                    sp.dma_start(x_sb[:, par, :], t1[bass.ds(g * P, P), :]).then_inc(x_in[par], 16)
                    sp.dma_start(att_sb[:, par, :, :], att_rows[bass.ds(g * P, P), :, :]).then_inc(x_in[par], 16)
            sp.wait_ge(w_ready, 1)
            sp.dma_start(weights.rearrange("(t p) e -> p t e", p=P), w_sb[:, :, :]).then_inc(stored_w, 16)
            sp.wait_ge(stored_w, 16)

        @block.gpsimd
        def _(pool):
            pool.sem_inc(out_free, 2)
            with pool.Fori(0, MT // 2) as k:
                for par in range(2):
                    g = 2 * k + par
                    pool.wait_ge(base_ready, 2 + g + 1)
                    pool.dma_start(base[bass.ds(g * P, P), :], base_sb[:, par, :]).then_inc(stored, 16)
                    pool.wait_ge(uT_copied, 2 + g + 1)
                    pool.dma_start(uT_cols[:, :, bass.ds(g * P, P)], uT_sb[:, par, :, :]).then_inc(stored, 16)
                    pool.wait_ge(stored, 32 * (g + 1))
                    pool.sem_inc(out_free, 1)

        @block.tensor
        def _(pe):
            pe.sem_inc(l_ready, 2)
            pe.wait_ge(const_in, CONST)
            with pe.Fori(0, MT // 2) as k:
                for par in range(2):
                    g = 2 * k + par
                    pe.wait_ge(u_ready, 2 + g + 1)
                    pe.wait_ge(uT_copied, g + 1)
                    for c in range(DC):
                        mm = pe.transpose(uT_ps[:, par, c * P:(c + 1) * P], u_sb[:, par, c * P:(c + 1) * P], ident[:, :])
                    mm.then_inc(uT_ready, 1)
                    pe.wait_ge(uT_copied, 2 + g + 1)
                    pe.wait_ge(l_copied, g + 1)
                    for c in range(DC):
                        mm = pe.matmul(l_ps[:, par, 0:EXPERTS], uT_sb[:, par, c, :], r_sb[:, c, :],
                                       start=c == 0, stop=c == DC - 1)
                    mm.then_inc(l_ready, 1)

        @block.scalar
        def _(act):
            act.sem_inc(uT_copied, 2)
            act.wait_ge(preset, 1)
            with act.Fori(0, MT // 2) as k:
                for par in range(2):
                    act.wait_ge(steps, 8 * k + 4 + par + 1)
                    act.activation(std[:, par, :], mean_var[:, par, 1:2], ACT.Sqrt, bias=eps[:, :]).then_inc(std_ready, 1)
                for par in range(2):
                    g = 2 * k + par
                    act.wait_ge(uT_ready, g + 1)
                    act.wait_ge(l_ready, g + 1)
                    act.wait_ge(out_free, g + 1)
                    act.copy(uT_sb[:, par, :, :], uT_ps[:, par, 0:D]).then_inc(uT_copied, 1)
            act.wait_ge(choice, 2)
            act.activation(probs[:, :, :], logits[:, :, :], ACT.Exp).then_inc(exp_done, 1)

        @block.vector
        def _(dve):
            dve.sem_inc(u_ready, 2)
            dve.sem_inc(base_ready, 2)
            dve.sem_inc(l_copied, 2)
            dve.memset(eps[:, :], LN_EPS).then_inc(preset, 1)

            def normalise(k):
                for par in range(2):
                    dve.wait_ge(base_ready, 2 * k + par + 1)
                    dve.wait_ge(x_in[par], 32 * (k + 1))
                    dve.tensor_tensor(t2_sb[:, par, :], x_sb[:, par, :], att_sb[:, par, :, :], ALU.add
                                      ).then_inc(steps, 1)
                for par in range(2):
                    dve.wait_ge(steps, 8 * k + par + 1)
                    dve.bn_stats(stats[:, par, :], t2_sb[:, par, :]).then_inc(steps, 1)
                dve.wait_ge(steps, 8 * k + 4)
                dve.memset(junk[:, :], 0.0)
                for par in range(2):
                    dve.bn_aggr(mean_var[:, par, :], stats[:, par, :]).then_inc(steps, 1)
                for par in range(2):
                    dve.wait_ge(std_ready, 2 * k + par + 1)
                    dve.reciprocal(rstd[:, par, :], std[:, par, :]).then_inc(steps, 1)
                for par in range(2):
                    g = 2 * k + par
                    dve.wait_ge(steps, 8 * k + 6 + par + 1)
                    dve.wait_ge(uT_copied, g + 1)
                    dve.tensor_scalar(u_sb[:, par, :], t2_sb[:, par, :], mean_var[:, par, 0:1], rstd[:, par, :],
                                      ALU.subtract, ALU.mult).then_inc(u_ready, 1)
                for par in range(2):
                    g = 2 * k + par
                    dve.wait_ge(u_ready, 2 + g + 1)
                    dve.wait_ge(out_free, g + 1)
                    dve.tensor_tensor(base_sb[:, par, :], t2_sb[:, par, :], u_sb[:, par, :], ALU.add
                                      ).then_inc(base_ready, 1)

            def take_logits(k):
                for par in range(2):
                    g = 2 * k + par
                    dve.wait_ge(l_ready, 2 + g + 1)
                    dve.tensor_copy(logits[:, bass.ds(g, 1), :], l_ps[:, par, 0:EXPERTS]).then_inc(l_copied, 1)

            normalise(0)
            with dve.Fori(0, MT // 2 - 1) as k:
                normalise(k + 1)
                take_logits(k)
            take_logits(MT // 2 - 1)

            done = [0]

            def step(ins):
                done[0] += 1
                ins.then_inc(choice, 1)
                dve.wait_ge(choice, done[0])

            def per_token(x):
                return x[:, :].unsqueeze(2).broadcast_to([P, MT, EXPERTS])

            dve.wait_ge(l_copied, 2 + MT)
            step(dve.tensor_reduce(row[:, :], logits[:, :, :], AX.X, ALU.max))
            step(dve.tensor_tensor(logits[:, :, :], logits[:, :, :], per_token(row), ALU.subtract))
            dve.wait_ge(exp_done, 1)
            step(dve.tensor_reduce(row[:, :], probs[:, :, :], AX.X, ALU.add))
            step(dve.reciprocal(row[:, :], row[:, :]))
            step(dve.tensor_tensor(probs[:, :, :], probs[:, :, :], per_token(row), ALU.mult))
            for j in range(EXPERTS):
                pj = probs[:, :, j:j + 1]
                dst = rank if j == 0 else above
                if j + 1 < EXPERTS:
                    step(dve.tensor_tensor(dst[:, :, j + 1:], pj.broadcast_to([P, MT, EXPERTS - 1 - j]),
                                           probs[:, :, j + 1:], ALU.is_ge))
                step(dve.tensor_tensor(dst[:, :, 0:j + 1], pj.broadcast_to([P, MT, j + 1]),
                                       probs[:, :, 0:j + 1], ALU.is_gt))
                if j:
                    step(dve.tensor_tensor(rank[:, :, :], rank[:, :, :], above[:, :, :], ALU.add))
            step(dve.tensor_scalar(rank[:, :, :], rank[:, :, :], float(TOP), None, ALU.is_lt))
            step(dve.tensor_tensor(probs[:, :, :], probs[:, :, :], rank[:, :, :], ALU.mult))
            step(dve.tensor_reduce(row[:, :], probs[:, :, :], AX.X, ALU.add))
            step(dve.tensor_scalar(row[:, :], row[:, :], 1e-12, None, ALU.max))
            step(dve.reciprocal(row[:, :], row[:, :]))
            dve.tensor_tensor(w_sb[:, :, :], probs[:, :, :], per_token(row), ALU.mult).then_inc(w_ready, 1)


def experts(nc, base, uT, weights, w1, b1, w2, b2, out):
    G = BANK
    TG = G // P
    LOOPS = TOKENS // G // 2
    with ExitStack() as ctx:
        a = Place(nc, ctx, "experts")
        w1_sb = a.sb("w1", [P, EXPERTS, DC, D])
        w2_sb = a.sb("w2", [P, EXPERTS, DC, D])
        b1_sb = a.sb("b1", [P, EXPERTS, DC])
        b2_sb = a.sb("b2", [P, EXPERTS, D])
        u_sb = a.sb("u", [P, 2, DC, G])
        wt_sb = a.sb("wt", [P, 2, TG, EXPERTS])
        acc = a.sb("acc", [P, 2, TG, D])
        h_sb = a.sb("h", [P, 2, DC, G])
        h_ps = a.ps("h_ps", [P, 2, DC, G])
        y_ps = a.ps("y_ps", [P, 2, TG, D])
        w_in = a.sem("w_in")
        group_in = a.pair("group_in")
        h_ready = a.sem("h_ready")
        h_done = a.sem("h_done")
        y_ready = a.sem("y_ready")
        b_added = a.sem("b_added")
        y_added = a.sem("y_added")
        acc_free = a.sem("acc_free")
        stored = a.sem("stored")
        CONST = 16 * 4
        block = ctx.enter_context(nc.Block())

        def rows(x, g):
            return x.rearrange("(t p) d -> p t d", p=P)[:, bass.ds(g * TG, TG), :]

        @block.sync
        def _(sp):
            sp.dma_start(w1_sb[:, :, :, :], w1.rearrange("e (c p) f -> p e c f", p=P)).then_inc(w_in, 16)
            sp.dma_start(w2_sb[:, :, :, :], w2.rearrange("e (c p) f -> p e c f", p=P)).then_inc(w_in, 16)
            sp.dma_start(b1_sb[:, :, :], b1).then_inc(w_in, 16)
            sp.dma_start(b2_sb[:, :, :], b2.partition_broadcast(P)).then_inc(w_in, 16)
            with sp.Fori(0, LOOPS) as i:
                for par in range(2):
                    g = 2 * i + par
                    sp.wait_ge(acc_free, g + 1)
                    sp.dma_start(u_sb[:, par, :, :], uT.rearrange("(c p) n -> p c n", p=P)[:, :, bass.ds(g * G, G)]
                                 ).then_inc(group_in[par], 16)
                    sp.dma_start(wt_sb[:, par, :, :], rows(weights, g)).then_inc(group_in[par], 16)
                    sp.dma_start(acc[:, par, :, :], rows(base, g)).then_inc(group_in[par], 16)

        @block.gpsimd
        def _(pool):
            pool.sem_inc(acc_free, 2)
            with pool.Fori(0, LOOPS) as i:
                for par in range(2):
                    g = 2 * i + par
                    pool.wait_ge(y_added, 2 * TG + EXPERTS * TG * (g + 1))
                    pool.dma_start(rows(out, g), acc[:, par, :, :]).then_inc(stored, 16)
                    pool.wait_ge(stored, 16 * (g + 1))
                    pool.sem_inc(acc_free, 1)

        @block.tensor
        def _(pe):
            pe.sem_inc(h_ready, 2 * DC)
            pe.sem_inc(y_ready, 2)
            pe.wait_ge(w_in, CONST)

            def hidden(g, par, e):
                n = EXPERTS * g + e
                for f in range(DC):
                    pe.wait_ge(h_done, DC * n + f + 1)
                    for c in range(DC):
                        mm = pe.matmul(h_ps[:, e % 2, f, :], w1_sb[:, e, c, f * P:(f + 1) * P],
                                       u_sb[:, par, c, :], start=c == 0, stop=c == DC - 1)
                    mm.then_inc(h_ready, 1)

            def output(g, e):
                n = EXPERTS * g + e
                pe.wait_ge(h_done, 2 * DC + DC * (n + 1))
                pe.wait_ge(y_added, TG * (n + 1))
                for t in range(TG):
                    for f in range(DC):
                        mm = pe.matmul(y_ps[:, e % 2, t, :], h_sb[:, e % 2, f, t * P:(t + 1) * P],
                                       w2_sb[:, e, f, :], start=f == 0, stop=f == DC - 1)
                mm.then_inc(y_ready, 1)

            with pe.Fori(0, LOOPS) as i:
                for par in range(2):
                    g = 2 * i + par
                    pe.wait_ge(group_in[par], 48 * (i + 1))
                    hidden(g, par, 0)
                    for e in range(1, EXPERTS):
                        hidden(g, par, e)
                        output(g, e - 1)
                    output(g, EXPERTS - 1)

        @block.scalar
        def _(act):
            act.sem_inc(h_done, 2 * DC)
            act.wait_ge(w_in, CONST)
            with act.Fori(0, LOOPS) as i:
                for par in range(2):
                    for e in range(EXPERTS):
                        n = EXPERTS * (2 * i + par) + e
                        act.wait_ge(y_ready, n + 1)
                        for f in range(DC):
                            act.wait_ge(h_ready, 2 * DC + DC * n + f + 1)
                            act.activation(h_sb[:, e % 2, f, :], h_ps[:, e % 2, f, :], ACT.Gelu,
                                           bias=b1_sb[:, e, f:f + 1]).then_inc(h_done, 1)

        @block.vector
        def _(dve):
            dve.sem_inc(y_added, 2 * TG)
            dve.wait_ge(w_in, CONST)
            with dve.Fori(0, LOOPS) as i:
                for par in range(2):
                    dve.wait_ge(group_in[par], 48 * (i + 1))
                    for e in range(EXPERTS):
                        n = EXPERTS * (2 * i + par) + e
                        for t in range(TG):
                            if e:
                                dve.wait_ge(y_added, 2 * TG + TG * (n - 1) + t + 1)
                            dve.scalar_tensor_tensor(acc[:, par, t, :], b2_sb[:, e, :], wt_sb[:, par, t, e:e + 1],
                                                     acc[:, par, t, :], ALU.mult, ALU.add).then_inc(b_added, 1)
                        dve.wait_ge(y_ready, 2 + n + 1)
                        for t in range(TG):
                            dve.wait_ge(b_added, TG * n + t + 1)
                            dve.scalar_tensor_tensor(acc[:, par, t, :], y_ps[:, e % 2, t, :],
                                                     wt_sb[:, par, t, e:e + 1], acc[:, par, t, :],
                                                     ALU.mult, ALU.add).then_inc(y_added, 1)


def build(nc, t, out):
    with nc.sbuf_tensor("ident", [P, P], F32) as ident:
        stages(nc, t, ident, out)


def stages(nc, t, ident, out):
    def scratch(name, shape):
        return nc.dram_tensor(name, list(shape), F32, kind="Internal").ap()

    q0T, k0T = scratch("q0T", (P, TOKENS)), scratch("k0T", (P, TOKENS))
    v0, t1 = scratch("v0", (TOKENS, D)), scratch("t1", (TOKENS, D))
    parts = scratch("parts", (P, 3 * PH * TOKENS))
    rows2 = scratch("rows2", (E + 2, TOKENS))
    ks, v = scratch("ks", (TOKENS, KS)), scratch("v", (H * TOKENS, 2 * E))
    dist = scratch("dist", (TOKENS, N))
    attended = scratch("attended", (H * TOKENS, E))
    base, uT, weights = scratch("base", (TOKENS, D)), scratch("uT", (D, TOKENS)), scratch("weights", (TOKENS, EXPERTS))

    project0(nc, t["xT"], t["wqk0"], t["bqk0"], t["signs0"], t["wv0"], t["bv0"], t["identity"], ident,
             q0T, k0T, v0)
    attend0(nc, q0T, k0T, v0, ident, t["gamma"], t["x"], t1)
    project1(nc, t1, t["wqkv"], t["bqkv"], t["share"], ident, parts, rows2, ks, v)
    distances(nc, rows2, ks, ident, dist)

    def rows(x, head, heads):
        return x[head * TOKENS:(head + heads) * TOKENS, :]

    def products(stage, first, heads, kind, **more):
        at = PRODUCT_HEADS.index(first)
        q, k_high, k_low = (parts[:, (at + m * PH) * TOKENS:(at + m * PH + heads) * TOKENS] for m in range(3))
        attend1(nc, stage, heads * B, q, [k_high, k_low], rows(v, first, heads), kind, ident,
                rows(attended, first, heads), **more)

    products("products", SDP, 2, "dot")
    attend1(nc, "l1", B, None, [], rows(v, L1, 1), "l1", ident, rows(attended, L1, 1), scores=dist)
    products("l2", L2, 1, "l2", norms=ks[:, NORM_AT:NORM_AT + 2], norm_rows=rows2[E:E + 2, :])
    route(nc, t1, attended, t["routerT"], ident, base, uT, weights)
    experts(nc, base, uT, weights, t["w1"], t["b1"], t["w2"], t["b2"], out)


def lay_out(inputs):
    import numpy as np

    def heads(w):
        return w.transpose(1, 0, 2).reshape(D, H * E)

    QUADS, Q_LOW, K_LOW = P // C0, (1, 3), (2, 3)

    def quads(b, *where):
        out = np.zeros((QUADS, C0), np.float32)
        out[list(where)] = b
        return out.reshape(P)

    q_low, k_low = (quads(np.ones(C0, np.float32), *where) for where in (Q_LOW, K_LOW))
    i = {name: np.asarray(x) for name, x in inputs.items()}
    x = i["x"].reshape(TOKENS, D)
    arrays = {
        "x": x, "xT": x.T, "identity": np.eye(P, dtype=np.float32),
        "wqk0": np.concatenate([i["L0_conv_Wq"]] * QUADS + [i["L0_conv_Wk"]] * QUADS).T,
        "bqk0": np.stack([quads(i["L0_conv_bq"], 0, 1, 2, 3), quads(i["L0_conv_bq"], *Q_LOW),
                          quads(i["L0_conv_bk"], 0, 1, 2, 3), quads(i["L0_conv_bk"], *K_LOW)], axis=1),
        "signs0": np.stack([1 - 2 * q_low, q_low, 1 - 2 * k_low, k_low], axis=1),
        "wv0": i["L0_conv_Wv"].T, "bv0": i["L0_conv_bv"], "gamma": i["L0_conv_gamma"],
        "wqkv": np.concatenate([heads(i[f"L1_attn_W{c}"]) for c in "qkv"], axis=1),
        "bqkv": np.concatenate([i[f"L1_attn_b{c}"].reshape(-1) for c in "qkv"]),
        "share": np.array([e % HALF_E in VECTOR_E for e in range(E)], np.float32),
        "routerT": i["L1_ffn_router_w"].T,
        "w1": i["L1_ffn_w1"], "b1": i["L1_ffn_b1"].reshape(EXPERTS, DC, P).transpose(2, 0, 1),
        "w2": i["L1_ffn_w2"], "b2": i["L1_ffn_b2"],
    }
    return {name: np.ascontiguousarray(x) for name, x in arrays.items()}


def kernel(**inputs):
    import concourse.bacc as bacc
    from concourse.bass_utils import run_bass_kernel_spmd

    nc = bacc.Bacc("TRN2", target_bir_lowering=False, num_devices=1)
    arrays = lay_out(inputs)
    tensors = {name: nc.dram_tensor(name, x.shape, mybir.dt.from_np(x.dtype), kind="ExternalInput").ap()
               for name, x in arrays.items()}
    out = nc.dram_tensor("out", (TOKENS, D), F32, kind="ExternalOutput").ap()
    build(nc, tensors, out)
    result = run_bass_kernel_spmd(nc, [arrays], core_ids=[0])
    return result.results[0]["out"].reshape(inputs["x"].shape)
```
